# Optimizing a Trainium2 kernel written in Bass

```python
import numpy as np
import jax
import jax.numpy as jnp

def _softmax(x, axis=-1):
    return jax.nn.softmax(x, axis=axis)

def _gelu(x):
    return jax.nn.gelu(x, approximate=True)

def _silu(x):
    return jax.nn.silu(x)

def _sigmoid(x):
    return jax.nn.sigmoid(x)

def _layernorm(x, axis=-1, eps=1e-05):
    m = jnp.mean(x, axis=axis, keepdims=True)
    v = jnp.var(x, axis=axis, keepdims=True)
    return (x - m) / jnp.sqrt(v + eps)

def _scatter_add(tgt, idx, src, axis=0):
    return tgt.at[idx].add(src)

def _segment_sum(src, seg, n):
    return jax.ops.segment_sum(src, seg, n)
kernel_name = 'mk_decoder_preln_d2_seqx_r8_bd673d'

def setup_inputs(seed: int=0):
    np.random.seed(seed)
    _w = jnp.asarray

    def _rec_inputs():
        import jax
        import jax.numpy as jnp
        _rk = jax.random.key(seed)
        x = -0.000125 + 0.9999 * jax.random.normal(jax.random.fold_in(_rk, 1), (4, 256, 256), jnp.float32)
        _lenS = 256 - jax.random.randint(jax.random.fold_in(_rk, 7), (4,), 0, max(1, 256 // 4) + 1, jnp.int32)
        _lenS2 = 256 - jax.random.randint(jax.random.fold_in(_rk, 8), (4,), 0, max(1, 256 // 4) + 1, jnp.int32)
        fside_BxS2xS2_0 = -3.05549e-07 + 0.0199987 * jax.random.normal(jax.random.fold_in(_rk, 11), (4, 256, 256), jnp.float32)
        _ctx_1024P = jax.random.normal(jax.random.fold_in(_rk, 12), (4, 16, 128), jnp.float32)
        _ctx_1024c = jax.random.dirichlet(jax.random.fold_in(_rk, 512), 0.3 * jnp.ones((16,), jnp.float32), (4, 256))
        _ctx_1024t = jnp.einsum('bsk,bkd->bsd', _ctx_1024c, _ctx_1024P)
        _ctx_1024t = _ctx_1024t * jax.lax.rsqrt(jnp.mean(jnp.square(_ctx_1024t)) + 1e-12) * 0.953939
        ctx_1024 = 6.82029e-06 + 0.0200006 * (_ctx_1024t + 0.3 * jax.random.normal(jax.random.fold_in(_rk, 612), (4, 256, 128), jnp.float32))
        return (x, fside_BxS2xS2_0, ctx_1024)
    x, fside_BxS2xS2_0, ctx_1024 = _rec_inputs()

    def _L0_attn_setup():
        import jax, jax.numpy as jnp
        import numpy as np
        EMBED_DIM = 256
        NUM_HEADS = 16
        HEAD_DIM = EMBED_DIM // NUM_HEADS

        def _xavier(key, shape):
            fan_in, fan_out = (shape[1], shape[0])
            limit = float(np.sqrt(6.0 / (fan_in + fan_out)))
            return jax.random.uniform(key, shape, jnp.float32, -limit, limit)
        key = jax.random.key(seed)
        kx, kq, kk, kv, ko = jax.random.split(key, 5)
        x = jax.random.normal(kx, (2, 256, EMBED_DIM), dtype=jnp.float32)
        Wq = _xavier(kq, (EMBED_DIM, EMBED_DIM))
        Wk = _xavier(kk, (EMBED_DIM, EMBED_DIM))
        Wv = _xavier(kv, (EMBED_DIM, EMBED_DIM))
        Wo = _xavier(ko, (EMBED_DIM, EMBED_DIM))
        return {'x': x, 'Wq': Wq, 'Wk': Wk, 'Wv': Wv, 'Wo': Wo}
    _L0_attn_all = _L0_attn_setup()
    _L0_attn_in = {k: v for k, v in _L0_attn_all.items() if k in ('Wq', 'Wk', 'Wv', 'Wo')}
    del _L0_attn_all

    def _L0_xattn_setup():
        import jax, jax.numpy as jnp
        import numpy as np
        EPS = 1e-06
        QMAX = 127.0

        def _smooth_quant_linear(x, w):
            amax_x = jnp.max(jnp.abs(x), axis=0)
            amax_w = jnp.max(jnp.abs(w), axis=0)
            s = jnp.sqrt(jnp.maximum(amax_x, EPS) / jnp.maximum(amax_w, EPS))
            s = jnp.maximum(s, EPS)
            xs = x / s
            ws = w * s
            x_scale = jnp.maximum(jnp.max(jnp.abs(xs), axis=-1, keepdims=True), EPS) / QMAX
            w_scale = jnp.maximum(jnp.max(jnp.abs(ws), axis=-1, keepdims=True), EPS) / QMAX
            x_q = jnp.clip(jnp.round(xs / x_scale), -QMAX, QMAX)
            w_q = jnp.clip(jnp.round(ws / w_scale), -QMAX, QMAX)
            return x_q @ w_q.T * x_scale * w_scale.T

        def _expert_forward(xe, guw, dw):
            h = _smooth_quant_linear(xe, guw)
            gate, up = jnp.split(h, 2, axis=-1)
            a = jax.nn.silu(gate) * up
            return _smooth_quant_linear(a, dw)
        key = jax.random.key(seed)
        k1, k2, k3 = jax.random.split(key, 3)
        E, T, D, I = (8, 256, 256, 128)
        x = jax.random.normal(k1, (E, T, D), dtype=jnp.float32)
        gate_up_weight = jax.random.normal(k2, (E, 2 * I, D), dtype=jnp.float32) * 0.02
        down_weight = jax.random.normal(k3, (E, D, I), dtype=jnp.float32) * 0.02
        return {'x': x, 'gate_up_weight': gate_up_weight, 'down_weight': down_weight}
    _L0_xattn_all = _L0_xattn_setup()
    _L0_xattn_in = {k: v for k, v in _L0_xattn_all.items() if k in ()}
    del _L0_xattn_all

    def _L0_ffn_setup():
        import jax, jax.numpy as jnp
        import numpy as np

        def _sparsify_2to4(h):
            B, S, I = h.shape
            g = h.reshape(B, S, I // 4, 4)
            a = jnp.abs(g)
            _, idx = jax.lax.top_k(a, 2)
            pos = jnp.arange(4)
            mask = (pos == idx[..., 0:1]) | (pos == idx[..., 1:2])
            return (g * mask.astype(g.dtype)).reshape(B, S, I)
        key = jax.random.key(seed)
        k1, k2, k3, k4 = jax.random.split(key, 4)
        B, S, H, I = (4, 256, 256, 1024)
        x = jax.random.normal(k1, (B, S, H), dtype=jnp.float32)
        w_gate = jax.random.normal(k2, (H, I), dtype=jnp.float32) / np.sqrt(H)
        w_up = jax.random.normal(k3, (H, I), dtype=jnp.float32) / np.sqrt(H)
        w_down = jax.random.normal(k4, (I, H), dtype=jnp.float32) / np.sqrt(I)
        return {'x': x, 'w_gate': w_gate, 'w_up': w_up, 'w_down': w_down}
    _L0_ffn_all = _L0_ffn_setup()
    _L0_ffn_in = {k: v for k, v in _L0_ffn_all.items() if k in ('w_gate', 'w_up', 'w_down')}
    del _L0_ffn_all

    def _L1_attn_setup():
        import jax, jax.numpy as jnp
        import numpy as np
        B_, L_, D_, E_, N_, R_, K_ = (2, 256, 256, 512, 16, 128, 4)
        key = jax.random.key(seed)
        ks = jax.random.split(key, 12)
        s = lambda k, shape, scale: jax.random.normal(k, shape, dtype=jnp.float32) * scale
        return {'resid': s(ks[0], (B_, L_, D_), 1.0), 'norm_w': jnp.ones((D_,), jnp.float32), 'W_skip': s(ks[1], (E_, D_), D_ ** (-0.5)), 'W_in': s(ks[2], (E_, D_), D_ ** (-0.5)), 'conv_w': s(ks[3], (E_, 1, K_), K_ ** (-0.5)), 'conv_b': s(ks[4], (E_,), 0.02), 'W_d1': s(ks[5], (R_, E_), E_ ** (-0.5)), 'W_d2': s(ks[6], (E_, R_), R_ ** (-0.5)), 'b_d2': s(ks[7], (E_,), 0.02) - 2.0, 'W_Bm': s(ks[8], (N_, E_), E_ ** (-0.5)), 'W_Cm': s(ks[9], (N_, E_), E_ ** (-0.5)), 'A_log': s(ks[10], (E_, N_), 0.5), 'W_D': jnp.ones((E_,), jnp.float32), 'W_out': s(ks[11], (D_, E_), E_ ** (-0.5))}
    _L1_attn_all = _L1_attn_setup()
    _L1_attn_in = {k: v for k, v in _L1_attn_all.items() if k in ('norm_w', 'W_skip', 'W_in', 'conv_w', 'conv_b', 'W_d1', 'W_d2', 'b_d2', 'W_Bm', 'W_Cm', 'A_log', 'W_D', 'W_out')}
    del _L1_attn_all

    def _L1_xattn_setup():
        import jax, jax.numpy as jnp
        import numpy as np
        key = jax.random.key(seed)
        ks = jax.random.split(key, 6)
        B, L, N, C, D = (8, 64, 256, 128, 128)
        return {'teacher_logits': jax.random.normal(ks[0], (B, L, N), dtype=jnp.float32), 'teacher_features': jax.random.normal(ks[1], (B, N, C), dtype=jnp.float32), 'Wq': jax.random.normal(ks[2], (D, C), dtype=jnp.float32) * (1.0 / np.sqrt(C)), 'bq': jnp.zeros((D,), dtype=jnp.float32), 'Wk': jax.random.normal(ks[3], (D, C), dtype=jnp.float32) * (1.0 / np.sqrt(C)), 'bk': jnp.zeros((D,), dtype=jnp.float32)}
    _L1_xattn_all = _L1_xattn_setup()
    _L1_xattn_in = {k: v for k, v in _L1_xattn_all.items() if k in ('Wq', 'bq', 'Wk', 'bk')}
    del _L1_xattn_all

    def _L1_ffn_setup():
        import jax, jax.numpy as jnp
        import numpy as np
        B, S, H = (1, 128, 256)
        E, F, FS = (32, 96, 512)
        TOP_K = 4
        SCALE = 0.02
        key = jax.random.key(seed)
        ks = jax.random.split(key, 9)
        return {'hidden_states': jax.random.normal(ks[0], (B, S, H), jnp.float32), 'router_weight': jax.random.normal(ks[1], (E, H), jnp.float32) * SCALE, 'w_gate': jax.random.normal(ks[2], (E, H, F), jnp.float32) * SCALE, 'w_up': jax.random.normal(ks[3], (E, H, F), jnp.float32) * SCALE, 'w_down': jax.random.normal(ks[4], (E, F, H), jnp.float32) * SCALE, 'sw_gate': jax.random.normal(ks[5], (H, FS), jnp.float32) * SCALE, 'sw_up': jax.random.normal(ks[6], (H, FS), jnp.float32) * SCALE, 'sw_down': jax.random.normal(ks[7], (FS, H), jnp.float32) * SCALE, 'sgate_w': jax.random.normal(ks[8], (H, 1), jnp.float32) * SCALE}
    _L1_ffn_all = _L1_ffn_setup()
    _L1_ffn_in = {k: v for k, v in _L1_ffn_all.items() if k in ('router_weight', 'w_gate', 'w_up', 'w_down', 'sw_gate', 'sw_up', 'sw_down', 'sgate_w')}
    del _L1_ffn_all
    return {'x': x, 'fside_BxS2xS2_0': fside_BxS2xS2_0, 'ctx_1024': ctx_1024, 'L0_attn_Wq': _L0_attn_in['Wq'], 'L0_attn_Wk': _L0_attn_in['Wk'], 'L0_attn_Wv': _L0_attn_in['Wv'], 'L0_attn_Wo': _L0_attn_in['Wo'], 'L0_ffn_w_gate': _L0_ffn_in['w_gate'], 'L0_ffn_w_up': _L0_ffn_in['w_up'], 'L0_ffn_w_down': _L0_ffn_in['w_down'], 'L1_attn_norm_w': _L1_attn_in['norm_w'], 'L1_attn_W_skip': _L1_attn_in['W_skip'], 'L1_attn_W_in': _L1_attn_in['W_in'], 'L1_attn_conv_w': _L1_attn_in['conv_w'], 'L1_attn_conv_b': _L1_attn_in['conv_b'], 'L1_attn_W_d1': _L1_attn_in['W_d1'], 'L1_attn_W_d2': _L1_attn_in['W_d2'], 'L1_attn_b_d2': _L1_attn_in['b_d2'], 'L1_attn_W_Bm': _L1_attn_in['W_Bm'], 'L1_attn_W_Cm': _L1_attn_in['W_Cm'], 'L1_attn_A_log': _L1_attn_in['A_log'], 'L1_attn_W_D': _L1_attn_in['W_D'], 'L1_attn_W_out': _L1_attn_in['W_out'], 'L1_xattn_Wq': _L1_xattn_in['Wq'], 'L1_xattn_bq': _L1_xattn_in['bq'], 'L1_xattn_Wk': _L1_xattn_in['Wk'], 'L1_xattn_bk': _L1_xattn_in['bk'], 'L1_ffn_router_weight': _L1_ffn_in['router_weight'], 'L1_ffn_w_gate': _L1_ffn_in['w_gate'], 'L1_ffn_w_up': _L1_ffn_in['w_up'], 'L1_ffn_w_down': _L1_ffn_in['w_down'], 'L1_ffn_sw_gate': _L1_ffn_in['sw_gate'], 'L1_ffn_sw_up': _L1_ffn_in['sw_up'], 'L1_ffn_sw_down': _L1_ffn_in['sw_down'], 'L1_ffn_sgate_w': _L1_ffn_in['sgate_w']}

def reference(x, fside_BxS2xS2_0, ctx_1024, L0_attn_Wq, L0_attn_Wk, L0_attn_Wv, L0_attn_Wo, L0_ffn_w_gate, L0_ffn_w_up, L0_ffn_w_down, L1_attn_norm_w, L1_attn_W_skip, L1_attn_W_in, L1_attn_conv_w, L1_attn_conv_b, L1_attn_W_d1, L1_attn_W_d2, L1_attn_b_d2, L1_attn_W_Bm, L1_attn_W_Cm, L1_attn_A_log, L1_attn_W_D, L1_attn_W_out, L1_xattn_Wq, L1_xattn_bq, L1_xattn_Wk, L1_xattn_bk, L1_ffn_router_weight, L1_ffn_w_gate, L1_ffn_w_up, L1_ffn_w_down, L1_ffn_sw_gate, L1_ffn_sw_up, L1_ffn_sw_down, L1_ffn_sgate_w):
    import jax
    import jax.numpy as jnp

    def _L0_attn_ref(x, Wq, Wk, Wv, Wo):
        import jax, jax.numpy as jnp
        import numpy as np
        EMBED_DIM = 256
        NUM_HEADS = 16
        HEAD_DIM = EMBED_DIM // NUM_HEADS

        def _xavier(key, shape):
            fan_in, fan_out = (shape[1], shape[0])
            limit = float(np.sqrt(6.0 / (fan_in + fan_out)))
            return jax.random.uniform(key, shape, jnp.float32, -limit, limit)
        B, S, E = x.shape
        H, D = (NUM_HEADS, HEAD_DIM)

        def heads(y):
            return y.reshape(B, S, H, D).transpose(0, 2, 1, 3)
        q = heads(jnp.einsum('bse,fe->bsf', x, Wq))
        k = heads(jnp.einsum('bse,fe->bsf', x, Wk))
        v = heads(jnp.einsum('bse,fe->bsf', x, Wv))
        scale = 1.0 / jnp.sqrt(jnp.float32(D))
        scores = jnp.einsum('bhsd,bhtd->bhst', q, k) * scale
        weights = jax.nn.softmax(scores, axis=-1)
        attn = jnp.einsum('bhst,bhtd->bhsd', weights, v)
        attn = attn.transpose(0, 2, 1, 3).reshape(B, S, E)
        out = jnp.einsum('bse,fe->bsf', attn, Wo)
        return out

    def _L0_xattn_ref(x, gate_up_weight, down_weight):
        import jax, jax.numpy as jnp
        import numpy as np
        EPS = 1e-06
        QMAX = 127.0

        def _smooth_quant_linear(x, w):
            amax_x = jnp.max(jnp.abs(x), axis=0)
            amax_w = jnp.max(jnp.abs(w), axis=0)
            s = jnp.sqrt(jnp.maximum(amax_x, EPS) / jnp.maximum(amax_w, EPS))
            s = jnp.maximum(s, EPS)
            xs = x / s
            ws = w * s
            x_scale = jnp.maximum(jnp.max(jnp.abs(xs), axis=-1, keepdims=True), EPS) / QMAX
            w_scale = jnp.maximum(jnp.max(jnp.abs(ws), axis=-1, keepdims=True), EPS) / QMAX
            x_q = jnp.clip(jnp.round(xs / x_scale), -QMAX, QMAX)
            w_q = jnp.clip(jnp.round(ws / w_scale), -QMAX, QMAX)
            return x_q @ w_q.T * x_scale * w_scale.T

        def _expert_forward(xe, guw, dw):
            h = _smooth_quant_linear(xe, guw)
            gate, up = jnp.split(h, 2, axis=-1)
            a = jax.nn.silu(gate) * up
            return _smooth_quant_linear(a, dw)
        return jax.vmap(_expert_forward)(x, gate_up_weight, down_weight)

    def _L0_ffn_ref(x, w_gate, w_up, w_down):
        import jax, jax.numpy as jnp
        import numpy as np

        def _sparsify_2to4(h):
            B, S, I = h.shape
            g = h.reshape(B, S, I // 4, 4)
            a = jnp.abs(g)
            _, idx = jax.lax.top_k(a, 2)
            pos = jnp.arange(4)
            mask = (pos == idx[..., 0:1]) | (pos == idx[..., 1:2])
            return (g * mask.astype(g.dtype)).reshape(B, S, I)
        h = jax.nn.silu(jnp.einsum('bsh,hi->bsi', x, w_gate)) * jnp.einsum('bsh,hi->bsi', x, w_up)
        h_sparse = _sparsify_2to4(h)
        return jnp.einsum('bsi,ih->bsh', h_sparse, w_down)

    def _L1_attn_ref(resid, norm_w, W_skip, W_in, conv_w, conv_b, W_d1, W_d2, b_d2, W_Bm, W_Cm, A_log, W_D, W_out):
        import jax, jax.numpy as jnp
        import numpy as np
        B_, L_, D_, E_, N_, R_, K_ = (2, 256, 256, 512, 16, 128, 4)
        eps = 1e-05
        E, K = (conv_w.shape[0], conv_w.shape[-1])
        x = resid * jax.lax.rsqrt(jnp.mean(resid * resid, -1, keepdims=True) + eps) * norm_w
        skip = x @ W_skip.T
        x = x @ W_in.T
        xc = jnp.swapaxes(x, 1, 2)
        xc = jax.lax.conv_general_dilated(xc, conv_w, (1,), [(K - 1, 0)], dimension_numbers=('NCH', 'OIH', 'NCH'), feature_group_count=E)
        xc = xc + conv_b[None, :, None]
        x = jax.nn.silu(jnp.swapaxes(xc, 1, 2))
        A = -jnp.exp(A_log)
        delta = jax.nn.softplus(x @ W_d1.T @ W_d2.T + b_d2)
        Bt = x @ W_Bm.T
        Ct = x @ W_Cm.T

        def step(h, inp):
            x_t, d_t, b_t, c_t = inp
            h = jnp.exp(d_t[:, :, None] * A) * h + (d_t * x_t)[:, :, None] * b_t[:, None, :]
            y = jnp.einsum('ben,bn->be', h, c_t)
            return (h, y)
        xs = (jnp.swapaxes(x, 0, 1), jnp.swapaxes(delta, 0, 1), jnp.swapaxes(Bt, 0, 1), jnp.swapaxes(Ct, 0, 1))
        h0 = jnp.zeros((x.shape[0], A.shape[0], A.shape[1]), x.dtype)
        _, ys = jax.lax.scan(step, h0, xs)
        y = jnp.swapaxes(ys, 0, 1)
        y = y + x * W_D
        y = y * jax.nn.silu(skip)
        return resid + y @ W_out.T

    def _L1_xattn_ref(teacher_logits, teacher_features, Wq, bq, Wk, bk):
        import jax, jax.numpy as jnp
        import numpy as np
        query = jnp.einsum('bnc,dc->bnd', teacher_features, Wq) + bq
        key = jnp.einsum('bnc,dc->bnd', teacher_features, Wk) + bk
        energy = jnp.einsum('bnd,bmd->bnm', query, key)
        attention = jax.nn.softmax(energy, axis=-1)
        x_m = jnp.einsum('bln,bmn->blm', teacher_logits, attention)
        return x_m

    def _L1_ffn_ref(hidden_states, router_weight, w_gate, w_up, w_down, sw_gate, sw_up, sw_down, sgate_w):
        import jax, jax.numpy as jnp
        import numpy as np
        B, S, H = (1, 128, 256)
        E, F, FS = (32, 96, 512)
        TOP_K = 4
        SCALE = 0.02
        b, s, h = hidden_states.shape
        x = hidden_states.reshape(-1, h)
        T = x.shape[0]
        logits = x @ router_weight.T
        probs = jax.nn.softmax(logits.astype(jnp.float32), axis=-1)
        topv, topi = jax.lax.top_k(probs, TOP_K)
        topv = topv / jnp.sum(topv, axis=-1, keepdims=True)
        topv = topv.astype(probs.dtype)
        combine = jnp.zeros((T, E), probs.dtype).at[jnp.arange(T)[:, None], topi].add(topv)
        g = jnp.einsum('th,ehf->etf', x, w_gate)
        u = jnp.einsum('th,ehf->etf', x, w_up)
        act = jax.nn.silu(g) * u
        out = jnp.einsum('te,etf,efh->th', combine, act, w_down)
        shared = jax.nn.silu(x @ sw_gate) * (x @ sw_up) @ sw_down
        out = out + jax.nn.sigmoid(x @ sgate_w) * shared
        return out.reshape(b, s, h)
    x = x + _L0_attn_ref(_layernorm(x, axis=-1), L0_attn_Wq, L0_attn_Wk, L0_attn_Wv, L0_attn_Wo)
    x = x + _L0_xattn_ref(_layernorm(x, axis=-1), fside_BxS2xS2_0, ctx_1024)
    x = x + _L0_ffn_ref(_layernorm(x, axis=-1), L0_ffn_w_gate, L0_ffn_w_up, L0_ffn_w_down)
    x = x + _L1_attn_ref(_layernorm(x, axis=-1), L1_attn_norm_w, L1_attn_W_skip, L1_attn_W_in, L1_attn_conv_w, L1_attn_conv_b, L1_attn_W_d1, L1_attn_W_d2, L1_attn_b_d2, L1_attn_W_Bm, L1_attn_W_Cm, L1_attn_A_log, L1_attn_W_D, L1_attn_W_out)
    x = x + _L1_xattn_ref(_layernorm(x, axis=-1), ctx_1024, L1_xattn_Wq, L1_xattn_bq, L1_xattn_Wk, L1_xattn_bk)
    x = x + _L1_ffn_ref(_layernorm(x, axis=-1), L1_ffn_router_weight, L1_ffn_w_gate, L1_ffn_w_up, L1_ffn_w_down, L1_ffn_sw_gate, L1_ffn_sw_up, L1_ffn_sw_down, L1_ffn_sgate_w)
    return x

_drawn_inputs = setup_inputs


def setup_inputs(seed=0):
    import zlib

    import numpy as np

    out = dict(_drawn_inputs(seed))
    spreads = {'L1_attn_norm_w': (1.0, 0.2),
     'L1_attn_W_D': (1.0, 0.6),
     'L1_xattn_bq': (0.0, 2.0),
     'L1_xattn_bk': (0.0, 2.0)}
    factors = {'fside_BxS2xS2_0': 2.92,
     'ctx_1024': 2.858,
     'L1_attn_conv_b': 8.0,
     'L1_attn_b_d2': 64.0,
     'L1_xattn_Wq': 64.0,
     'L1_xattn_Wk': 64.0,
     'L1_ffn_router_weight': 25.794,
     'L1_ffn_w_gate': 28.448,
     'L1_ffn_w_up': 24.756,
     'L1_ffn_w_down': 24.784,
     'L1_ffn_sw_gate': 8.0,
     'L1_ffn_sw_up': 8.0,
     'L1_ffn_sw_down': 8.0,
     'L1_ffn_sgate_w': 24.214,
     'L1_attn_W_d1': 8.0,
     'L1_attn_W_d2': 8.0,
     'L1_attn_W_Bm': 8.0,
     'L1_attn_W_Cm': 8.0,
     'L1_attn_A_log': 8.0}
    for name, (base, spread) in spreads.items():
        noise = np.random.default_rng([zlib.crc32(name.encode()), seed]).standard_normal(out[name].shape)
        drawn = base * np.exp(spread * noise) if base else spread * noise
        out[name] = jnp.asarray(drawn.astype(out[name].dtype))
    for name, factor in factors.items():
        out[name] = (out[name] * factor).astype(out[name].dtype)
    return out
```

```python
from contextlib import ExitStack, contextmanager

import numpy as np
import concourse.bass as bass
from concourse import mybir

F32 = mybir.dt.float32
BF16 = mybir.dt.bfloat16
F32R = mybir.dt.float32r
ALU = mybir.AluOpType
ACT = mybir.ActivationFunctionType
AX = mybir.AxisListType

P = 128
B, S, D = 4, 256, 256
TT = S // P
KD = D // P
T = B * S
HEADS, HD, HP = 16, 16, 32
HG = HEADS * HP // P
I0 = D // 2
FF = 1024
EI, NS, R, KC = 512, 16, 128, 4
KE = EI // P
NX, FX, FSH = 32, 96, 512
NCH = (NX * FX + FSH) // P
SCH = FSH // P
HALF = T // 2
EPS_LN = 1e-5
EPS_Q = 1e-6
QMAX = 127.0
MAGIC = 12582912.0
ROUNDS = 6


@contextmanager
def fresh_addresses(nc):
    nc.disable_value_cache = True
    yield
    nc.disable_value_cache = False


class Count:

    def __init__(self, sem, per):
        self.sem, self.per = sem, per

    def credit(self, eng):
        eng.sem_inc(self.sem, self.per)

    def now(self, eng, i, k):
        eng.wait_ge(self.sem, (i + 1) * self.per + k + 1)

    def before(self, eng, i, k):
        eng.wait_ge(self.sem, i * self.per + k + 1)


def counts(sems, **per):
    return [Count(sems.new(name), n) for name, n in per.items()]


def buffers(ctx, nc):
    def sb(name, shape, dt=F32):
        return ctx.enter_context(nc.sbuf_tensor(name, shape, dt))

    def ps(name, banks=1):
        return ctx.enter_context(nc.psum_tensor(name, [P, 512 * banks], F32))

    return sb, ps


class Semaphores:

    def __init__(self, nc):
        self.nc, self.used, self.stale, self.cleared = nc, [], [], []

    def new(self, name):
        self.used.append(self.nc.alloc_semaphore(name))
        return self.used[-1]

    def clear_stale(self, eng):
        for sem in self.stale:
            eng.sem_clear(sem)
        self.cleared, self.stale = self.stale, []

    def next_phase(self):
        for sem in self.cleared:
            self.nc.release_semaphore(sem)
        self.cleared, self.stale, self.used = [], self.stale + self.used, []


class Norm:

    def __init__(self, ctx, nc):
        sb, _ = buffers(ctx, nc)
        self.sems = Semaphores(nc)
        self.X = sb("X", [P, B, TT, D])
        self.XN = sb("XN", [P, B, TT, D])
        self.xnT = sb("xnT", [P, KD, T])
        self.stats = sb("ln_stats", [P, B * TT, 6])
        self.mv = sb("ln_mean_var", [P, B * TT, 2])
        self.ve = sb("ln_var_eps", [P, B * TT])
        self.rstd = sb("ln_rstd", [P, B * TT])
        self.mhalf = sb("minus_half", [P, B * TT])
        self.half = sb("plus_half", [P, B * TT])
        self.magic = sb("magic", [P, 1])
        self.ident = sb("identity", [P, P])
        self.ones = sb("ones", [P, P])
        sem = lambda n: nc.alloc_semaphore(n)
        self.x_loaded = sem("x_loaded")
        self.consts = sem("consts")
        self.stats_ready = sem("ln_stats_ready")
        self.mv_ready = sem("ln_mv_ready")
        self.ve_ready = sem("ln_ve_ready")
        self.rstd_ready = sem("ln_rstd_ready")
        self.xn_ready = sem("ln_xn_ready")
        self.turned = sem("ln_turned")
        self.xnT_ready = sem("ln_xnT_ready")

    def vector(self, eng, r):
        n = B * TT
        if r == 0:
            eng.wait_ge(self.x_loaded, 16 * B)
        for t in range(n):
            eng.bn_stats(self.stats[:, t, :], self.X[:, t // TT, t % TT, :]).then_inc(self.stats_ready, 1)
        for t in range(n):
            eng.wait_ge(self.stats_ready, r * n + t + 1)
            eng.bn_aggr(self.mv[:, t, :], self.stats[:, t, :]).then_inc(self.mv_ready, 1)
        eng.wait_ge(self.rstd_ready, r + 1)
        for t in range(n):
            eng.tensor_scalar(self.XN[:, t // TT, t % TT, :], self.X[:, t // TT, t % TT, :],
                              self.mv[:, t, 0:1], self.rstd[:, t:t + 1],
                              ALU.subtract, ALU.mult).then_inc(self.xn_ready, 1)

    def gpsimd(self, eng, r):
        if r == 0:
            eng.wait_ge(self.consts, 6)
        eng.wait_ge(self.mv_ready, (r + 1) * B * TT)
        eng.tensor_scalar(self.ve[:, :], self.mv[:, :, 1], EPS_LN, None, ALU.add).then_inc(self.ve_ready, 1)
        eng.wait_ge(self.ve_ready, r + 1)
        eng.tensor_tensor(self.rstd[:, :], self.ve[:, :], self.mhalf[:, :], ALU.pow).then_inc(self.rstd_ready, 1)

    def tensor(self, eng, r, banks, src=None, ready=None, per=1):
        src = self.XN if src is None else src
        if r == 0:
            eng.wait_ge(self.consts, 6)
        for b in range(B):
            if ready is None:
                eng.wait_ge(self.xn_ready, r * B * TT + TT * (b + 1))
            else:
                eng.wait_ge(ready, per * (b + 1))
            if b >= 2:
                eng.wait_ge(self.xnT_ready, r * B + b - 1)
            for h in range(TT):
                for k in range(KD):
                    mm = eng.transpose(banks[b % 2][:, k * S + h * P:k * S + (h + 1) * P],
                                       src[:, b, h, k * P:(k + 1) * P], self.ident[:, :])
            mm.then_inc(self.turned, 1)

    def scalar(self, eng, r, banks, scale=None):
        for b in range(B):
            eng.wait_ge(self.turned, r * B + b + 1)
            if scale is None:
                mm = eng.activation(self.xnT[:, :, b * S:(b + 1) * S],
                                    banks[b % 2][:, :].rearrange("p (k t) -> p k t", k=KD), ACT.Copy)
            else:
                for k in range(KD):
                    mm = eng.activation(self.xnT[:, k, b * S:(b + 1) * S],
                                        banks[b % 2][:, k * S:(k + 1) * S], ACT.Copy, scale=scale[:, k:k + 1])
            mm.then_inc(self.xnT_ready, 1)


EARLY = (
    ("wq", [P, KD, D]), ("wk", [P, KD, D]), ("wv", [P, KD, D]), ("wo", [P, KD, D]), ("fsT", [P, B, KD, D]),
    ("f_gate", [P, KD, FF]), ("f_up", [P, KD, FF]), ("f_down", [P, FF // P, D]),
)
LATE = (
    ("ctxT", [P, B, S]), ("m_small", [P, KD + 8 * KE + KE * NS]),
    ("m_skip", [P, KD, EI]), ("m_in", [P, KD, EI]), ("m_d1", [P, KE, R]), ("m_d2", [P, EI]),
    ("m_bc", [P, KE, 2 * NS]), ("m_out", [P, KE, D]),
    ("x_qk", [P, 2 * P + 2]), ("router", [P, KD, NX + 1]),
)


def weights(ctx, nc, shapes):
    sb, _ = buffers(ctx, nc)
    return {n: (sb(n, shape), nc.alloc_semaphore(f"{n}_loaded")) for n, shape in shapes}


def load_weights(eng, w, dram):
    for name, (tile, sem) in w.items():
        eng.dma_start(tile[(slice(None),) * len(tile.shape)], dram[name]).then_inc(sem, 16)


def attention(nc, nm, w, dram):
    with ExitStack() as ctx:
        sb, ps = buffers(ctx, nc)
        wqp, wkp = sb("wq_padded", [P, KD, HG * P]), sb("wk_padded", [P, KD, HG * P])
        xcur = sb("a_x", [P, KD, S])
        qT, kT = sb("a_qT", [P, HG, S]), sb("a_kT", [P, HG, S])
        V1 = sb("a_v_ones", [P, TT, HEADS, HP])
        PR = sb("a_probs", [P, 2, 4, TT, S])
        PT = sb("a_probsT", [P, 2, TT, S])
        nmax = sb("a_neg_max", [P, HEADS, TT])
        aT = sb("a_outT", [P, S])
        rden = sb("a_rden", [P, TT, 4])
        aN = sb("a_out", [P, TT, D])
        xoT = sb("a_xoT", [P, KD, S])
        SC = [ps(f"a_scores{j}") for j in range(4)]
        PTp = [ps(f"a_probsT_ps{j}") for j in range(2)]
        M0, M1 = ps("a_m0"), ps("a_m1")
        padded = nm.sems.new("a_padded")
        (xcur_ready, proj_ps, proj_sb, sc_ps, mx, mxs, ex, pt_ps, pt_sb, pv_ps, aT_sb, at_ps, rd, nrm,
         xoT_ps, xoT_sb, o_ps, x_added) = cs = counts(
            nm.sems, a_xcur_ready=1, a_proj_ps=5, a_proj_sb=5, a_sc_ps=16, a_mx=16, a_mxs=16, a_ex=32, a_pt_ps=16,
            a_pt_sb=16, a_pv_ps=16, a_aT_sb=4, a_at_ps=4, a_rd=4, a_nrm=4, a_xoT_ps=1, a_xoT_sb=1,
            a_o_ps=1, a_x_added=1)
        owner = dict(gpsimd=[xcur_ready], tensor=[proj_ps, sc_ps, pt_ps, pv_ps, at_ps, xoT_ps, o_ps],
                     vector=[mx, mxs, pt_sb, rd, nrm, x_added], scalar=[proj_sb, ex, aT_sb, xoT_sb])
        assert sum(map(len, owner.values())) == len(cs)
        block = ctx.enter_context(nc.Block())

        @block.sync
        def _(eng):
            for b in range(B):
                eng.dma_start(nm.X[:, b, :, :], dram["x"][b]).then_inc(nm.x_loaded, 16)
            load_weights(eng, w, dram)

        @block.gpsimd
        def _(eng):
            nm.sems.clear_stale(eng)
            for c in owner["gpsimd"]:
                c.credit(eng)
            eng.memset(nm.mhalf[:, :], -0.5).then_inc(nm.consts, 1)
            eng.memset(nm.half[:, :], 0.5).then_inc(nm.consts, 1)
            eng.memset(nm.ones[:, :], 1.0).then_inc(nm.consts, 1)
            eng.memset(nm.magic[:, :], MAGIC).then_inc(nm.consts, 1)
            eng.memset(nm.ident[:, :], 0.0).then_inc(nm.consts, 1)
            eng.wait_ge(nm.consts, 5)
            eng.affine_select(out=nm.ident[:, :], in_=nm.ident[:, :], compare_op=ALU.not_equal, fill=1.0,
                              base=0, pattern=[[-1, P]], channel_multiplier=1).then_inc(nm.consts, 1)
            eng.memset(wqp[:, :, :], 0.0).then_inc(padded, 1)
            eng.memset(wkp[:, :, :], 0.0).then_inc(padded, 1)
            eng.memset(V1[:, :, :, :], 1.0).then_inc(padded, 1)
            eng.wait_ge(padded, 3)
            for name, tile in (("wq", wqp), ("wk", wkp)):
                eng.wait_ge(w[name][1], 16)
                for k in range(KD):
                    eng.tensor_copy(tile[:, k, :].rearrange("p (h c) -> p h c", c=HP)[:, :, 0:HD],
                                    w[name][0][:, k, :].rearrange("p (h c) -> p h c", c=HD)).then_inc(padded, 1)
            nm.gpsimd(eng, 0)
            eng.wait_ge(nm.xnT_ready, B)
            with eng.Fori(0, B) as i:
                proj_ps.before(eng, i, 4)
                eng.tensor_copy(xcur[:, :, :], nm.xnT[:, :, bass.ds(i * S, S)]).then_inc(xcur_ready.sem, 1)

        @block.tensor
        def _(eng):
            for c in owner["tensor"]:
                c.credit(eng)
            nm.tensor(eng, 0, PTp)
            eng.wait_ge(nm.xnT_ready, B)
            eng.wait_ge(padded, 7)
            eng.wait_ge(w["wv"][1], 16)
            eng.wait_ge(w["wo"][1], 16)

            def project(i):
                xcur_ready.now(eng, i, 0)
                for n in range(4):
                    bank = (M0, M1)[n % 2]
                    if n == 0:
                        x_added.before(eng, i, 0)
                    elif n == 1:
                        xoT_sb.before(eng, i, 0)
                    else:
                        proj_sb.now(eng, i, n - 2)
                    for a in range(2):
                        g = 2 * (n % 2) + a
                        for k in range(KD):
                            mm = eng.matmul(bank[:, a * S:(a + 1) * S], (wqp, wkp)[n // 2][:, k, g * P:(g + 1) * P],
                                            xcur[:, k, :], start=(k == 0), stop=(k == KD - 1))
                    mm.then_inc(proj_ps.sem, 1)
                proj_sb.now(eng, i, 2)
                for h in range(TT):
                    for k in range(KD):
                        mm = eng.matmul(M0[:, h * D:(h + 1) * D], xcur[:, k, h * P:(h + 1) * P],
                                        w["wv"][0][:, k, :], start=(k == 0), stop=(k == KD - 1))
                mm.then_inc(proj_ps.sem, 1)

            def scores(i, g):
                proj_sb.now(eng, i, 2 + g // 2)
                for h in range(TT):
                    for j in range(4):
                        if h == 0:
                            (ex.now(eng, i, 8 * (g - 1) + 2 * j + 1) if g else ex.before(eng, i, 24 + 2 * j + 1))
                        mm = eng.matmul(SC[j][:, h * S:(h + 1) * S], qT[HP * j:HP * (j + 1), g, h * P:(h + 1) * P],
                                        kT[HP * j:HP * (j + 1), g, :], start=True, stop=True)
                        if h == TT - 1:
                            mm.then_inc(sc_ps.sem, 1)

            def turn(i, g, j):
                u = 4 * g + j
                ex.now(eng, i, 8 * g + 2 * j + 1)
                (pt_sb.now(eng, i, u - 2) if u >= 2 else pt_sb.before(eng, i, 14 + u))
                for c in range(TT):
                    for h in range(TT):
                        mm = eng.transpose(PTp[j % 2][:, c * S + h * P:c * S + (h + 1) * P],
                                           PR[:, g % 2, j, h, c * P:(c + 1) * P], nm.ident[:, :])
                mm.then_inc(pt_ps.sem, 1)

            def values(i, g, j):
                pt_sb.now(eng, i, 4 * g + j)
                if g == 0 and j == 0:
                    proj_sb.now(eng, i, 4)
                if j == 0 and g:
                    aT_sb.now(eng, i, g - 1)
                for c in range(TT):
                    mm = eng.matmul(M1[HP * j:HP * (j + 1), 0:S], V1[:, c, 4 * g + j, :], PT[:, j % 2, c, :],
                                    start=(c == 0), stop=(c == TT - 1))
                mm.then_inc(pv_ps.sem, 1)

            def turn_back(i, g):
                aT_sb.now(eng, i, g)
                if g:
                    nrm.now(eng, i, g - 1)
                for h in range(TT):
                    mm = eng.transpose(M0[:, h * P:(h + 1) * P], aT[:, h * P:(h + 1) * P], nm.ident[:, :])
                mm.then_inc(at_ps.sem, 1)

            with eng.Fori(0, B) as i:
                project(i)
                scores(i, 0)
                for g in range(HG):
                    turn(i, g, 0)
                    if g:
                        turn_back(i, g - 1)
                    turn(i, g, 1)
                    values(i, g, 0)
                    turn(i, g, 2)
                    values(i, g, 1)
                    turn(i, g, 3)
                    if g < HG - 1:
                        scores(i, g + 1)
                    values(i, g, 2)
                    values(i, g, 3)
                turn_back(i, HG - 1)
                nrm.now(eng, i, HG - 1)
                for h in range(TT):
                    for k in range(KD):
                        mm = eng.transpose(M1[:, k * S + h * P:k * S + (h + 1) * P], aN[:, h, k * P:(k + 1) * P],
                                           nm.ident[:, :])
                mm.then_inc(xoT_ps.sem, 1)
                xoT_sb.now(eng, i, 0)
                for h in range(TT):
                    for k in range(KD):
                        mm = eng.matmul(M0[:, h * D:(h + 1) * D], xoT[:, k, h * P:(h + 1) * P], w["wo"][0][:, k, :],
                                        start=(k == 0), stop=(k == KD - 1))
                mm.then_inc(o_ps.sem, 1)

        @block.vector
        def _(eng):
            for c in owner["vector"]:
                c.credit(eng)
            nm.vector(eng, 0)

            with eng.Fori(0, B) as i:
                for g in range(HG):
                    for j in range(4):
                        h4 = 4 * g + j
                        sc_ps.now(eng, i, h4)
                        ex.before(eng, i, 2 * h4 + 1)
                        eng.tensor_reduce(nmax[:, h4, :], SC[j][:, :].rearrange("p (h t) -> p h t", h=TT),
                                          AX.X, ALU.max, negate=True).then_inc(mx.sem, 1)
                        mx.now(eng, i, h4)
                        eng.tensor_scalar(nmax[:, h4, :], nmax[:, h4, :], HD ** -0.5, None,
                                          ALU.mult).then_inc(mxs.sem, 1)
                    for j in range(4):
                        u = 4 * g + j
                        pt_ps.now(eng, i, u)
                        (pv_ps.now(eng, i, u - 2) if u >= 2 else pv_ps.before(eng, i, 14 + u))
                        eng.tensor_copy(PT[:, j % 2, :, :],
                                        PTp[j % 2][:, :].rearrange("p (c t) -> p c t", c=TT)).then_inc(pt_sb.sem, 1)
                    for gg in ((g - 1,) if g < HG - 1 else (g - 1, g)):
                        if gg < 0:
                            continue
                        at_ps.now(eng, i, gg)
                        view = M0[:, 0:TT * P].rearrange("p (h j c) -> p h j c", h=TT, j=4)
                        if gg:
                            nrm.now(eng, i, gg - 1)
                        else:
                            nrm.before(eng, i, HG - 1)
                        eng.reciprocal(rden[:, :, :], view[:, :, :, HD]).then_inc(rd.sem, 1)
                        rd.now(eng, i, gg)
                        xoT_ps.before(eng, i, 0)
                        for h in range(TT):
                            op = eng.tensor_tensor(
                                aN[:, h, gg * 4 * HD:(gg + 1) * 4 * HD].rearrange("p (j c) -> p j c", j=4),
                                view[:, h, :, 0:HD], rden[:, h, :, None].to_broadcast((P, 4, HD)), ALU.mult)
                            op.then_inc(nrm.sem, 1) if h == TT - 1 else None
                o_ps.now(eng, i, 0)
                eng.tensor_tensor(nm.X[:, i, :, :], nm.X[:, i, :, :],
                                  M0[:, :].rearrange("p (h f) -> p h f", h=TT), ALU.add).then_inc(x_added.sem, 1)

        @block.scalar
        def _(eng):
            for c in owner["scalar"]:
                c.credit(eng)
            nm.scalar(eng, 0, PTp)

            def exps(i, g):
                for j in range(4):
                    mxs.now(eng, i, 4 * g + j)
                    if g < 2:
                        pt_ps.before(eng, i, 4 * (g + 2) + j)
                    else:
                        pt_ps.now(eng, i, 4 * (g - 2) + j)
                    for h in range(TT):
                        eng.activation(PR[:, g % 2, j, h, :], SC[j][:, h * S:(h + 1) * S], ACT.Exp,
                                       bias=nmax[:, 4 * g + j, h:h + 1], scale=HD ** -0.5).then_inc(ex.sem, 1)

            def keep_outT(i, g):
                pv_ps.now(eng, i, 4 * g + 3)
                (at_ps.now(eng, i, g - 1) if g else at_ps.before(eng, i, HG - 1))
                eng.activation(aT[:, :], M1[:, 0:S], ACT.Copy).then_inc(aT_sb.sem, 1)

            with eng.Fori(0, B) as i:
                for n in range(4):
                    proj_ps.now(eng, i, n)
                    sc_ps.before(eng, i, 15)
                    eng.activation((qT, kT)[n // 2][:, 2 * (n % 2):2 * (n % 2) + 2, :],
                                   (M0, M1)[n % 2][:, :].rearrange("p (a t) -> p a t", a=2), ACT.Copy).then_inc(proj_sb.sem, 1)
                proj_ps.now(eng, i, 4)
                pv_ps.before(eng, i, 15)
                eng.wait_ge(padded, 7)
                eng.activation(V1[:, :, :, 0:HD], M0[:, :].rearrange("p (h n c) -> p h n c", h=TT, c=HD),
                               ACT.Copy).then_inc(proj_sb.sem, 1)
                for g in range(HG):
                    exps(i, g)
                    if g:
                        keep_outT(i, g - 1)
                keep_outT(i, HG - 1)
                xoT_ps.now(eng, i, 0)
                o_ps.before(eng, i, 0)
                eng.activation(xoT[:, :, :], M1[:, :].rearrange("p (k t) -> p k t", k=KD), ACT.Copy).then_inc(xoT_sb.sem, 1)


def quantised(nc, nm, w, dram):
    with ExitStack() as ctx:
        sb, ps = buffers(ctx, nc)
        am = sb("q_amax", [P, 5])
        amf = sb("q_amax_floor", [P, 5])
        rw = sb("q_recip_w", [P, 3])
        ratio, root = sb("q_ratio", [P, 2]), sb("q_root", [P, 2])
        s1, rs1 = sb("q_s1", [P, 2]), sb("q_rs1", [P, 2])
        OP = sb("q_scaled", [P, 4, S])
        ra, sc, rsc = sb("q_row_amax", [P, 4]), sb("q_scale", [P, 4]), sb("q_rscale", [P, 4])
        Q1, Q2 = sb("q_shifted", [P, 4, S]), sb("q_clipped", [P, 4, S])
        QT = sb("q_turned", [P, 4, S], BF16)
        diag = sb("q_diag", [P, 2, P])
        XS = sb("q_x_scale_row", [P, S])
        gd, ud, sg, aa = (sb(f"q_{n}", [P, S]) for n in ("gate", "up", "silu", "act"))
        am2, amf2 = sb("q_amax2", [P, 1]), sb("q_amax2_floor", [P, 1])
        ratio2, root2 = sb("q_ratio2", [P, 1]), sb("q_root2", [P, 1])
        s2, rs2 = sb("q_s2", [P, 1]), sb("q_rs2", [P, 1])
        OP2 = sb("q_scaled2", [P, 2, S])
        ra2, sc2, rsc2 = sb("q_row_amax2", [P, 4]), sb("q_scale2", [P, 4]), sb("q_rscale2", [P, 4])
        Q3, Q4 = sb("q_shifted2", [P, 4, P]), sb("q_clipped2", [P, 4, P])
        QT2 = sb("q_turned2", [P, 4, P], BF16)
        diag2 = sb("q_diag2", [P, 2, P])
        WS = sb("q_w_scale_row", [P, S])
        yd = sb("q_y", [P, TT, D])
        TP = ps("q_tp", 2)
        TB = ps("q_tb", 2)
        GU = ps("q_gu")
        T2, B2 = ps("q_t2"), ps("q_b2")
        RW = ps("q_rows")
        (am_r, amf_r, rw_r, rt_r, root_r, s_r, rs_r, op_r, ra_r, sc_r, rsc_r, q2_r, dg_r, gd_r, ud_r, aa_r,
         am2_r, amf2_r, rt2_r, s2_r, rs2_r, op2_r, ra2_r, sc2_r, rsc2_r, q4_r, dg2_r, y_r, x_r,
         root2_r, tp_r, tb_r, xsr_r, gu_r, t2_r, b2_r, wsr_r, yy_r,
         q1_r, qt_r, xs_r, sg_r, q3_r, qt2_r, ws_r) = cs = counts(
            nm.sems, q_am=3, q_amf=1, q_rw=1, q_rt=1, q_root_r=1, q_s=1, q_rs=1, q_op=4, q_ra=2, q_sc=1, q_rsc=1,
            q_q2=1, q_dg=2, q_gd=1, q_ud=1, q_aa=1, q_am2=1, q_amf2=1, q_rt2=1, q_s2r=1, q_rs2r=1, q_op2=2,
            q_ra2=1, q_sc2=1, q_rsc2=1, q_q4=1, q_dg2=2, q_yr=2, q_xr=1, q_root2r=1, q_tp_r=2, q_tb_r=2, q_xsr=1,
            q_gu_r=2, q_t2r=1, q_b2r=1, q_wsr=1, q_yyr=1, q_q1=4, q_qt=2, q_xs=1, q_sgr=1, q_q3=4, q_qt2=1, q_wsr2=1)
        pool = [root_r, root2_r]
        pe = [tp_r, tb_r, xsr_r, gu_r, t2_r, b2_r, wsr_r, yy_r]
        act = [q1_r, qt_r, xs_r, sg_r, q3_r, qt2_r, ws_r]
        block = ctx.enter_context(nc.Block())

        @block.gpsimd
        def _(eng):
            nm.sems.clear_stale(eng)
            for c in pool:
                c.credit(eng)
            nm.gpsimd(eng, 1)
            with eng.Fori(0, B) as i:
                rt_r.now(eng, i, 0)
                eng.tensor_tensor(root[:, :], ratio[:, :], nm.half[:, 0:2], ALU.pow).then_inc(root_r.sem, 1)
                rt2_r.now(eng, i, 0)
                eng.tensor_tensor(root2[:, :], ratio2[:, :], nm.half[:, 0:1], ALU.pow).then_inc(root2_r.sem, 1)

        @block.tensor
        def _(eng):
            for c in pe:
                c.credit(eng)
            nm.tensor(eng, 1, (GU, T2))
            eng.wait_ge(nm.xnT_ready, 2 * B)
            with eng.Fori(0, B) as i:
                for o in range(2):
                    op_r.now(eng, i, 2 * o + 1)
                    q1_r.before(eng, i, 2 * o + 1)
                    for r in range(2):
                        for k in range(KD):
                            mm = eng.transpose(TP[:, (2 * o + r) * D + k * P:(2 * o + r) * D + (k + 1) * P],
                                               OP[:, 2 * o + k, r * P:(r + 1) * P], nm.ident[:, :])
                    mm.then_inc(tp_r.sem, 1)
                dg_r.now(eng, i, 1)
                xs_r.before(eng, i, 0)
                ws_r.before(eng, i, 0)
                for r in range(2):
                    mm = eng.matmul(RW[:, r * P:(r + 1) * P], nm.ones[:, :], diag[:, r, :], start=True, stop=True)
                mm.then_inc(xsr_r.sem, 1)
                q2_r.now(eng, i, 0)
                for o in range(2):
                    qt_r.before(eng, i, o)
                    for r in range(2):
                        for k in range(KD):
                            mm = eng.transpose(TB[:, (2 * o + k) * S + r * P:(2 * o + k) * S + (r + 1) * P],
                                               Q2[:, 2 * o + r, k * P:(k + 1) * P], nm.ident[:, :])
                    mm.then_inc(tb_r.sem, 1)
                qt_r.now(eng, i, 1)
                ud_r.before(eng, i, 0)
                for o in range(2):
                    for k in range(KD):
                        mm = eng.matmul(GU[:, o * S:(o + 1) * S], QT[:, 2 + k, o * P:(o + 1) * P], QT[:, k, :],
                                        start=(k == 0), stop=(k == KD - 1))
                    mm.then_inc(gu_r.sem, 1)
                op2_r.now(eng, i, 1)
                q3_r.before(eng, i, 3)
                for o in range(2):
                    for r in range(2):
                        mm = eng.transpose(T2[:, (2 * o + r) * P:(2 * o + r + 1) * P], OP2[:, o, r * P:(r + 1) * P],
                                           nm.ident[:, :])
                mm.then_inc(t2_r.sem, 1)
                dg2_r.now(eng, i, 1)
                ws_r.before(eng, i, 0)
                xs_r.now(eng, i, 0)
                for r in range(2):
                    mm = eng.matmul(RW[:, S + r * P:S + (r + 1) * P], nm.ones[:, :], diag2[:, r, :], start=True, stop=True)
                mm.then_inc(wsr_r.sem, 1)
                q4_r.now(eng, i, 0)
                qt2_r.before(eng, i, 0)
                for r in range(4):
                    mm = eng.transpose(B2[:, r * P:(r + 1) * P], Q4[:, r, :], nm.ident[:, :])
                mm.then_inc(b2_r.sem, 1)
                qt2_r.now(eng, i, 0)
                ud_r.now(eng, i, 0)
                y_r.before(eng, i, 1)
                for h in range(TT):
                    mm = eng.matmul(GU[:, h * D:(h + 1) * D], QT2[:, h, :], QT2[:, 2:4, :], start=True, stop=True)
                mm.then_inc(yy_r.sem, 1)

        @block.scalar
        def _(eng):
            for c in act:
                c.credit(eng)
            nm.scalar(eng, 1, (GU, T2))
            with eng.Fori(0, B) as i:
                rsc_r.now(eng, i, 0)
                for r in range(4):
                    q2_r.before(eng, i, 0)
                    tp_r.now(eng, i, r // 2)
                    eng.activation(Q1[:, r, :], TP[:, r * D:(r + 1) * D], ACT.Identity, bias=nm.magic[:, 0:1],
                                   scale=rsc[:, r:r + 1]).then_inc(q1_r.sem, 1)
                xsr_r.now(eng, i, 0)
                ud_r.before(eng, i, 0)
                eng.activation(XS[:, :], RW[:, 0:S], ACT.Copy).then_inc(xs_r.sem, 1)
                for o in range(2):
                    tb_r.now(eng, i, o)
                    gu_r.before(eng, i, 1)
                    eng.activation(QT[:, 2 * o:2 * o + 2, :], TB[:, 2 * o * S:(2 * o + 2) * S].rearrange("p (k t) -> p k t", k=2),
                                   ACT.Copy, bias=-MAGIC).then_inc(qt_r.sem, 1)
                gd_r.now(eng, i, 0)
                aa_r.before(eng, i, 0)
                eng.activation(sg[:, :], gd[:, :], ACT.Silu).then_inc(sg_r.sem, 1)
                rsc2_r.now(eng, i, 0)
                t2_r.now(eng, i, 0)
                q4_r.before(eng, i, 0)
                for r in range(4):
                    eng.activation(Q3[:, r, :], T2[:, r * P:(r + 1) * P], ACT.Identity, bias=nm.magic[:, 0:1],
                                   scale=rsc2[:, r:r + 1]).then_inc(q3_r.sem, 1)
                wsr_r.now(eng, i, 0)
                y_r.before(eng, i, 1)
                eng.activation(WS[:, :], RW[:, S:2 * S], ACT.Copy).then_inc(ws_r.sem, 1)
                b2_r.now(eng, i, 0)
                yy_r.before(eng, i, 0)
                eng.activation(QT2[:, :, :], B2[:, :].rearrange("p (r t) -> p r t", r=4), ACT.Copy,
                               bias=-MAGIC).then_inc(qt2_r.sem, 1)

        @block.vector
        def _(eng):
            for c in cs:
                if c not in pool + pe + act:
                    c.credit(eng)
            nm.vector(eng, 1)
            eng.wait_ge(nm.xnT_ready, 2 * B)
            eng.wait_ge(w["fsT"][1], 16)
            eng.wait_ge(w["ctxT"][1], 16)
            fsT, ctxT = w["fsT"][0], w["ctxT"][0]
            with eng.Fori(0, B) as i:
                xb = nm.xnT[:, :, bass.ds(i * S, S)]
                amf_r.before(eng, i, 0)
                eng.tensor_reduce(am[:, 0:2], xb, AX.X, ALU.max, apply_absolute_value=True).then_inc(am_r.sem, 1)
                eng.tensor_reduce(am[:, 2:4], fsT[:, i, :, :], AX.X, ALU.max, apply_absolute_value=True).then_inc(am_r.sem, 1)
                eng.tensor_reduce(am[:, 4:5], ctxT[:, i, :], AX.X, ALU.max, apply_absolute_value=True).then_inc(am_r.sem, 1)
                am_r.now(eng, i, 2)
                rt2_r.before(eng, i, 0)
                eng.tensor_scalar(amf[:, :], am[:, :], EPS_Q, None, ALU.max).then_inc(amf_r.sem, 1)
                amf_r.now(eng, i, 0)
                eng.reciprocal(rw[:, :], amf[:, 2:5]).then_inc(rw_r.sem, 1)
                rw_r.now(eng, i, 0)
                root_r.before(eng, i, 0)
                eng.tensor_tensor(ratio[:, :], amf[:, 0:2], rw[:, 0:2], ALU.mult).then_inc(rt_r.sem, 1)
                root_r.now(eng, i, 0)
                op_r.before(eng, i, 3)
                eng.tensor_scalar(s1[:, :], root[:, :], EPS_Q, None, ALU.max).then_inc(s_r.sem, 1)
                s_r.now(eng, i, 0)
                eng.reciprocal(rs1[:, :], s1[:, :]).then_inc(rs_r.sem, 1)
                rs_r.now(eng, i, 0)
                tp_r.before(eng, i, 1)
                for k in range(KD):
                    eng.tensor_scalar(OP[:, k, :], nm.xnT[:, k, bass.ds(i * S, S)], rs1[:, k:k + 1], None,
                                      ALU.mult).then_inc(op_r.sem, 1)
                for k in range(KD):
                    eng.tensor_scalar(OP[:, 2 + k, :], fsT[:, i, k, :], s1[:, k:k + 1], None, ALU.mult).then_inc(op_r.sem, 1)
                for o in range(2):
                    tp_r.now(eng, i, o)
                    sc_r.before(eng, i, 0)
                    eng.tensor_reduce(ra[:, 2 * o:2 * o + 2], TP[:, 2 * o * D:(2 * o + 2) * D].rearrange("p (r f) -> p r f", r=2),
                                      AX.X, ALU.max, apply_absolute_value=True).then_inc(ra_r.sem, 1)
                ra_r.now(eng, i, 1)
                dg_r.before(eng, i, 1)
                ud_r.before(eng, i, 0)
                eng.tensor_scalar(sc[:, :], ra[:, :], EPS_Q, 1.0 / QMAX, ALU.max, ALU.mult).then_inc(sc_r.sem, 1)
                sc_r.now(eng, i, 0)
                q1_r.before(eng, i, 3)
                eng.reciprocal(rsc[:, :], sc[:, :]).then_inc(rsc_r.sem, 1)
                xsr_r.before(eng, i, 0)
                for r in range(2):
                    eng.tensor_scalar(diag[:, r, :], nm.ident[:, :], sc[:, r:r + 1], None, ALU.mult).then_inc(dg_r.sem, 1)
                q1_r.now(eng, i, 3)
                tb_r.before(eng, i, 1)
                eng.tensor_scalar(Q2[:, :, :], Q1[:, :, :], MAGIC + QMAX, MAGIC - QMAX, ALU.min, ALU.max).then_inc(q2_r.sem, 1)
                xs_r.now(eng, i, 0)
                gu_r.now(eng, i, 1)
                sg_r.before(eng, i, 0)
                eng.scalar_tensor_tensor(gd[:, :], GU[:, 0:S], sc[:, 2:3], XS[:, :], ALU.mult, ALU.mult).then_inc(gd_r.sem, 1)
                aa_r.before(eng, i, 0)
                eng.scalar_tensor_tensor(ud[:, :], GU[:, S:2 * S], sc[:, 3:4], XS[:, :], ALU.mult, ALU.mult).then_inc(ud_r.sem, 1)
                sg_r.now(eng, i, 0)
                ud_r.now(eng, i, 0)
                op2_r.before(eng, i, 1)
                am2_r.before(eng, i, 0)
                eng.tensor_tensor(aa[:, :], sg[:, :], ud[:, :], ALU.mult).then_inc(aa_r.sem, 1)
                aa_r.now(eng, i, 0)
                amf2_r.before(eng, i, 0)
                eng.tensor_reduce(am2[:, :], aa[:, :], AX.X, ALU.max, apply_absolute_value=True).then_inc(am2_r.sem, 1)
                am2_r.now(eng, i, 0)
                eng.tensor_scalar(amf2[:, :], am2[:, :], EPS_Q, None, ALU.max).then_inc(amf2_r.sem, 1)
                amf2_r.now(eng, i, 0)
                root2_r.before(eng, i, 0)
                eng.tensor_tensor(ratio2[:, :], amf2[:, :], rw[:, 2:3], ALU.mult).then_inc(rt2_r.sem, 1)
                root2_r.now(eng, i, 0)
                op2_r.before(eng, i, 1)
                eng.tensor_scalar(s2[:, :], root2[:, :], EPS_Q, None, ALU.max).then_inc(s2_r.sem, 1)
                s2_r.now(eng, i, 0)
                eng.reciprocal(rs2[:, :], s2[:, :]).then_inc(rs2_r.sem, 1)
                rs2_r.now(eng, i, 0)
                t2_r.before(eng, i, 0)
                eng.tensor_scalar(OP2[:, 0, :], aa[:, :], rs2[:, 0:1], None, ALU.mult).then_inc(op2_r.sem, 1)
                eng.tensor_scalar(OP2[:, 1, :], ctxT[:, i, :], s2[:, 0:1], None, ALU.mult).then_inc(op2_r.sem, 1)
                t2_r.now(eng, i, 0)
                sc2_r.before(eng, i, 0)
                eng.tensor_reduce(ra2[:, :], T2[:, :].rearrange("p (r f) -> p r f", r=4), AX.X, ALU.max,
                                  apply_absolute_value=True).then_inc(ra2_r.sem, 1)
                ra2_r.now(eng, i, 0)
                y_r.before(eng, i, 1)
                eng.tensor_scalar(sc2[:, :], ra2[:, :], EPS_Q, 1.0 / QMAX, ALU.max, ALU.mult).then_inc(sc2_r.sem, 1)
                sc2_r.now(eng, i, 0)
                q3_r.before(eng, i, 3)
                eng.reciprocal(rsc2[:, :], sc2[:, :]).then_inc(rsc2_r.sem, 1)
                wsr_r.before(eng, i, 0)
                for r in range(2):
                    eng.tensor_scalar(diag2[:, r, :], nm.ident[:, :], sc2[:, 2 + r:3 + r], None, ALU.mult).then_inc(dg2_r.sem, 1)
                q3_r.now(eng, i, 3)
                b2_r.before(eng, i, 0)
                eng.tensor_scalar(Q4[:, :, :], Q3[:, :, :], MAGIC + QMAX, MAGIC - QMAX, ALU.min, ALU.max).then_inc(q4_r.sem, 1)
                yy_r.now(eng, i, 0)
                ws_r.now(eng, i, 0)
                x_r.before(eng, i, 0)
                for h in range(TT):
                    eng.scalar_tensor_tensor(yd[:, h, :], GU[:, h * D:(h + 1) * D], sc2[:, h:h + 1], WS[:, :],
                                             ALU.mult, ALU.mult).then_inc(y_r.sem, 1)
                y_r.now(eng, i, 1)
                eng.tensor_tensor(nm.X[:, i, :, :], nm.X[:, i, :, :], yd[:, :, :], ALU.add).then_inc(x_r.sem, 1)


def sparse(nc, nm, w, dram):
    with ExitStack() as ctx:
        sb, ps = buffers(ctx, nc)
        H, A = sb("s_h", [P, 4, HALF]), sb("s_abs", [P, 4, HALF])
        SG = sb("s_silu", [P, 2, HALF])
        C = sb("s_wins", [P, 6, HALF], BF16)
        W1 = sb("s_sums1", [P, 4, HALF], BF16)
        W2 = sb("s_sums2", [P, 4, HALF], BF16)
        HS = sb("s_kept", [P, 2, 4, HALF])
        GP, UP = [ps(f"s_gate{n}") for n in range(2)], [ps(f"s_up{n}") for n in range(2)]
        OUT = [ps(f"s_out{n}") for n in range(2)]
        NT = HALF // P
        (g_ps, u_ps, o_ps, sg_r, ab_r, h_r, c_r, hs_r, x_r, w1_r, w2_r) = cs = counts(
            nm.sems, s_gate_ps=8, s_up_ps=8, s_down=2, s_silu_r=8, s_abs_r=2, s_h_r=8, s_c_r=8, s_hs_r=8, s_x_r=1,
            s_w1_r=8, s_w2_r=8)
        pe, act, pool = [g_ps, u_ps, o_ps], [sg_r, ab_r], [w1_r, w2_r]
        block = ctx.enter_context(nc.Block())
        gate, up, down = w["f_gate"][0], w["f_up"][0], w["f_down"][0]

        @block.gpsimd
        def _(eng):
            nm.sems.clear_stale(eng)
            for c in pool:
                c.credit(eng)
            nm.gpsimd(eng, 2)
            with eng.Fori(0, 2) as i:
                for gb in range(2):
                    c_r.now(eng, i, 4 * gb + 3)
                    (w2_r.now(eng, i, 3) if gb else w2_r.before(eng, i, 7))
                    for j, (a, b) in enumerate(((0, 2), (5, 3), (2, 5), (4, 3))):
                        eng.tensor_tensor(W1[:, j, :], C[:, a, :], C[:, b, :], ALU.add).then_inc(w1_r.sem, 1)
                    w1_r.now(eng, i, 4 * gb + 3)
                    (hs_r.now(eng, i, 3) if gb else hs_r.before(eng, i, 7))
                    eng.tensor_tensor(W2[:, 0, :], W1[:, 0, :], C[:, 4, :], ALU.add).then_inc(w2_r.sem, 1)
                    eng.tensor_tensor(W2[:, 1, :], W1[:, 1, :], C[:, 0, :], ALU.subtract).then_inc(w2_r.sem, 1)
                    eng.tensor_tensor(W2[:, 2, :], C[:, 1, :], W1[:, 2, :], ALU.subtract).then_inc(w2_r.sem, 1)
                    eng.tensor_tensor(W2[:, 3, :], W1[:, 3, :], C[:, 1, :], ALU.add).then_inc(w2_r.sem, 1)

        @block.tensor
        def _(eng):
            for c in pe:
                c.credit(eng)
            nm.tensor(eng, 2, GP)
            eng.wait_ge(nm.xnT_ready, 3 * B)
            for name in ("f_gate", "f_up", "f_down"):
                eng.wait_ge(w[name][1], 16)

            def gates(i, gb, j):
                u = 4 * gb + j
                xh = lambda k: nm.xnT[:, k, bass.ds(i * HALF, HALF)]
                if u >= 2:
                    sg_r.now(eng, i, u - 2)
                    h_r.now(eng, i, u - 2)
                else:
                    sg_r.before(eng, i, 6 + u)
                    h_r.before(eng, i, 6 + u)
                for bank, wt, c in ((GP[j % 2], gate, g_ps), (UP[j % 2], up, u_ps)):
                    for k in range(KD):
                        mm = eng.matmul(bank[:, :], wt[:, k, u * P:(u + 1) * P], xh(k), start=(k == 0), stop=(k == KD - 1))
                    mm.then_inc(c.sem, 1)

            def downs(i, gb):
                for j in range(4):
                    hs_r.now(eng, i, 4 * gb + j)
                    if gb == 0 and j == 0:
                        x_r.before(eng, i, 0)
                    for t in range(NT):
                        mm = eng.matmul(OUT[t // 2][:, (t % 2) * D:(t % 2 + 1) * D], HS[:, gb, j, t * P:(t + 1) * P],
                                        down[:, 4 * gb + j, :], start=(gb == 0 and j == 0 and t % 2 == 0),
                                        stop=(gb == 1 and j == 3), skip_group_check=True)
                mm.then_inc(o_ps.sem, 1)

            with eng.Fori(0, 2) as i:
                for gb in range(2):
                    for j in range(4):
                        gates(i, gb, j)
                    if gb:
                        downs(i, 0)
                downs(i, 1)

        @block.scalar
        def _(eng):
            for c in act:
                c.credit(eng)
            nm.scalar(eng, 2, GP)
            with eng.Fori(0, 2) as i:
                for gb in range(2):
                    for j in range(4):
                        u = 4 * gb + j
                        g_ps.now(eng, i, u)
                        (h_r.now(eng, i, u - 2) if u >= 2 else h_r.before(eng, i, 6 + u))
                        eng.activation(SG[:, j % 2, :], GP[j % 2][:, :], ACT.Silu).then_inc(sg_r.sem, 1)
                    h_r.now(eng, i, 4 * gb + 3)
                    (c_r.now(eng, i, 3) if gb else c_r.before(eng, i, 7))
                    eng.activation(A[:, :, :], H[:, :, :], ACT.Abs).then_inc(ab_r.sem, 1)

        @block.vector
        def _(eng):
            for c in cs:
                if c not in pe + act + pool:
                    c.credit(eng)
            nm.vector(eng, 2)
            with eng.Fori(0, 2) as i:
                for gb in range(2):
                    for j in range(4):
                        u = 4 * gb + j
                        sg_r.now(eng, i, u)
                        u_ps.now(eng, i, u)
                        (hs_r.now(eng, i, 3) if gb else hs_r.before(eng, i, 7))
                        (ab_r.now(eng, i, 0) if gb else ab_r.before(eng, i, 1))
                        eng.tensor_tensor(H[:, j, :], SG[:, j % 2, :], UP[j % 2][:, :], ALU.mult).then_inc(h_r.sem, 1)
                    ab_r.now(eng, i, gb)
                    (w2_r.now(eng, i, 3) if gb else w2_r.before(eng, i, 7))
                    eng.tensor_tensor(C[:, 0:2, :], A[:, 0:4:2, :], A[:, 1:4:2, :], ALU.is_ge).then_inc(c_r.sem, 1)
                    eng.tensor_tensor(C[:, 2:4, :], A[:, 0:2, :], A[:, 2:4, :], ALU.is_ge).then_inc(c_r.sem, 1)
                    eng.tensor_tensor(C[:, 4, :], A[:, 0, :], A[:, 3, :], ALU.is_ge).then_inc(c_r.sem, 1)
                    eng.tensor_tensor(C[:, 5, :], A[:, 1, :], A[:, 2, :], ALU.is_ge).then_inc(c_r.sem, 1)
                    o_ps.before(eng, i, gb)
                    for j, (least, op) in enumerate(((2.0, ALU.is_ge), (1.0, ALU.is_ge), (0.0, ALU.is_ge), (1.0, ALU.is_le))):
                        w2_r.now(eng, i, 4 * gb + 3)
                        eng.scalar_tensor_tensor(HS[:, gb, j, :], W2[:, j, :], least, H[:, j, :], op, ALU.mult).then_inc(hs_r.sem, 1)
                o_ps.now(eng, i, 1)
                for n in range(2):
                    op = eng.tensor_tensor(nm.X[:, bass.ds(i * 2 + n, 1), :, :], nm.X[:, bass.ds(i * 2 + n, 1), :, :],
                                           OUT[n][:, :].rearrange("p (b h f) -> p b h f", b=1, h=TT), ALU.add)
                op.then_inc(x_r.sem, 1)


def scan_inputs(nc, nm, w, dram, keep):
    with ExitStack() as ctx:
        sb, ps = buffers(ctx, nc)
        NT = B * TT
        sq = sb("m_square", [P, D])
        ss, ms, rms = sb("m_sum_sq", [P, NT]), sb("m_mean_sq", [P, NT]), sb("m_rms", [P, NT])
        XR = sb("m_xr", [P, B, TT, D])
        cin = sb("m_conv_in", [P, 2, 2, S + KC - 1])
        cv = sb("m_conv", [P, 2, 2, S])
        d1 = sb("m_d1T", [P, HALF])
        az, ez, lz = sb("m_abs_z", [P, HALF]), sb("m_exp_z", [P, HALF]), sb("m_ln_z", [P, HALF])
        bc = sb("m_bcT", [2 * NS, T])
        small = w["m_small"][0]
        norm_w, conv_b, b_d2 = small[:, 0:KD], small[:, KD:KD + KE], small[:, KD + KE:KD + 2 * KE]
        conv_w = small[:, KD + 4 * KE:KD + 4 * KE + KE * KC]
        a_log = small[:, KD + 4 * KE + KE * KC:]
        IN, SK = [ps(f"m_in{n}") for n in range(2)], [ps(f"m_skip{n}") for n in range(2)]
        D2 = [ps(f"m_d2_{n}") for n in range(2)]
        D1, BC = ps("m_d1_ps"), ps("m_bc_ps")
        sem = lambda n: nm.sems.new(n)
        sq_ready, ms_ready, rms_ready, xr_ready = sem("m_sq"), sem("m_ms"), sem("m_rms_r"), sem("m_xr_r")
        a_ready, padded, nw_ready, bc_out = sem("m_a"), sem("m_pad"), sem("m_nw"), sem("m_bc_out")
        (in_ps, sk_ps, d1_ps, d2_ps, bc_ps, cin_r, x2_r, gt_r, d1_r, bc_r, az_r, ez_r, lz_r, cv_r, tap_r, rz_r,
         dl_r, dx_r) = cs = counts(
            nm.sems, m_in_ps=4, m_sk_ps=4, m_d1p=1, m_d2p=4, m_bcp=1, m_cin_r=4, m_x2_r=4, m_gt_r=4, m_d1r=1,
            m_bc_r=1, m_az_r=4, m_ez_r=4, m_lz_r=4, m_cv_r=4, m_tap_r=12, m_rz_r=4, m_dl_r=4, m_dx_r=4)
        pe = [in_ps, sk_ps, d1_ps, d2_ps, bc_ps]
        act = [cin_r, x2_r, gt_r, d1_r, bc_r, az_r, ez_r, lz_r]
        pool = [dx_r]
        block = ctx.enter_context(nc.Block())

        def half(t, e, i):
            return t[:, e, bass.ds(i * HALF, HALF)]

        @block.sync
        def _(eng):
            bc_r.now(eng, 1, 0)
            eng.dma_start(keep.bc_dram, bc[:, :]).then_inc(bc_out, 16)
            eng.wait_ge(bc_out, 16)

        @block.gpsimd
        def _(eng):
            nm.sems.clear_stale(eng)
            for c in pool:
                c.credit(eng)
            eng.memset(cin[:, :, :, 0:KC - 1], 0.0).then_inc(padded, 1)
            nm.gpsimd(eng, 3)
            eng.wait_ge(sq_ready, NT)
            eng.tensor_scalar(ms[:, :], ss[:, :], 1.0 / D, EPS_LN, ALU.mult, ALU.add).then_inc(ms_ready, 1)
            eng.wait_ge(ms_ready, 1)
            eng.tensor_tensor(rms[:, :], ms[:, :], nm.mhalf[:, :], ALU.pow).then_inc(rms_ready, 1)
            with eng.Fori(0, 2) as i:
                for e in range(KE):
                    dl_r.now(eng, i, e)
                    eng.tensor_tensor(half(keep.dx, e, i), half(keep.delta, e, i), half(keep.x2, e, i),
                                      ALU.mult).then_inc(dx_r.sem, 1)
            dx_r.now(eng, 1, 3)
            eng.tensor_tensor(nm.X[:, :, :, :], nm.X[:, :, :, :], nm.XN[:, :, :, :], ALU.add).then_inc(keep.x_plus, 1)

        @block.tensor
        def _(eng):
            for c in pe:
                c.credit(eng)
            nm.tensor(eng, 3, IN, XR, xr_ready, TT)
            eng.wait_ge(nm.xnT_ready, 4 * B)
            for name in ("m_skip", "m_in", "m_d1", "m_d2", "m_bc"):
                eng.wait_ge(w[name][1], 16)
            with eng.Fori(0, 2) as i:
                for e in range(KE):
                    for bank, wt, out_c, used in ((IN[e % 2], w["m_in"][0], in_ps, cin_r), (SK[e % 2], w["m_skip"][0], sk_ps, gt_r)):
                        (used.now(eng, i, e - 2) if e >= 2 else used.before(eng, i, e + 2))
                        for k in range(KD):
                            mm = eng.matmul(bank[:, :], wt[:, k, e * P:(e + 1) * P], half(nm.xnT, k, i),
                                            start=(k == 0), stop=(k == KD - 1))
                        mm.then_inc(out_c.sem, 1)
                d1_r.before(eng, i, 0)
                for e in range(KE):
                    x2_r.now(eng, i, e)
                    mm = eng.matmul(D1[:, :], w["m_d1"][0][:, e, :], half(keep.x2, e, i), start=(e == 0), stop=(e == KE - 1))
                mm.then_inc(d1_ps.sem, 1)
                bc_r.before(eng, i, 0)
                for e in range(KE):
                    with fresh_addresses(nc):
                        mm = eng.matmul(BC[0:2 * NS, :], w["m_bc"][0][:, e, :], half(keep.x2, e, i), start=(e == 0),
                                        stop=(e == KE - 1))
                mm.then_inc(bc_ps.sem, 1)
                d1_r.now(eng, i, 0)
                for e in range(KE):
                    if e >= 2:
                        az_r.now(eng, i, e - 2)
                        rz_r.now(eng, i, e - 2)
                    else:
                        az_r.before(eng, i, e + 2)
                        rz_r.before(eng, i, e + 2)
                    eng.matmul(D2[e % 2][:, :], w["m_d2"][0][:, e * P:(e + 1) * P], d1[:, :], start=True,
                               stop=True).then_inc(d2_ps.sem, 1)

        @block.scalar
        def _(eng):
            for c in act:
                c.credit(eng)
            eng.wait_ge(w["m_small"][1], 16)
            for t in range(NT):
                eng.wait_ge(nm.xn_ready, 3 * NT + t + 1)
                if t:
                    eng.wait_ge(sq_ready, t)
                eng.activation(sq[:, :], nm.XN[:, t // TT, t % TT, :], ACT.Square,
                               accum_out=ss[:, t:t + 1]).then_inc(sq_ready, 1)
            eng.activation(keep.A[:, :], a_log, ACT.Exp).then_inc(a_ready, 1)
            nm.scalar(eng, 3, IN, norm_w)
            with eng.Fori(0, 2) as i:
                for e in range(KE):
                    in_ps.now(eng, i, e)
                    (cv_r.now(eng, i, e - 2) if e >= 2 else cv_r.before(eng, i, e + 2))
                    eng.activation(cin[:, e % 2, :, KC - 1:], IN[e % 2][:, :].rearrange("p (b t) -> p b t", b=2),
                                   ACT.Copy).then_inc(cin_r.sem, 1)
                    sk_ps.now(eng, i, e)
                    eng.activation(half(keep.gate, e, i), SK[e % 2][:, :], ACT.Silu).then_inc(gt_r.sem, 1)
                    if e:
                        cv_r.now(eng, i, e - 1)
                        eng.activation(half(keep.x2, e - 1, i), cv[:, (e - 1) % 2, :, :].rearrange("p b t -> p (b t)"),
                                       ACT.Silu, bias=conv_b[:, e - 1:e]).then_inc(x2_r.sem, 1)
                cv_r.now(eng, i, KE - 1)
                eng.activation(half(keep.x2, KE - 1, i), cv[:, (KE - 1) % 2, :, :].rearrange("p b t -> p (b t)"),
                               ACT.Silu, bias=conv_b[:, KE - 1:KE]).then_inc(x2_r.sem, 1)
                d1_ps.now(eng, i, 0)
                d2_ps.before(eng, i, 3)
                eng.activation(d1[:, :], D1[:, :], ACT.Copy).then_inc(d1_r.sem, 1)
                bc_ps.now(eng, i, 0)
                eng.activation(bc[:, bass.ds(i * HALF, HALF)], BC[0:2 * NS, :], ACT.Copy).then_inc(bc_r.sem, 1)
                for e in range(KE):
                    d2_ps.now(eng, i, e)
                    (ez_r.now(eng, i, e - 1) if e else ez_r.before(eng, i, 3))
                    eng.activation(az[:, :], D2[e % 2][:, :], ACT.Abs, bias=b_d2[:, e:e + 1]).then_inc(az_r.sem, 1)
                    az_r.now(eng, i, e)
                    (lz_r.now(eng, i, e - 1) if e else lz_r.before(eng, i, 3))
                    eng.activation(ez[:, :], az[:, :], ACT.Exp, scale=-1.0).then_inc(ez_r.sem, 1)
                    ez_r.now(eng, i, e)
                    (dl_r.now(eng, i, e - 1) if e else dl_r.before(eng, i, 3))
                    eng.activation(lz[:, :], ez[:, :], ACT.Ln, bias=1.0).then_inc(lz_r.sem, 1)

        @block.vector
        def _(eng):
            for c in cs:
                if c not in pe + act + pool:
                    c.credit(eng)
            nm.vector(eng, 3)
            eng.wait_ge(rms_ready, 1)
            for t in range(NT):
                eng.tensor_scalar(XR[:, t // TT, t % TT, :], nm.XN[:, t // TT, t % TT, :], rms[:, t:t + 1], None,
                                  ALU.mult).then_inc(xr_ready, 1)
            eng.wait_ge(padded, 1)
            eng.wait_ge(a_ready, 1)
            eng.tensor_scalar(keep.A[:, :], keep.A[:, :], -1.0, None, ALU.mult).then_inc(a_ready, 1)

            def delta(i, e):
                d2_ps.now(eng, i, e)
                az_r.now(eng, i, e)
                (dl_r.now(eng, i, e - 1) if e else dl_r.before(eng, i, 3))
                eng.tensor_scalar(keep.rz[:, :], D2[e % 2][:, :], b_d2[:, e:e + 1], 0.0, ALU.add, ALU.max).then_inc(rz_r.sem, 1)
                lz_r.now(eng, i, e)
                rz_r.now(eng, i, e)
                eng.tensor_tensor(half(keep.delta, e, i), keep.rz[:, :], lz[:, :], ALU.add).then_inc(dl_r.sem, 1)

            with eng.Fori(0, 2) as i:
                for e in range(KE):
                    cin_r.now(eng, i, e)
                    (x2_r.now(eng, i, e - 2) if e >= 2 else x2_r.before(eng, i, e + 2))
                    eng.tensor_scalar(cv[:, e % 2, :, :], cin[:, e % 2, :, 0:S], conv_w[:, e * KC:e * KC + 1], None,
                                      ALU.mult).then_inc(tap_r.sem, 1)
                    for q in range(1, KC):
                        tap_r.now(eng, i, 3 * e + q - 1)
                        eng.scalar_tensor_tensor(cv[:, e % 2, :, :], cin[:, e % 2, :, q:q + S],
                                                 conv_w[:, e * KC + q:e * KC + q + 1], cv[:, e % 2, :, :],
                                                 ALU.mult, ALU.add).then_inc((cv_r if q == KC - 1 else tap_r).sem, 1)
                for e in range(KE):
                    delta(i, e)


class Keep:

    def __init__(self, ctx, nc):
        sb, _ = buffers(ctx, nc)
        self.x2, self.gate = sb("m_x2T", [P, KE, T]), sb("m_gateT", [P, KE, T])
        self.delta, self.dx = sb("m_deltaT", [P, KE, T]), sb("m_dxT", [P, KE, T])
        self.A = sb("m_A", [P, KE * NS])
        self.rz = sb("m_relu_z", [P, HALF])
        self.x_plus = nc.alloc_semaphore("m_x_plus")
        self.bc_dram = nc.dram_tensor("bc_scratch", (2 * NS, T), F32, kind="Internal").ap()


def scan(nc, nm, w, dram, keep):
    with ExitStack() as ctx:
        sb, ps = buffers(ctx, nc)
        NH = NS // 2
        U = 2 * KE
        NB, ND = 4, 2
        Bb, Cb = sb("m_B", [P, 2, NH, S]), sb("m_C", [P, 2, NH, S])
        dec = sb("m_decay", [P, ND, NH, S])
        hb = sb("m_h", [P, NB, NH, S])
        y1, yT = sb("m_y1", [P, 2, S]), sb("m_yT", [P, KE, S])
        Y = ps("m_y_ps", 2)
        O = ps("m_out_ps")
        W_D = w["m_small"][0][:, KD + 2 * KE:KD + 3 * KE]
        zeroed = nm.sems.new("m_zeroed")
        b_in = [nm.sems.new(f"m_b_in{n}") for n in range(2)]
        c_in = [nm.sems.new(f"m_c_in{n}") for n in range(2)]
        (y_ps, o_ps, dec_r, u_r, h_r, p_r, y1_r, x_r, yT_r) = cs = counts(
            nm.sems, m_y_r=U, m_o_r=1, m_dec_r=U, m_u_r=U, m_h_r=U, m_p_r=U, m_y1_r=KE, m_xadd=1, m_yT_r=KE)
        pe, act, pool = [y_ps, o_ps], [dec_r], [u_r, yT_r]
        block = ctx.enter_context(nc.Block())

        @block.sync
        def _(eng):
            with eng.Fori(0, B) as i:
                for nh in range(2):
                    u_r.before(eng, i, KE * (nh + 1) - 1)
                    eng.dma_start(Bb[:, nh, :, :], keep.bc_dram[nh * NH:(nh + 1) * NH, bass.ds(i * S, S)][None, :, :]
                                  .to_broadcast((P, NH, S))).then_inc(b_in[nh], 16)
                    p_r.before(eng, i, KE * (nh + 1) - 1)
                    eng.dma_start(Cb[:, nh, :, :], keep.bc_dram[NS + nh * NH:NS + (nh + 1) * NH, bass.ds(i * S, S)][None, :, :]
                                  .to_broadcast((P, NH, S))).then_inc(c_in[nh], 16)

        @block.scalar
        def _(eng):
            for c in act:
                c.credit(eng)
            eng.wait_ge(zeroed, 1)
            with fresh_addresses(nc), eng.Fori(0, B) as i:
                for u in range(U):
                    nh, e = u // KE, u % KE
                    (h_r.now(eng, i, u - ND) if u >= ND else h_r.before(eng, i, U - ND + u))
                    for n in range(NH):
                        s = e * NS + nh * NH + n
                        a = eng.activation(dec[:, u % ND, n, 1:S], keep.delta[:, e, bass.ds(i * S + 1, S - 1)], ACT.Exp,
                                           scale=keep.A[:, s:s + 1])
                    a.then_inc(dec_r.sem, 1)

        @block.gpsimd
        def _(eng):
            nm.sems.clear_stale(eng)
            for c in pool:
                c.credit(eng)
            eng.memset(dec[:, :, :, 0:1], 0.0).then_inc(zeroed, 1)

            def gated(i, e):
                y1_r.now(eng, i, e)
                o_ps.before(eng, i, 0)
                eng.tensor_tensor(yT[:, e, :], y1[:, e % 2, :], keep.gate[:, e, bass.ds(i * S, S)], ALU.mult).then_inc(yT_r.sem, 1)

            with fresh_addresses(nc), eng.Fori(0, B) as i:
                for u in range(U):
                    nh, e = u // KE, u % KE
                    if e == 0:
                        eng.wait_ge(b_in[nh], 16 * i + 16)
                    (y_ps.now(eng, i, u - NB) if u >= NB else y_ps.before(eng, i, U - NB + u))
                    eng.tensor_tensor(hb[:, u % NB, :, :], Bb[:, nh, :, :],
                                      keep.dx[:, e, bass.ds(i * S, S)][:, None, :].to_broadcast((P, NH, S)),
                                      ALU.mult).then_inc(u_r.sem, 1)
                for e in range(KE):
                    gated(i, e)

        @block.vector
        def _(eng):
            for c in cs:
                if c not in pe + act + pool:
                    c.credit(eng)
            flat = lambda t: t.rearrange("p n t -> p (n t)")
            eng.wait_ge(keep.x_plus, 1)
            with eng.Fori(0, B) as i:
                for u in range(U):
                    nh, e = u // KE, u % KE
                    dec_r.now(eng, i, u)
                    u_r.now(eng, i, u)
                    eng.tensor_tensor_scan(flat(hb[:, u % NB, :, :]), flat(dec[:, u % ND, :, :]), flat(hb[:, u % NB, :, :]),
                                           0.0, ALU.mult, ALU.add).then_inc(h_r.sem, 1)
                    if e == 0:
                        eng.wait_ge(c_in[nh], 16 * i + 16)
                    h_r.now(eng, i, u)
                    eng.tensor_tensor(hb[:, u % NB, :, :], hb[:, u % NB, :, :], Cb[:, nh, :, :], ALU.mult).then_inc(p_r.sem, 1)
                for e in range(KE):
                    y_ps.now(eng, i, KE + e | 1)
                    (yT_r.now(eng, i, e - 2) if e >= 2 else yT_r.before(eng, i, e + 2))
                    eng.scalar_tensor_tensor(y1[:, e % 2, :], keep.x2[:, e, bass.ds(i * S, S)], W_D[:, e:e + 1],
                                             Y[:, e * S:(e + 1) * S], ALU.mult, ALU.add).then_inc(y1_r.sem, 1)
                o_ps.now(eng, i, 0)
                eng.tensor_tensor(nm.X[:, i, :, :], nm.X[:, i, :, :], O[:, :].rearrange("p (h f) -> p h f", h=TT),
                                  ALU.add).then_inc(x_r.sem, 1)

        @block.tensor
        def _(eng):
            for c in pe:
                c.credit(eng)
            eng.wait_ge(w["m_out"][1], 16)
            with eng.Fori(0, B) as i:
                for u in range(U):
                    nh, e = u // KE, u % KE
                    p_r.now(eng, i, u)
                    if u == 0:
                        y1_r.before(eng, i, KE - 1)
                    for n in range(NH):
                        mm = eng.matmul(Y[:, e * S:(e + 1) * S], nm.ident[:, :], hb[:, u % NB, n, :],
                                        start=(nh == 0 and n == 0 and e % 2 == 0), stop=(nh == 1 and n == NH - 1),
                                        skip_group_check=True)
                    mm.then_inc(y_ps.sem, 1)
                x_r.before(eng, i, 0)
                for h in range(TT):
                    for e in range(KE):
                        yT_r.now(eng, i, e)
                        mm = eng.matmul(O[:, h * D:(h + 1) * D], yT[:, e, h * P:(h + 1) * P], w["m_out"][0][:, e, :],
                                        start=(e == 0), stop=(e == KE - 1))
                mm.then_inc(o_ps.sem, 1)


def selective_scan(nc, nm, w, dram):
    with ExitStack() as ctx:
        keep = Keep(ctx, nc)
        scan_inputs(nc, nm, w, dram, keep)
        nm.sems.next_phase()
        scan(nc, nm, w, dram, keep)


def context_attention(nc, nm, w, dram):
    with ExitStack() as ctx:
        sb, ps = buffers(ctx, nc)
        qT, kT = sb("c_qT", [P, S]), sb("c_kT", [P, S])
        nmax, sums, rs = sb("c_neg_max", [P, TT]), sb("c_sums", [P, TT]), sb("c_rsums", [P, TT])
        E, AT = sb("c_probs", [P, TT, S]), sb("c_probsT", [P, KD, S])
        AN = sb("c_probs_norm", [P, TT, S])
        xcur = sb("c_x", [P, KD, S])
        QP, KP, EP, TP, OP = (ps(f"c_{n}") for n in ("q", "k", "energy", "turned", "out"))
        L0, L1 = ps("c_ln0"), ps("c_ln1")
        (q_ps, k_ps, e_ps, t_ps, o_ps, q_sb, k_sb, ex, at_sb, mx, rs_r, an_r, x_r, xc_r) = cs = counts(
            nm.sems, c_q_ps=1, c_k_ps=1, c_e_ps=1, c_t_ps=1, c_o_ps=1, c_q_sb=1, c_k_sb=1, c_ex=2, c_at=1, c_mx=1,
            c_rs=1, c_an=2, c_xadd=1, c_xc=1)
        pe, act, pool = [q_ps, k_ps, e_ps, t_ps, o_ps], [q_sb, k_sb, ex, at_sb], [xc_r]
        qk = w["x_qk"][0]
        block = ctx.enter_context(nc.Block())

        @block.gpsimd
        def _(eng):
            nm.sems.clear_stale(eng)
            for c in pool:
                c.credit(eng)
            nm.gpsimd(eng, 4)
            eng.wait_ge(nm.xnT_ready, 5 * B)
            with eng.Fori(0, B) as i:
                o_ps.before(eng, i, 0)
                eng.tensor_copy(xcur[:, :, :], nm.xnT[:, :, bass.ds(i * S, S)]).then_inc(xc_r.sem, 1)

        @block.tensor
        def _(eng):
            for c in pe:
                c.credit(eng)
            nm.tensor(eng, 4, (L0, L1))
            eng.wait_ge(w["ctxT"][1], 16)
            eng.wait_ge(w["x_qk"][1], 16)
            with eng.Fori(0, B) as i:
                q_sb.before(eng, i, 0)
                eng.matmul(QP[:, 0:S], qk[:, 0:P], w["ctxT"][0][:, i, :], start=True, stop=True).then_inc(q_ps.sem, 1)
                k_sb.before(eng, i, 0)
                eng.matmul(KP[:, 0:S], qk[:, P:2 * P], w["ctxT"][0][:, i, :], start=True, stop=True).then_inc(k_ps.sem, 1)
                q_sb.now(eng, i, 0)
                k_sb.now(eng, i, 0)
                ex.before(eng, i, 1)
                for h in range(TT):
                    mm = eng.matmul(EP[:, h * S:(h + 1) * S], qT[:, h * P:(h + 1) * P], kT[:, :], start=True, stop=True)
                mm.then_inc(e_ps.sem, 1)
                an_r.now(eng, i, 1)
                at_sb.before(eng, i, 0)
                for h in range(TT):
                    for k in range(KD):
                        mm = eng.transpose(TP[:, k * S + h * P:k * S + (h + 1) * P], AN[:, h, k * P:(k + 1) * P], nm.ident[:, :])
                mm.then_inc(t_ps.sem, 1)
                at_sb.now(eng, i, 0)
                xc_r.now(eng, i, 0)
                x_r.before(eng, i, 0)
                for h in range(TT):
                    for k in range(KD):
                        mm = eng.matmul(OP[:, h * S:(h + 1) * S], xcur[:, k, h * P:(h + 1) * P], AT[:, k, :],
                                        start=(k == 0), stop=(k == KD - 1))
                mm.then_inc(o_ps.sem, 1)

        @block.scalar
        def _(eng):
            for c in act:
                c.credit(eng)
            nm.scalar(eng, 4, (L0, L1))
            with eng.Fori(0, B) as i:
                e_ps.before(eng, i, 0)
                q_ps.now(eng, i, 0)
                eng.activation(qT[:, :], QP[:, 0:S], ACT.Identity, bias=qk[:, 2 * P:2 * P + 1]).then_inc(q_sb.sem, 1)
                k_ps.now(eng, i, 0)
                eng.activation(kT[:, :], KP[:, 0:S], ACT.Identity, bias=qk[:, 2 * P + 1:2 * P + 2]).then_inc(k_sb.sem, 1)
                mx.now(eng, i, 0)
                an_r.before(eng, i, 1)
                for h in range(TT):
                    eng.activation(E[:, h, :], EP[:, h * S:(h + 1) * S], ACT.Exp, bias=nmax[:, h:h + 1],
                                   accum_out=sums[:, h:h + 1]).then_inc(ex.sem, 1)
                t_ps.now(eng, i, 0)
                o_ps.before(eng, i, 0)
                eng.activation(AT[:, :, :], TP[:, :].rearrange("p (k t) -> p k t", k=KD), ACT.Copy).then_inc(at_sb.sem, 1)

        @block.vector
        def _(eng):
            for c in cs:
                if c not in pe + act + pool:
                    c.credit(eng)
            nm.vector(eng, 4)
            with eng.Fori(0, B) as i:
                e_ps.now(eng, i, 0)
                ex.before(eng, i, 1)
                eng.tensor_reduce(nmax[:, :], EP[:, :].rearrange("p (h t) -> p h t", h=TT), AX.X, ALU.max,
                                  negate=True).then_inc(mx.sem, 1)
                ex.now(eng, i, 1)
                an_r.before(eng, i, 1)
                eng.reciprocal(rs[:, :], sums[:, :]).then_inc(rs_r.sem, 1)
                rs_r.now(eng, i, 0)
                t_ps.before(eng, i, 0)
                for h in range(TT):
                    eng.tensor_scalar(AN[:, h, :], E[:, h, :], rs[:, h:h + 1], None, ALU.mult).then_inc(an_r.sem, 1)
                o_ps.now(eng, i, 0)
                eng.tensor_tensor(nm.X[:, i, :, :], nm.X[:, i, :, :], OP[:, :].rearrange("p (h f) -> p h f", h=TT),
                                  ALU.add).then_inc(x_r.sem, 1)


def experts(nc, nm, w, dram):
    with ExitStack() as ctx:
        sb, ps = buffers(ctx, nc)
        NT, NR, NW = B * TT, NX + 1, NX + 4
        nmax, tops = sb("e_neg_max", [P, NT]), sb("e_tops", [P, NT, 8])
        EV, REST = sb("e_exp", [P, NT, NW]), sb("e_rest", [P, NT, NW])
        tot, rtot = sb("e_total", [P, NT]), sb("e_rtotal", [P, NT])
        SH0, SH = sb("e_share0", [P, NT, NX]), sb("e_share", [P, NT, NR])
        SHT = sb("e_shareT", [NR, T])
        RING = 3
        W = sb("e_weights", [P, RING, 3 * KD * P])
        WH, WL = (sb(f"e_weights_{n}", [P, RING, 3 * KD * P], F32R) for n in ("high", "low"))
        XH, XL = (sb(f"e_x_{n}", [P, KD, T], F32R) for n in ("high", "low"))
        AH, AL = (sb(f"e_act_{n}", [P, 2, HALF], F32R) for n in ("high", "low"))
        CB = sb("e_share_rows", [P, RING, T])
        SG = sb("e_silu", [P, 2, HALF])
        GU = sb("e_gated", [P, 2, HALF])
        AC = sb("e_act", [P, 2, HALF])
        GP, UP = [ps(f"e_gate{n}") for n in range(2)], [ps(f"e_up{n}") for n in range(2)]
        OUT = [ps(f"e_out{n}") for n in range(4)]
        sem = lambda n: nm.sems.new(n)
        lg_r, nmx_r, ev_r, sg_r, top_r, cut_r, rest_r = (sem(f"e_{n}") for n in ("lg", "nmx", "ev", "sgm", "top", "cut", "rest"))
        sh0_r, tot_r, rtot_r, sh_r, sht_ps, sht_r, sht_out, done = (
            sem(f"e_{n}") for n in ("sh0", "tot", "rtot", "sh", "shtp", "sht", "shtout", "done"))
        w_in = [sem(f"e_w_in{n}") for n in range(RING)]
        c_in = [[sem(f"e_c_in{n}{a}") for a in range(2)] for n in range(RING)]
        (g_ps, u_ps, dn, si, gu_r, ac_r, wh_r, wl_r, ah_r, al_r) = cs = counts(
            nm.sems, e_g_ps=6, e_u_ps=6, e_dn=6, e_si=6, e_gu=6, e_ac=6, e_wh=3, e_wl=3, e_ah=6, e_al=6)
        pe, act, pool = [g_ps, u_ps, dn], [si, wh_r, ah_r], [ac_r]
        xh_r, xl_r = sem("e_xh"), sem("e_xl")
        share_dram = nc.dram_tensor("share_scratch", (NR, T), F32, kind="Internal").ap()
        HT = HALF // P
        PASSES = 1 + NX * FX // P // RING
        LAST = PASSES

        def passes(eng, body):
            body(0, RING, True, False)
            with eng.Fori(1, PASSES) as i:
                body(i, RING, False, False)
            body(LAST, 1, False, True)

        block = ctx.enter_context(nc.Block())

        def owners(i, r):
            if i is None:
                return [(a * P // 2, P // 2, NX) for a in range(2)]
            cut, e = FX - r * (P - FX), (RING + 1) * (i - 1) + r
            return [(0, cut, e), (cut, P - cut, e + 1)]

        @block.sync
        def _(eng):
            eng.wait_ge(sht_r, 2)
            eng.dma_start(share_dram, SHT[:, :]).then_inc(sht_out, 16)
            eng.wait_ge(sht_out, 16)

            def loads(i, slots, first, last):
                for r in range(slots):
                    if not first:
                        wl_r.before(eng, i, r)
                    eng.dma_start(W[:, r, :], dram["experts"][bass.ds(i * RING + r, 1)].rearrange("a p n -> (a p) n"))\
                       .then_inc(w_in[r], 16)
                    for a, (p, n, e) in enumerate(owners(None if first or last else i, r)):
                        if not first:
                            ac_r.before(eng, i, 2 * r + 1)
                        eng.dma_start(CB[p:p + n, r, :], share_dram[bass.ds(e, 1), :].to_broadcast((n, T)))\
                           .then_inc(c_in[r][a], 16)

            passes(eng, loads)

        @block.gpsimd
        def _(eng):
            nm.sems.clear_stale(eng)
            for c in pool:
                c.credit(eng)
            nm.gpsimd(eng, 5)
            eng.memset(EV[:, :, NX:NW], -1.0).then_inc(cut_r, 1)

            def share(i, slots, first, last):
                for r in range(slots):
                    eng.wait_ge(c_in[r][0], 16 * i + 16)
                    eng.wait_ge(c_in[r][1], 16 * i + 16)
                    for h in range(2):
                        u = 2 * r + h
                        gu_r.now(eng, i, u)
                        (al_r.now(eng, i, u - 2) if u >= 2 else al_r.before(eng, i, 4 + u))
                        eng.tensor_tensor(AC[:, h, :], GU[:, h, :], CB[:, r, h * HALF:(h + 1) * HALF], ALU.mult).then_inc(ac_r.sem, 1)

            passes(eng, share)

        @block.tensor
        def _(eng):
            for c in pe:
                c.credit(eng)
            nm.tensor(eng, 5, GP)
            eng.wait_ge(nm.xnT_ready, 6 * B)
            eng.wait_ge(w["router"][1], 16)
            for t in range(NT):
                for k in range(KD):
                    mm = eng.matmul(OUT[0][:, t * 64:t * 64 + NR], nm.xnT[:, k, t * P:(t + 1) * P], w["router"][0][:, k, :],
                                    start=(k == 0), stop=(k == KD - 1))
            mm.then_inc(lg_r, 1)
            eng.wait_ge(sh_r, 2)
            for t in range(NT):
                mm = eng.transpose(OUT[2 + t // 4][0:NR, (t % 4) * P:(t % 4 + 1) * P], SH[:, t, :], nm.ident[:, :])
            mm.then_inc(sht_ps, 1)
            eng.wait_ge(sht_r, 2)

            eng.wait_ge(xl_r, KD)

            def down(r, h, ready, start=False, stop=False):
                ready()
                at = slice(2 * KD * P, None)
                for t in range(HT):
                    n = h * HT + t
                    for s, (a, x) in enumerate(((AH, WH), (AH, WL), (AL, WH))):
                        mm = eng.matmul(OUT[n // 2][:, (n % 2) * D:(n % 2 + 1) * D], a[:, h, t * P:(t + 1) * P], x[:, r, at],
                                        start=(start and n % 2 == 0 and s == 0), stop=(stop and s == 2), skip_group_check=True)
                mm.then_inc(dn.sem, 1)

            def chunks(i, slots, first, last):
                for u in range(2 * slots):
                    r, h = u // 2, u % 2
                    if h == 0:
                        wl_r.now(eng, i, r)
                    if u >= 2:
                        si.now(eng, i, u - 2)
                        gu_r.now(eng, i, u - 2)
                    else:
                        si.before(eng, i, 4 + u)
                        gu_r.before(eng, i, 4 + u)
                    for bank, at, cnt in ((GP[h], 0, g_ps), (UP[h], KD * P, u_ps)):
                        parts = [(a, x, k) for k in range(KD) for a, x in ((WH, XH), (WH, XL), (WL, XH))]
                        for s, (a, x, k) in enumerate(parts):
                            mm = eng.matmul(bank[:, :], a[:, r, at + k * P:at + (k + 1) * P],
                                            x[:, k, h * HALF:(h + 1) * HALF], start=(s == 0), stop=(s == len(parts) - 1))
                        mm.then_inc(cnt.sem, 1)
                    if u >= 2:
                        down(r - 1, h, lambda: al_r.now(eng, i, u - 2), first and r == 1)
                    elif not first:
                        down(RING - 1, h, lambda: al_r.before(eng, i, 4 + u))

            passes(eng, chunks)
            for h in range(2):
                down(0, h, lambda: al_r.now(eng, LAST, h), stop=True)

        @block.scalar
        def _(eng):
            for c in act:
                c.credit(eng)
            nm.scalar(eng, 5, GP)
            for k in range(KD):
                eng.wait_ge(nm.xnT_ready, 6 * B)
                eng.activation(XH[:, k, :], nm.xnT[:, k, :], ACT.Copy).then_inc(xh_r, 1)
            eng.wait_ge(nmx_r, 1)
            eng.wait_ge(cut_r, 1)
            lg = OUT[0][:, :].rearrange("p (t c) -> p t c", c=64)
            for t in range(NT):
                eng.activation(EV[:, t, 0:NX], lg[:, t, 0:NX], ACT.Exp, bias=nmax[:, t:t + 1]).then_inc(ev_r, 1)
            eng.activation(SH[:, :, NX], lg[:, :, NX], ACT.Sigmoid).then_inc(sh_r, 1)
            for n in range(2):
                eng.wait_ge(sht_ps, 1)
                eng.activation(SHT[:, n * HALF:(n + 1) * HALF], OUT[2 + n][0:NR, :], ACT.Copy).then_inc(sht_r, 1)

            def high(i, u, ac, free):
                ac()
                free()
                eng.activation(AH[:, u % 2, :], AC[:, u % 2, :], ACT.Copy).then_inc(ah_r.sem, 1)

            def high_weights(i, r, first):
                if r == RING:
                    dn.now(eng, i, 1)
                elif not first:
                    dn.before(eng, i, 2 * r + 1)
                eng.wait_ge(w_in[r % RING], 16 * (i + r // RING) + 16)
                eng.activation(WH[:, r % RING, :], W[:, r % RING, :], ACT.Copy).then_inc(wh_r.sem, 1)

            high_weights(0, 0, True)

            def silus(i, slots, first, last):
                for u in range(2 * slots):
                    if u % 2 == 0 and not last:
                        high_weights(i, u // 2 + 1, first)
                    g_ps.now(eng, i, u)
                    (gu_r.now(eng, i, u - 2) if u >= 2 else gu_r.before(eng, i, 4 + u))
                    eng.activation(SG[:, u % 2, :], GP[u % 2][:, :], ACT.Silu).then_inc(si.sem, 1)
                    if u:
                        high(i, u - 1, lambda: ac_r.now(eng, i, u - 1),
                             lambda: dn.now(eng, i, u - 3) if u >= 3 else dn.before(eng, i, u + 3))
                    elif not first:
                        high(i, 5, lambda: ac_r.before(eng, i, 5), lambda: dn.before(eng, i, 3))

            passes(eng, silus)
            high(LAST, 1, lambda: ac_r.now(eng, LAST, 1), lambda: dn.before(eng, LAST, 5))

        @block.vector
        def _(eng):
            for c in cs:
                if c not in pe + act + pool:
                    c.credit(eng)
            nm.vector(eng, 5)
            for k in range(KD):
                eng.wait_ge(xh_r, k + 1)
                eng.tensor_tensor(XL[:, k, :], nm.xnT[:, k, :], XH[:, k, :].bitcast(F32), ALU.subtract).then_inc(xl_r, 1)
            eng.wait_ge(lg_r, 1)
            lg = OUT[0][:, :].rearrange("p (t c) -> p t c", c=64)
            eng.tensor_reduce(nmax[:, :], lg[:, :, 0:NX], AX.X, ALU.max, negate=True).then_inc(nmx_r, 1)
            for t in range(NT):
                eng.wait_ge(ev_r, t + 1)
                eng.max(tops[:, t, :], EV[:, t, 0:NX]).then_inc(top_r, 1)
            eng.wait_ge(top_r, NT)
            eng.memset(tops[:, :, 4:8], -1.0).then_inc(cut_r, 1)
            eng.wait_ge(cut_r, 2)
            for t in range(NT):
                eng.match_replace(REST[:, t, :], tops[:, t, :], EV[:, t, :], 0.0).then_inc(rest_r, 1)
            eng.wait_ge(rest_r, NT)
            eng.tensor_tensor(SH0[:, :, :], EV[:, :, 0:NX], REST[:, :, 0:NX], ALU.subtract).then_inc(sh0_r, 1)
            eng.wait_ge(sh0_r, 1)
            eng.tensor_reduce(tot[:, :], SH0[:, :, :], AX.X, ALU.add).then_inc(tot_r, 1)
            eng.wait_ge(tot_r, 1)
            eng.reciprocal(rtot[:, :], tot[:, :]).then_inc(rtot_r, 1)
            eng.wait_ge(rtot_r, 1)
            eng.tensor_tensor(SH[:, :, 0:NX], SH0[:, :, :], rtot[:, :, None].to_broadcast((P, NT, NX)), ALU.mult).then_inc(sh_r, 1)

            def low(i, u, ah, free):
                ah()
                free()
                eng.tensor_tensor(AL[:, u % 2, :], AC[:, u % 2, :], AH[:, u % 2, :].bitcast(F32), ALU.subtract)\
                   .then_inc(al_r.sem, 1)

            def low_weights(i, r, first):
                wh_r.now(eng, i, r)
                if r == RING:
                    dn.now(eng, i, 1)
                elif not first:
                    dn.before(eng, i, 2 * r + 1)
                eng.tensor_tensor(WL[:, r % RING, :], W[:, r % RING, :], WH[:, r % RING, :].bitcast(F32), ALU.subtract)\
                   .then_inc(wl_r.sem, 1)

            low_weights(0, 0, True)

            def gated(i, slots, first, last):
                for u in range(2 * slots):
                    if u % 2 == 0 and not last:
                        low_weights(i, u // 2 + 1, first)
                    si.now(eng, i, u)
                    u_ps.now(eng, i, u)
                    (ac_r.now(eng, i, u - 2) if u >= 2 else ac_r.before(eng, i, 4 + u))
                    eng.tensor_tensor(GU[:, u % 2, :], SG[:, u % 2, :], UP[u % 2][:, :], ALU.mult).then_inc(gu_r.sem, 1)
                    if u:
                        low(i, u - 1, lambda: ah_r.now(eng, i, u - 1),
                            lambda: dn.now(eng, i, u - 3) if u >= 3 else dn.before(eng, i, u + 3))
                    elif not first:
                        low(i, 5, lambda: ah_r.before(eng, i, 5), lambda: dn.before(eng, i, 3))

            passes(eng, gated)
            low(LAST, 1, lambda: ah_r.now(eng, LAST, 1), lambda: dn.before(eng, LAST, 5))
            dn.now(eng, LAST, 1)
            for b in range(B):
                eng.tensor_tensor(nm.X[:, b, :, :], nm.X[:, b, :, :], OUT[b][:, :].rearrange("p (h f) -> p h f", h=TT),
                                  ALU.add).then_inc(done, 1)
            eng.wait_ge(done, B)


def store(nc, nm, out):
    with ExitStack() as ctx:
        stored = nm.sems.new("stored")
        block = ctx.enter_context(nc.Block())

        @block.sync
        def _(eng):
            for b in range(B):
                eng.dma_start(out[b].rearrange("(h p) f -> p h f", p=P), nm.X[:, b, :, :]).then_inc(stored, 16)
            eng.wait_ge(stored, 16 * B)


def build(nc, dram, out, upto=99):
    with ExitStack() as ctx:
        nm = Norm(ctx, nc)
        late = weights(ctx, nc, LATE)
        with ExitStack() as first:
            w = weights(first, nc, EARLY) | late
            for phase in (attention, quantised, sparse)[:upto]:
                phase(nc, nm, w, dram)
                nm.sems.next_phase()
        for phase in PHASES[:max(upto - 3, 0)]:
            phase(nc, nm, late, dram)
            nm.sems.next_phase()
        store(nc, nm, out)


PHASES = (selective_scan, context_attention, experts)


def layout(i):
    c = np.ascontiguousarray

    def tiles(a):
        return c(a.reshape(-1, P, a.shape[-1]).transpose(1, 0, 2))

    def cols(a):
        return a.reshape(-1, P).T

    out = {
        "x": c(i["x"].reshape(B, TT, P, D).transpose(0, 2, 1, 3)),
        "wq": tiles(i["L0_attn_Wq"].T), "wk": tiles(i["L0_attn_Wk"].T),
        "wv": tiles(i["L0_attn_Wv"].T), "wo": tiles(i["L0_attn_Wo"].T),
        "fsT": c(i["fside_BxS2xS2_0"].transpose(0, 2, 1).reshape(B, KD, P, D).transpose(2, 0, 1, 3)),
        "ctxT": c(i["ctx_1024"].transpose(2, 0, 1)),
        "f_gate": tiles(i["L0_ffn_w_gate"].reshape(D, 2, P, 4).transpose(0, 1, 3, 2).reshape(D, FF)),
        "f_up": tiles(i["L0_ffn_w_up"].reshape(D, 2, P, 4).transpose(0, 1, 3, 2).reshape(D, FF)),
        "f_down": c(i["L0_ffn_w_down"].reshape(2, P, 4, D).transpose(1, 0, 2, 3).reshape(P, 8, D)),
        "m_small": c(np.concatenate([
            cols(i["L1_attn_norm_w"]), cols(i["L1_attn_conv_b"]), cols(i["L1_attn_b_d2"]), cols(i["L1_attn_W_D"]),
            np.zeros((P, KE), np.float32),
            i["L1_attn_conv_w"].reshape(KE, P, KC).transpose(1, 0, 2).reshape(P, KE * KC),
            i["L1_attn_A_log"].reshape(KE, P, NS).transpose(1, 0, 2).reshape(P, KE * NS)], axis=1)),
        "m_skip": tiles(i["L1_attn_W_skip"].T), "m_in": tiles(i["L1_attn_W_in"].T),
        "m_d1": tiles(i["L1_attn_W_d1"].T), "m_d2": c(i["L1_attn_W_d2"].T),
        "m_bc": tiles(np.concatenate([i["L1_attn_W_Bm"], i["L1_attn_W_Cm"]], axis=0).T),
        "m_out": tiles(i["L1_attn_W_out"].T),
        "x_qk": c(np.concatenate([i["L1_xattn_Wq"].T, i["L1_xattn_Wk"].T, i["L1_xattn_bq"][:, None],
                                  i["L1_xattn_bk"][:, None]], axis=1)),
        "router": tiles(np.concatenate([i["L1_ffn_router_weight"].T, i["L1_ffn_sgate_w"]], axis=1)),
    }

    def experts(w, shared):
        flat = np.concatenate([shared, w.transpose(1, 0, 2).reshape(D, NX * FX)], axis=1)
        return flat.reshape(KD, P, NCH, P).transpose(2, 1, 0, 3)

    gate = experts(i["L1_ffn_w_gate"], i["L1_ffn_sw_gate"])
    up = experts(i["L1_ffn_w_up"], i["L1_ffn_sw_up"])
    down = np.concatenate([i["L1_ffn_sw_down"], i["L1_ffn_w_down"].reshape(NX * FX, D)], axis=0).reshape(NCH, P, 1, D)
    order = [0, 1, 2, *range(SCH, NCH), SCH - 1]
    out["experts"] = c(np.concatenate([gate.reshape(NCH, P, 256), up.reshape(NCH, P, 256),
                                       down.reshape(NCH, P, 256)], axis=2)[order])
    return out


def kernel(**inputs):
    import concourse.bacc as bacc
    from concourse.bass_utils import run_bass_kernel_spmd as run

    arrays = layout({k: np.asarray(v) for k, v in inputs.items()})
    nc = bacc.Bacc("TRN2", target_bir_lowering=False, num_devices=1)
    dram = {n: nc.dram_tensor(f"in_{n}", a.shape, mybir.dt.from_np(a.dtype), kind="ExternalInput").ap()
            for n, a in arrays.items()}
    out = nc.dram_tensor("out_x", (B, S, D), F32, kind="ExternalOutput").ap()
    build(nc, dram, out)
    r = run(nc, [{f"in_{n}": a for n, a in arrays.items()}], core_ids=[0])
    return r.results[0]["out_x"]
```

```python
from contextlib import ExitStack, contextmanager

import numpy as np
import concourse.bass as bass
from concourse import mybir

F32 = mybir.dt.float32
BF16 = mybir.dt.bfloat16
F32R = mybir.dt.float32r
ALU = mybir.AluOpType
ACT = mybir.ActivationFunctionType
AX = mybir.AxisListType

P = 128
B, S, D = 4, 256, 256
TT = S // P
KD = D // P
T = B * S
HEADS, HD, HP = 16, 16, 32
HG = HEADS * HP // P
I0 = D // 2
FF = 1024
EI, NS, R, KC = 512, 16, 128, 4
KE = EI // P
NX, FX, FSH = 32, 96, 512
NCH = (NX * FX + FSH) // P
SCH = FSH // P
HALF = T // 2
EPS_LN = 1e-5
EPS_Q = 1e-6
QMAX = 127.0
MAGIC = 12582912.0
ROUNDS = 6


@contextmanager
def fresh_addresses(nc):
    nc.disable_value_cache = True
    yield
    nc.disable_value_cache = False


class Count:

    def __init__(self, sem, per):
        self.sem, self.per = sem, per

    def credit(self, eng, passes=1):
        eng.sem_inc(self.sem, passes * self.per)

    def now(self, eng, i, k):
        eng.wait_ge(self.sem, (i + 1) * self.per + k + 1)

    def before(self, eng, i, k):
        eng.wait_ge(self.sem, i * self.per + k + 1)

    def of(self, eng, b, k):
        eng.wait_ge(self.sem, b * self.per + k + 1)


def counts(sems, **per):
    return [Count(sems.new(name), n) for name, n in per.items()]


def buffers(ctx, nc):
    def sb(name, shape, dt=F32):
        return ctx.enter_context(nc.sbuf_tensor(name, shape, dt))

    def ps(name, banks=1):
        return ctx.enter_context(nc.psum_tensor(name, [P, 512 * banks], F32))

    return sb, ps


class Semaphores:

    def __init__(self, nc):
        self.nc, self.used, self.stale, self.cleared = nc, [], [], []

    def new(self, name):
        self.used.append(self.nc.alloc_semaphore(name))
        return self.used[-1]

    def clear_stale(self, eng):
        for sem in self.stale:
            eng.sem_clear(sem)
        self.cleared, self.stale = self.stale, []

    def next_phase(self):
        for sem in self.cleared:
            self.nc.release_semaphore(sem)
        self.cleared, self.stale, self.used = [], self.stale + self.used, []


class Norm:

    def __init__(self, ctx, nc):
        sb, _ = buffers(ctx, nc)
        self.sems = Semaphores(nc)
        self.X = sb("X", [P, B, TT, D])
        self.XN = sb("XN", [P, B, TT, D])
        self.xnT = sb("xnT", [P, KD, T])
        self.stats = sb("ln_stats", [P, B * TT, 6])
        self.mv = sb("ln_mean_var", [P, B * TT, 2])
        self.ve = sb("ln_var_eps", [P, B * TT])
        self.rstd = sb("ln_rstd", [P, B * TT])
        self.mhalf = sb("minus_half", [P, B * TT])
        self.half = sb("plus_half", [P, B * TT])
        self.magic = sb("magic", [P, 1])
        self.ident = sb("identity", [P, P])
        self.ones = sb("ones", [P, P])
        sem = lambda n: nc.alloc_semaphore(n)
        self.x_loaded = sem("x_loaded")
        self.consts = sem("consts")
        self.stats_ready = sem("ln_stats_ready")
        self.mv_ready = sem("ln_mv_ready")
        self.ve_ready = sem("ln_ve_ready")
        self.rstd_ready = sem("ln_rstd_ready")
        self.xn_ready = sem("ln_xn_ready")
        self.turned = sem("ln_turned")
        self.xnT_ready = sem("ln_xnT_ready")

    def vector(self, eng, r):
        n = B * TT
        if r == 0:
            eng.wait_ge(self.x_loaded, 16 * B)
        for t in range(n):
            eng.bn_stats(self.stats[:, t, :], self.X[:, t // TT, t % TT, :]).then_inc(self.stats_ready, 1)
        for t in range(n):
            eng.wait_ge(self.stats_ready, r * n + t + 1)
            eng.bn_aggr(self.mv[:, t, :], self.stats[:, t, :]).then_inc(self.mv_ready, 1)
        eng.wait_ge(self.rstd_ready, r + 1)
        for t in range(n):
            eng.tensor_scalar(self.XN[:, t // TT, t % TT, :], self.X[:, t // TT, t % TT, :],
                              self.mv[:, t, 0:1], self.rstd[:, t:t + 1],
                              ALU.subtract, ALU.mult).then_inc(self.xn_ready, 1)

    def gpsimd(self, eng, r):
        if r == 0:
            eng.wait_ge(self.consts, 6)
        eng.wait_ge(self.mv_ready, (r + 1) * B * TT)
        eng.tensor_scalar(self.ve[:, :], self.mv[:, :, 1], EPS_LN, None, ALU.add).then_inc(self.ve_ready, 1)
        eng.wait_ge(self.ve_ready, r + 1)
        eng.tensor_tensor(self.rstd[:, :], self.ve[:, :], self.mhalf[:, :], ALU.pow).then_inc(self.rstd_ready, 1)

    def tensor(self, eng, r, banks, src=None, ready=None, per=1):
        src = self.XN if src is None else src
        if r == 0:
            eng.wait_ge(self.consts, 6)
        for b in range(B):
            if ready is None:
                eng.wait_ge(self.xn_ready, r * B * TT + TT * (b + 1))
            else:
                eng.wait_ge(ready, per * (b + 1))
            if b >= 2:
                eng.wait_ge(self.xnT_ready, r * B + b - 1)
            for h in range(TT):
                for k in range(KD):
                    mm = eng.transpose(banks[b % 2][:, k * S + h * P:k * S + (h + 1) * P],
                                       src[:, b, h, k * P:(k + 1) * P], self.ident[:, :])
            mm.then_inc(self.turned, 1)

    def scalar(self, eng, r, banks, scale=None, after=None):
        for b in range(B):
            eng.wait_ge(self.turned, r * B + b + 1)
            if scale is None:
                mm = eng.activation(self.xnT[:, :, b * S:(b + 1) * S],
                                    banks[b % 2][:, :].rearrange("p (k t) -> p k t", k=KD), ACT.Copy)
            else:
                for k in range(KD):
                    mm = eng.activation(self.xnT[:, k, b * S:(b + 1) * S],
                                        banks[b % 2][:, k * S:(k + 1) * S], ACT.Copy, scale=scale[:, k:k + 1])
            mm.then_inc(self.xnT_ready, 1)
            if after is not None:
                after(eng, r, b)


def split_product(eng, out, terms, start=True, stop=True):
    parts = [(a, b) for sh, sl, mh, ml in terms for a, b in ((sh, mh), (sh, ml), (sl, mh))]
    for s, (a, b) in enumerate(parts):
        mm = eng.matmul(out, a, b, start=(start and s == 0), stop=(stop and s == len(parts) - 1), skip_group_check=True)
    return mm


class SplitX:

    def __init__(self, nm, sb, name):
        self.nm = nm
        self.high, self.low = (sb(f"{name}_x_{n}", [P, KD, T], F32R) for n in ("high", "low"))
        self.high_ready, self.low_ready = (nm.sems.new(f"{name}_x_{n}_ready") for n in ("high", "low"))

    def half(self, k, i):
        return tuple(x[:, k, i * HALF:(i + 1) * HALF] for x in (self.high, self.low))

    def scalar(self, eng, r, b):
        if b % 2:
            at = slice((b - 1) * S, (b + 1) * S)
            eng.wait_ge(self.nm.xnT_ready, r * B + b + 1)
            eng.activation(self.high[:, :, at], self.nm.xnT[:, :, at], ACT.Copy).then_inc(self.high_ready, 1)

    def vector(self, eng):
        for i in range(2):
            at = slice(i * HALF, (i + 1) * HALF)
            eng.wait_ge(self.high_ready, i + 1)
            eng.tensor_tensor(self.low[:, :, at], self.nm.xnT[:, :, at], self.high[:, :, at].bitcast(F32),
                              ALU.subtract).then_inc(self.low_ready, 1)


SPLIT = ("f_gate", "f_up", "f_down")


EARLY = (
    ("wq", [P, KD, D]), ("wk", [P, KD, D]), ("wv", [P, KD, D]), ("wo", [P, KD, D]), ("fsT", [P, B, KD, D]),
    ("f_gate", [P, KD, FF]), ("f_up", [P, KD, FF]), ("f_down", [P, FF // P, D]),
)
LATE = (
    ("ctxT", [P, B, S]), ("m_small", [P, KD + 8 * KE + KE * NS]),
    ("m_skip", [P, KD, EI]), ("m_in", [P, KD, EI]), ("m_d1", [P, KE, R]), ("m_d2", [P, EI]),
    ("m_bc", [P, KE, 2 * NS]), ("m_out", [P, KE, D]),
    ("x_qk", [P, 2 * P + 2]), ("router", [P, KD, NX + 1]),
)


def weights(ctx, nc, shapes):
    sb, _ = buffers(ctx, nc)
    return {n: (sb(n, shape), nc.alloc_semaphore(f"{n}_loaded")) for n, shape in shapes}


def load_weights(eng, w, dram):
    for name, (tile, sem) in w.items():
        eng.dma_start(tile[(slice(None),) * len(tile.shape)], dram[name]).then_inc(sem, 16)


def attention(nc, nm, w, split, dram):
    with ExitStack() as ctx:
        sb, ps = buffers(ctx, nc)
        masks = sb("a_part_masks", [P, 2])
        wide = {"wq": (split["f_gate_high"], split["f_gate_low"]), "wk": (split["f_up_high"], split["f_up_low"])}
        xcur = sb("a_x", [P, KD, S])
        x = SplitX(nm, sb, "a")
        PAIRS = HEADS // 2
        qS, kS = sb("a_q_parts", [P, PAIRS, S], F32R), sb("a_k_parts", [P, PAIRS, S], F32R)
        V1 = sb("a_v_ones", [P, TT, HEADS, HP])
        PR = sb("a_probs", [P, 2, 4, TT, S])
        PT = sb("a_probsT", [P, 2, TT, S])
        nmax = sb("a_neg_max", [P, HEADS, TT])
        aT = sb("a_outT", [P, S])
        rden = sb("a_rden", [P, TT, 4])
        aN = nm.XN[:, 0, :, :]
        xoT = sb("a_xoT", [P, KD, S])
        SC = [ps(f"a_scores{j}") for j in range(4)]
        PTp = [ps(f"a_probsT_ps{j}") for j in range(2)]
        M0, M1 = ps("a_m0"), ps("a_m1")
        xcur_ready = nm.sems.new("a_x_ready")
        masks_in, v_ones = nm.sems.new("a_masks_in"), nm.sems.new("a_v_ones")
        w_high, w_low = ({e: nm.sems.new(f"a_w_{n}_{e}") for e in ("pool", "dve")} for n in ("high", "low"))
        PROJ = 2 * HG
        (proj_ps, proj_high, proj_sb, v_sb, sc_ps, mx, mxs, ex) = counts(
            nm.sems, a_proj_ps=PROJ + 1, a_proj_high=PROJ, a_proj_sb=PROJ, a_v_sb=1, a_sc_ps=16, a_mx=16, a_mxs=16, a_ex=32)
        (pt_ps, pt_sb, pv_ps, aT_sb, at_ps, rd, nrm, xoT_ps, xoT_sb, o_ps, x_added) = counts(
            nm.sems, a_pt_ps=16, a_pt_sb=16, a_pv_ps=16, a_aT_sb=4, a_at_ps=4, a_rd=4, a_nrm=4, a_xoT_ps=1, a_xoT_sb=1,
            a_o_ps=1, a_x_added=1)
        block = ctx.enter_context(nc.Block())

        def widen(eng, name, e):
            eng.wait_ge(w[name][1], 16)
            high, low = wide[name]
            for k in range(KD):
                once = w[name][0][:, k, :].rearrange("p (h c) -> p h c", c=HD)[:, :, None, :].to_broadcast((P, HEADS, 4, HD))
                four = lambda tile: tile[:, k, :].rearrange("p (h r c) -> p h r c", r=4, c=HD)
                eng.tensor_copy(four(high), once).then_inc(w_high[e], 1)
                eng.wait_ge(w_high[e], k + 1)
                eng.tensor_tensor(four(low), once, four(high).bitcast(F32), ALU.subtract).then_inc(w_low[e], 1)

        def batches(eng, body):
            with eng.Fori(0, B - 1) as i:
                body(i, True)
            body(B - 1, False)

        @block.sync
        def _(eng):
            for b in range(B):
                eng.dma_start(nm.X[:, b, :, :], dram["x"][b]).then_inc(nm.x_loaded, 16)
            eng.dma_start(masks[:, :], dram["part_masks"]).then_inc(masks_in, 16)
            load_weights(eng, w, dram)

        @block.gpsimd
        def _(eng):
            nm.sems.clear_stale(eng)
            eng.memset(nm.mhalf[:, :], -0.5).then_inc(nm.consts, 1)
            eng.memset(nm.half[:, :], 0.5).then_inc(nm.consts, 1)
            eng.memset(nm.ones[:, :], 1.0).then_inc(nm.consts, 1)
            eng.memset(nm.magic[:, :], MAGIC).then_inc(nm.consts, 1)
            eng.memset(nm.ident[:, :], 0.0).then_inc(nm.consts, 1)
            eng.wait_ge(nm.consts, 5)
            eng.affine_select(out=nm.ident[:, :], in_=nm.ident[:, :], compare_op=ALU.not_equal, fill=1.0,
                              base=0, pattern=[[-1, P]], channel_multiplier=1).then_inc(nm.consts, 1)
            eng.memset(V1[:, :, :, :], 1.0).then_inc(v_ones, 1)
            nm.gpsimd(eng, 0)
            widen(eng, "wq", "pool")
            eng.wait_ge(nm.xnT_ready, B)
            with eng.Fori(0, B - 1) as i:
                proj_ps.of(eng, i, PROJ)
                eng.tensor_copy(xcur[:, :, :], nm.xnT[:, :, bass.ds((i + 1) * S, S)]).then_inc(xcur_ready, 1)

        @block.tensor
        def _(eng):
            for c in (pt_ps, pv_ps, at_ps, xoT_ps, o_ps):
                c.credit(eng)
            nm.tensor(eng, 0, PTp)

            def project(b, n, bank):
                g, name = n // 2, ("wq", "wk")[n % 2]
                for a in range(2):
                    at = slice((2 * g + a) * P, (2 * g + a + 1) * P)
                    mm = split_product(eng, bank[:, a * S:(a + 1) * S], [
                        (wide[name][0][:, k, at], wide[name][1][:, k, at],
                         x.high[:, k, bass.ds(b * S, S)], x.low[:, k, bass.ds(b * S, S)]) for k in range(KD)])
                mm.then_inc(proj_ps.sem, 1)

            def project_v(x_of_batch):
                for h in range(TT):
                    for k in range(KD):
                        mm = eng.matmul(M0[:, h * D:(h + 1) * D], x_of_batch[:, k, h * P:(h + 1) * P], w["wv"][0][:, k, :],
                                        start=(k == 0), stop=(k == KD - 1))
                mm.then_inc(proj_ps.sem, 1)

            def scores(g, j):
                rows, pair = slice(4 * HD * (j % 2), 4 * HD * (j % 2 + 1)), 2 * g + j // 2
                for h in range(TT):
                    mm = eng.matmul(SC[j][:, h * S:(h + 1) * S], qS[rows, pair, h * P:(h + 1) * P],
                                    kS[rows, pair, :], start=True, stop=True)
                mm.then_inc(sc_ps.sem, 1)

            def turn(i, g, j, more):
                u = 4 * g + j
                ex.of(eng, i, 8 * g + 2 * j + 1)
                if g < HG - 1:
                    proj_sb.of(eng, i, 2 * g + 3)
                    scores(g + 1, j)
                elif more:
                    proj_sb.of(eng, i + 1, 1)
                    scores(0, j)
                (pt_sb.now(eng, i, u - 2) if u >= 2 else pt_sb.before(eng, i, 14 + u))
                for c in range(TT):
                    for h in range(TT):
                        mm = eng.transpose(PTp[j % 2][:, c * S + h * P:c * S + (h + 1) * P],
                                           PR[:, g % 2, j, h, c * P:(c + 1) * P], nm.ident[:, :])
                mm.then_inc(pt_ps.sem, 1)

            def values(i, g, j):
                pt_sb.now(eng, i, 4 * g + j)
                if j == 0:
                    (nrm.now(eng, i, g - 1) if g else x_added.before(eng, i, 0))
                if g == 0 and j == 0:
                    v_sb.of(eng, i, 0)
                for c in range(TT):
                    mm = eng.matmul(M1[HP * j:HP * (j + 1), 0:S], V1[:, c, 4 * g + j, :], PT[:, j % 2, c, :],
                                    start=(c == 0), stop=(c == TT - 1))
                mm.then_inc(pv_ps.sem, 1)

            def turn_back(i, g):
                aT_sb.now(eng, i, g)
                for h in range(TT):
                    mm = eng.transpose(M1[:, h * P:(h + 1) * P], aT[:, h * P:(h + 1) * P], nm.ident[:, :])
                mm.then_inc(at_ps.sem, 1)

            banks = (M0, M1, *PTp)
            eng.wait_ge(x.low_ready, 1)
            eng.wait_ge(w_low["pool"], KD)
            eng.wait_ge(w_low["dve"], KD)
            for n in range(PROJ):
                if n >= len(banks):
                    proj_sb.of(eng, 0, n - len(banks))
                elif n == 2:
                    eng.wait_ge(nm.xnT_ready, B)
                project(0, n, banks[n % len(banks)])
                if n == 3:
                    proj_sb.of(eng, 0, 1)
                    for j in range(4):
                        scores(0, j)
            proj_sb.of(eng, 0, PROJ - len(banks))
            eng.wait_ge(w["wv"][1], 16)
            project_v(nm.xnT)
            proj_sb.of(eng, 0, PROJ - 1)
            eng.wait_ge(x.low_ready, 2)

            def batch(i, more):
                def next_projection(n):
                    if more:
                        (proj_sb.of(eng, i + 1, n - 1) if n else v_sb.of(eng, i, 0))
                        project(i + 1, n, M0)

                for g in range(HG):
                    turn(i, g, 0, more)
                    if g:
                        turn_back(i, g - 1)
                    turn(i, g, 1, more)
                    next_projection(2 * g)
                    values(i, g, 0)
                    turn(i, g, 2, more)
                    values(i, g, 1)
                    turn(i, g, 3, more)
                    values(i, g, 2)
                    next_projection(2 * g + 1)
                    values(i, g, 3)
                if more:
                    proj_sb.of(eng, i + 1, PROJ - 1)
                    eng.wait_ge(xcur_ready, i + 1)
                    project_v(xcur)
                turn_back(i, HG - 1)
                nrm.now(eng, i, HG - 1)
                for h in range(TT):
                    for k in range(KD):
                        mm = eng.transpose(M1[:, k * S + h * P:k * S + (h + 1) * P], aN[:, h, k * P:(k + 1) * P],
                                           nm.ident[:, :])
                mm.then_inc(xoT_ps.sem, 1)
                xoT_sb.now(eng, i, 0)
                for h in range(TT):
                    for k in range(KD):
                        mm = eng.matmul(M1[:, h * D:(h + 1) * D], xoT[:, k, h * P:(h + 1) * P], w["wo"][0][:, k, :],
                                        start=(k == 0), stop=(k == KD - 1))
                mm.then_inc(o_ps.sem, 1)

            eng.wait_ge(w["wo"][1], 16)
            batches(eng, batch)

        @block.vector
        def _(eng):
            for c in (pt_sb, rd, nrm, x_added):
                c.credit(eng)
            nm.vector(eng, 0)
            widen(eng, "wk", "dve")
            x.vector(eng)
            eng.wait_ge(masks_in, 16)

            def parts(b, n, bank):
                proj_high.of(eng, b, n)
                tile = (qS, kS)[n % 2][:, n // 2 * 2:n // 2 * 2 + 2, :]
                eng.scalar_tensor_tensor(tile, tile.bitcast(F32), masks[:, n % 2:n % 2 + 1],
                                         bank[:, :].rearrange("p (a t) -> p a t", a=2), ALU.mult, ALU.add).then_inc(proj_sb.sem, 1)

            def maxima(b, g, j):
                h4 = 4 * g + j
                sc_ps.of(eng, b, h4)
                eng.tensor_reduce(nmax[:, h4, :], SC[j][:, :].rearrange("p (h t) -> p h t", h=TT),
                                  AX.X, ALU.max, negate=True).then_inc(mx.sem, 1)
                mx.of(eng, b, h4)
                eng.tensor_scalar(nmax[:, h4, :], nmax[:, h4, :], HD ** -0.5, None, ALU.mult).then_inc(mxs.sem, 1)

            def keep_probsT(i, g, j):
                u = 4 * g + j
                pt_ps.now(eng, i, u)
                (pv_ps.now(eng, i, u - 2) if u >= 2 else pv_ps.before(eng, i, 14 + u))
                eng.tensor_copy(PT[:, j % 2, :, :], PTp[j % 2][:, :].rearrange("p (c t) -> p c t", c=TT)).then_inc(pt_sb.sem, 1)

            def normalise(i, g):
                at_ps.now(eng, i, g)
                view = M1[:, 0:TT * P].rearrange("p (h j c) -> p h j c", h=TT, j=4)
                (nrm.now(eng, i, g - 1) if g else nrm.before(eng, i, HG - 1))
                eng.reciprocal(rden[:, :, :], view[:, :, :, HD]).then_inc(rd.sem, 1)
                rd.now(eng, i, g)
                xoT_ps.before(eng, i, 0)
                for h in range(TT):
                    op = eng.tensor_tensor(
                        aN[:, h, g * 4 * HD:(g + 1) * 4 * HD].rearrange("p (j c) -> p j c", j=4),
                        view[:, h, :, 0:HD], rden[:, h, :, None].to_broadcast((P, 4, HD)), ALU.mult)
                op.then_inc(nrm.sem, 1)

            banks = (M0, M1, *PTp)
            for n in range(PROJ):
                parts(0, n, banks[n % len(banks)])
                if n == 3:
                    for j in range(4):
                        maxima(0, 0, j)

            def batch(i, more):
                for g in range(HG):
                    for j in range(4):
                        keep_probsT(i, g, j)
                        if g < HG - 1:
                            maxima(i, g + 1, j)
                        elif more:
                            maxima(i + 1, 0, j)
                        if j == 0 and g:
                            normalise(i, g - 1)
                        if j % 2 and more:
                            parts(i + 1, 2 * g + j // 2, M0)
                normalise(i, HG - 1)
                o_ps.now(eng, i, 0)
                eng.tensor_tensor(nm.X[:, i, :, :], nm.X[:, i, :, :],
                                  M1[:, :].rearrange("p (h f) -> p h f", h=TT), ALU.add).then_inc(x_added.sem, 1)

            batches(eng, batch)

        @block.scalar
        def _(eng):
            for c in (aT_sb, xoT_sb):
                c.credit(eng)
            nm.scalar(eng, 0, PTp, after=x.scalar)

            def high(b, n, bank, free):
                proj_ps.of(eng, b, n)
                free()
                eng.activation((qS, kS)[n % 2][:, n // 2 * 2:n // 2 * 2 + 2, :],
                               bank[:, :].rearrange("p (a t) -> p a t", a=2), ACT.Copy).then_inc(proj_high.sem, 1)

            def keep_v(b, free):
                proj_ps.of(eng, b, PROJ)
                free()
                eng.activation(V1[:, :, :, 0:HD], M0[:, :].rearrange("p (h n c) -> p h n c", h=TT, c=HD),
                               ACT.Copy).then_inc(v_sb.sem, 1)

            def exps(b, g, free):
                for j in range(4):
                    mxs.of(eng, b, 4 * g + j)
                    free(j)
                    for h in range(TT):
                        eng.activation(PR[:, g % 2, j, h, :], SC[j][:, h * S:(h + 1) * S], ACT.Exp,
                                       bias=nmax[:, 4 * g + j, h:h + 1], scale=HD ** -0.5).then_inc(ex.sem, 1)

            def keep_outT(i, g):
                pv_ps.now(eng, i, 4 * g + 3)
                (at_ps.now(eng, i, g - 1) if g else at_ps.before(eng, i, HG - 1))
                eng.activation(aT[:, :], M1[:, 0:S], ACT.Copy).then_inc(aT_sb.sem, 1)

            banks = (M0, M1, *PTp)
            for n in range(PROJ):
                high(0, n, banks[n % len(banks)], lambda: None)
                if n == 3:
                    exps(0, 0, lambda j: None)
            eng.wait_ge(v_ones, 1)
            keep_v(0, lambda: None)

            def batch(i, more):
                for g in range(HG):
                    used = lambda: sc_ps.of(eng, i, 4 * g + 3)
                    turned = lambda j: (pt_ps.now(eng, i, 4 * (g - 1) + j) if g else pt_ps.before(eng, i, 12 + j))
                    if more:
                        high(i + 1, 2 * g, M0, used)
                    if g < HG - 1:
                        exps(i, g + 1, turned)
                    elif more:
                        exps(i + 1, 0, turned)
                    if more:
                        high(i + 1, 2 * g + 1, M0, used)
                    keep_outT(i, g)
                if more:
                    keep_v(i + 1, lambda: pv_ps.now(eng, i, 15))
                xoT_ps.now(eng, i, 0)
                o_ps.before(eng, i, 0)
                eng.activation(xoT[:, :, :], M1[:, :].rearrange("p (k t) -> p k t", k=KD), ACT.Copy).then_inc(xoT_sb.sem, 1)

            batches(eng, batch)


def quantised(nc, nm, w, split, dram):
    with ExitStack() as ctx:
        sb, ps = buffers(ctx, nc)
        am = sb("q_amax", [P, 5])
        amf = sb("q_amax_floor", [P, 5])
        rw = sb("q_recip_w", [P, 3])
        ratio, root = sb("q_ratio", [P, 2]), sb("q_root", [P, 2])
        s1, rs1 = sb("q_s1", [P, 2]), sb("q_rs1", [P, 2])
        OP = sb("q_scaled", [P, 4, S])
        ra, sc, rsc = sb("q_row_amax", [P, 4]), sb("q_scale", [P, 4]), sb("q_rscale", [P, 4])
        Q1, Q2 = sb("q_shifted", [P, 4, S]), sb("q_clipped", [P, 4, S])
        QT = sb("q_turned", [P, 4, S], BF16)
        diag = sb("q_diag", [P, 2, P])
        XS = sb("q_x_scale_row", [P, S])
        gd, ud, sg, aa = (sb(f"q_{n}", [P, S]) for n in ("gate", "up", "silu", "act"))
        am2, amf2 = sb("q_amax2", [P, 1]), sb("q_amax2_floor", [P, 1])
        ratio2, root2 = sb("q_ratio2", [P, 1]), sb("q_root2", [P, 1])
        s2, rs2 = sb("q_s2", [P, 1]), sb("q_rs2", [P, 1])
        OP2 = sb("q_scaled2", [P, 2, S])
        ra2, sc2, rsc2 = sb("q_row_amax2", [P, 4]), sb("q_scale2", [P, 4]), sb("q_rscale2", [P, 4])
        Q3, Q4 = sb("q_shifted2", [P, 4, P]), sb("q_clipped2", [P, 4, P])
        QT2 = sb("q_turned2", [P, 4, P], BF16)
        diag2 = sb("q_diag2", [P, 2, P])
        WS = sb("q_w_scale_row", [P, S])
        yd = sb("q_y", [P, TT, D])
        TP = ps("q_tp", 2)
        TB = ps("q_tb", 2)
        GU = ps("q_gu")
        T2, B2 = ps("q_t2"), ps("q_b2")
        RW = ps("q_rows")
        (am_r, amf_r, rw_r, rt_r, root_r, s_r, rs_r, op_r, ra_r, sc_r, rsc_r, q2_r, dg_r, gd_r, ud_r, aa_r,
         am2_r, amf2_r, rt2_r, s2_r, rs2_r, op2_r, ra2_r, sc2_r, rsc2_r, q4_r, dg2_r, y_r, x_r,
         root2_r, tp_r, tb_r, xsr_r, gu_r, t2_r, b2_r, wsr_r, yy_r,
         q1_r, qt_r, xs_r, sg_r, q3_r, qt2_r, ws_r) = cs = counts(
            nm.sems, q_am=3, q_amf=1, q_rw=1, q_rt=1, q_root_r=1, q_s=1, q_rs=1, q_op=4, q_ra=2, q_sc=1, q_rsc=1,
            q_q2=1, q_dg=2, q_gd=1, q_ud=1, q_aa=1, q_am2=1, q_amf2=1, q_rt2=1, q_s2r=1, q_rs2r=1, q_op2=2,
            q_ra2=1, q_sc2=1, q_rsc2=1, q_q4=1, q_dg2=2, q_yr=2, q_xr=1, q_root2r=1, q_tp_r=2, q_tb_r=2, q_xsr=1,
            q_gu_r=2, q_t2r=1, q_b2r=1, q_wsr=1, q_yyr=1, q_q1=4, q_qt=2, q_xs=1, q_sgr=1, q_q3=4, q_qt2=1, q_wsr2=1)
        w_high = {name: nm.sems.new(f"q_{name}_high") for name in SPLIT}
        pool = [root_r, root2_r]
        pe = [tp_r, tb_r, xsr_r, gu_r, t2_r, b2_r, wsr_r, yy_r]
        act = [q1_r, qt_r, xs_r, sg_r, q3_r, qt2_r, ws_r]
        block = ctx.enter_context(nc.Block())

        @block.gpsimd
        def _(eng):
            nm.sems.clear_stale(eng)
            for c in pool:
                c.credit(eng)
            for name in SPLIT:
                eng.wait_ge(w[name][1], 16)
            nm.gpsimd(eng, 1)
            with fresh_addresses(nc), eng.Fori(0, B) as i:
                rt_r.now(eng, i, 0)
                eng.tensor_tensor(root[:, :], ratio[:, :], nm.half[:, 0:2], ALU.pow).then_inc(root_r.sem, 1)
                rt2_r.now(eng, i, 0)
                eng.tensor_tensor(root2[:, :], ratio2[:, :], nm.half[:, 0:1], ALU.pow).then_inc(root2_r.sem, 1)
                for name in SPLIT:
                    tiles = w[name][0], split[f"{name}_high"], split[f"{name}_low"]
                    if name == "f_down":
                        tile, high, low = (a[:, bass.ds(i * 2, 2), :] for a in tiles)
                    else:
                        tile, high, low = (a[:, :, bass.ds(i * D, D)] for a in tiles)
                    eng.tensor_copy(high, tile).then_inc(w_high[name], 1)
                    eng.wait_ge(w_high[name], i + 1)
                    eng.tensor_tensor(low, tile, high.bitcast(F32), ALU.subtract)

        @block.tensor
        def _(eng):
            for c in pe:
                c.credit(eng)
            nm.tensor(eng, 1, (GU, T2))
            eng.wait_ge(nm.xnT_ready, 2 * B)
            with eng.Fori(0, B) as i:
                for o in range(2):
                    op_r.now(eng, i, 2 * o + 1)
                    q1_r.before(eng, i, 2 * o + 1)
                    for r in range(2):
                        for k in range(KD):
                            mm = eng.transpose(TP[:, (2 * o + r) * D + k * P:(2 * o + r) * D + (k + 1) * P],
                                               OP[:, 2 * o + k, r * P:(r + 1) * P], nm.ident[:, :])
                    mm.then_inc(tp_r.sem, 1)
                dg_r.now(eng, i, 1)
                xs_r.before(eng, i, 0)
                ws_r.before(eng, i, 0)
                for r in range(2):
                    mm = eng.matmul(RW[:, r * P:(r + 1) * P], nm.ones[:, :], diag[:, r, :], start=True, stop=True)
                mm.then_inc(xsr_r.sem, 1)
                q2_r.now(eng, i, 0)
                for o in range(2):
                    qt_r.before(eng, i, o)
                    for r in range(2):
                        for k in range(KD):
                            mm = eng.transpose(TB[:, (2 * o + k) * S + r * P:(2 * o + k) * S + (r + 1) * P],
                                               Q2[:, 2 * o + r, k * P:(k + 1) * P], nm.ident[:, :])
                    mm.then_inc(tb_r.sem, 1)
                qt_r.now(eng, i, 1)
                ud_r.before(eng, i, 0)
                for o in range(2):
                    for k in range(KD):
                        mm = eng.matmul(GU[:, o * S:(o + 1) * S], QT[:, 2 + k, o * P:(o + 1) * P], QT[:, k, :],
                                        start=(k == 0), stop=(k == KD - 1))
                    mm.then_inc(gu_r.sem, 1)
                op2_r.now(eng, i, 1)
                q3_r.before(eng, i, 3)
                for o in range(2):
                    for r in range(2):
                        mm = eng.transpose(T2[:, (2 * o + r) * P:(2 * o + r + 1) * P], OP2[:, o, r * P:(r + 1) * P],
                                           nm.ident[:, :])
                mm.then_inc(t2_r.sem, 1)
                dg2_r.now(eng, i, 1)
                ws_r.before(eng, i, 0)
                xs_r.now(eng, i, 0)
                for r in range(2):
                    mm = eng.matmul(RW[:, S + r * P:S + (r + 1) * P], nm.ones[:, :], diag2[:, r, :], start=True, stop=True)
                mm.then_inc(wsr_r.sem, 1)
                q4_r.now(eng, i, 0)
                qt2_r.before(eng, i, 0)
                for r in range(4):
                    mm = eng.transpose(B2[:, r * P:(r + 1) * P], Q4[:, r, :], nm.ident[:, :])
                mm.then_inc(b2_r.sem, 1)
                qt2_r.now(eng, i, 0)
                ud_r.now(eng, i, 0)
                y_r.before(eng, i, 1)
                for h in range(TT):
                    mm = eng.matmul(GU[:, h * D:(h + 1) * D], QT2[:, h, :], QT2[:, 2:4, :], start=True, stop=True)
                mm.then_inc(yy_r.sem, 1)

        @block.scalar
        def _(eng):
            for c in act:
                c.credit(eng)
            nm.scalar(eng, 1, (GU, T2))
            with eng.Fori(0, B) as i:
                rsc_r.now(eng, i, 0)
                for r in range(4):
                    q2_r.before(eng, i, 0)
                    tp_r.now(eng, i, r // 2)
                    eng.activation(Q1[:, r, :], TP[:, r * D:(r + 1) * D], ACT.Identity, bias=nm.magic[:, 0:1],
                                   scale=rsc[:, r:r + 1]).then_inc(q1_r.sem, 1)
                xsr_r.now(eng, i, 0)
                ud_r.before(eng, i, 0)
                eng.activation(XS[:, :], RW[:, 0:S], ACT.Copy).then_inc(xs_r.sem, 1)
                for o in range(2):
                    tb_r.now(eng, i, o)
                    gu_r.before(eng, i, 1)
                    eng.activation(QT[:, 2 * o:2 * o + 2, :], TB[:, 2 * o * S:(2 * o + 2) * S].rearrange("p (k t) -> p k t", k=2),
                                   ACT.Copy, bias=-MAGIC).then_inc(qt_r.sem, 1)
                gd_r.now(eng, i, 0)
                aa_r.before(eng, i, 0)
                eng.activation(sg[:, :], gd[:, :], ACT.Silu).then_inc(sg_r.sem, 1)
                rsc2_r.now(eng, i, 0)
                t2_r.now(eng, i, 0)
                q4_r.before(eng, i, 0)
                for r in range(4):
                    eng.activation(Q3[:, r, :], T2[:, r * P:(r + 1) * P], ACT.Identity, bias=nm.magic[:, 0:1],
                                   scale=rsc2[:, r:r + 1]).then_inc(q3_r.sem, 1)
                wsr_r.now(eng, i, 0)
                y_r.before(eng, i, 1)
                eng.activation(WS[:, :], RW[:, S:2 * S], ACT.Copy).then_inc(ws_r.sem, 1)
                b2_r.now(eng, i, 0)
                yy_r.before(eng, i, 0)
                eng.activation(QT2[:, :, :], B2[:, :].rearrange("p (r t) -> p r t", r=4), ACT.Copy,
                               bias=-MAGIC).then_inc(qt2_r.sem, 1)

        @block.vector
        def _(eng):
            for c in cs:
                if c not in pool + pe + act:
                    c.credit(eng)
            nm.vector(eng, 1)
            eng.wait_ge(nm.xnT_ready, 2 * B)
            eng.wait_ge(w["fsT"][1], 16)
            eng.wait_ge(w["ctxT"][1], 16)
            fsT, ctxT = w["fsT"][0], w["ctxT"][0]
            with eng.Fori(0, B) as i:
                xb = nm.xnT[:, :, bass.ds(i * S, S)]
                amf_r.before(eng, i, 0)
                eng.tensor_reduce(am[:, 0:2], xb, AX.X, ALU.max, apply_absolute_value=True).then_inc(am_r.sem, 1)
                eng.tensor_reduce(am[:, 2:4], fsT[:, i, :, :], AX.X, ALU.max, apply_absolute_value=True).then_inc(am_r.sem, 1)
                eng.tensor_reduce(am[:, 4:5], ctxT[:, i, :], AX.X, ALU.max, apply_absolute_value=True).then_inc(am_r.sem, 1)
                am_r.now(eng, i, 2)
                rt2_r.before(eng, i, 0)
                eng.tensor_scalar(amf[:, :], am[:, :], EPS_Q, None, ALU.max).then_inc(amf_r.sem, 1)
                amf_r.now(eng, i, 0)
                eng.reciprocal(rw[:, :], amf[:, 2:5]).then_inc(rw_r.sem, 1)
                rw_r.now(eng, i, 0)
                root_r.before(eng, i, 0)
                eng.tensor_tensor(ratio[:, :], amf[:, 0:2], rw[:, 0:2], ALU.mult).then_inc(rt_r.sem, 1)
                root_r.now(eng, i, 0)
                op_r.before(eng, i, 3)
                eng.tensor_scalar(s1[:, :], root[:, :], EPS_Q, None, ALU.max).then_inc(s_r.sem, 1)
                s_r.now(eng, i, 0)
                eng.reciprocal(rs1[:, :], s1[:, :]).then_inc(rs_r.sem, 1)
                rs_r.now(eng, i, 0)
                tp_r.before(eng, i, 1)
                for k in range(KD):
                    eng.tensor_scalar(OP[:, k, :], nm.xnT[:, k, bass.ds(i * S, S)], rs1[:, k:k + 1], None,
                                      ALU.mult).then_inc(op_r.sem, 1)
                for k in range(KD):
                    eng.tensor_scalar(OP[:, 2 + k, :], fsT[:, i, k, :], s1[:, k:k + 1], None, ALU.mult).then_inc(op_r.sem, 1)
                for o in range(2):
                    tp_r.now(eng, i, o)
                    sc_r.before(eng, i, 0)
                    eng.tensor_reduce(ra[:, 2 * o:2 * o + 2], TP[:, 2 * o * D:(2 * o + 2) * D].rearrange("p (r f) -> p r f", r=2),
                                      AX.X, ALU.max, apply_absolute_value=True).then_inc(ra_r.sem, 1)
                ra_r.now(eng, i, 1)
                dg_r.before(eng, i, 1)
                ud_r.before(eng, i, 0)
                eng.tensor_scalar(sc[:, :], ra[:, :], EPS_Q, 1.0 / QMAX, ALU.max, ALU.mult).then_inc(sc_r.sem, 1)
                sc_r.now(eng, i, 0)
                q1_r.before(eng, i, 3)
                eng.reciprocal(rsc[:, :], sc[:, :]).then_inc(rsc_r.sem, 1)
                xsr_r.before(eng, i, 0)
                for r in range(2):
                    eng.tensor_scalar(diag[:, r, :], nm.ident[:, :], sc[:, r:r + 1], None, ALU.mult).then_inc(dg_r.sem, 1)
                q1_r.now(eng, i, 3)
                tb_r.before(eng, i, 1)
                eng.tensor_scalar(Q2[:, :, :], Q1[:, :, :], MAGIC + QMAX, MAGIC - QMAX, ALU.min, ALU.max).then_inc(q2_r.sem, 1)
                xs_r.now(eng, i, 0)
                gu_r.now(eng, i, 1)
                sg_r.before(eng, i, 0)
                eng.scalar_tensor_tensor(gd[:, :], GU[:, 0:S], sc[:, 2:3], XS[:, :], ALU.mult, ALU.mult).then_inc(gd_r.sem, 1)
                aa_r.before(eng, i, 0)
                eng.scalar_tensor_tensor(ud[:, :], GU[:, S:2 * S], sc[:, 3:4], XS[:, :], ALU.mult, ALU.mult).then_inc(ud_r.sem, 1)
                sg_r.now(eng, i, 0)
                ud_r.now(eng, i, 0)
                op2_r.before(eng, i, 1)
                am2_r.before(eng, i, 0)
                eng.tensor_tensor(aa[:, :], sg[:, :], ud[:, :], ALU.mult).then_inc(aa_r.sem, 1)
                aa_r.now(eng, i, 0)
                amf2_r.before(eng, i, 0)
                eng.tensor_reduce(am2[:, :], aa[:, :], AX.X, ALU.max, apply_absolute_value=True).then_inc(am2_r.sem, 1)
                am2_r.now(eng, i, 0)
                eng.tensor_scalar(amf2[:, :], am2[:, :], EPS_Q, None, ALU.max).then_inc(amf2_r.sem, 1)
                amf2_r.now(eng, i, 0)
                root2_r.before(eng, i, 0)
                eng.tensor_tensor(ratio2[:, :], amf2[:, :], rw[:, 2:3], ALU.mult).then_inc(rt2_r.sem, 1)
                root2_r.now(eng, i, 0)
                op2_r.before(eng, i, 1)
                eng.tensor_scalar(s2[:, :], root2[:, :], EPS_Q, None, ALU.max).then_inc(s2_r.sem, 1)
                s2_r.now(eng, i, 0)
                eng.reciprocal(rs2[:, :], s2[:, :]).then_inc(rs2_r.sem, 1)
                rs2_r.now(eng, i, 0)
                t2_r.before(eng, i, 0)
                eng.tensor_scalar(OP2[:, 0, :], aa[:, :], rs2[:, 0:1], None, ALU.mult).then_inc(op2_r.sem, 1)
                eng.tensor_scalar(OP2[:, 1, :], ctxT[:, i, :], s2[:, 0:1], None, ALU.mult).then_inc(op2_r.sem, 1)
                t2_r.now(eng, i, 0)
                sc2_r.before(eng, i, 0)
                eng.tensor_reduce(ra2[:, :], T2[:, :].rearrange("p (r f) -> p r f", r=4), AX.X, ALU.max,
                                  apply_absolute_value=True).then_inc(ra2_r.sem, 1)
                ra2_r.now(eng, i, 0)
                y_r.before(eng, i, 1)
                eng.tensor_scalar(sc2[:, :], ra2[:, :], EPS_Q, 1.0 / QMAX, ALU.max, ALU.mult).then_inc(sc2_r.sem, 1)
                sc2_r.now(eng, i, 0)
                q3_r.before(eng, i, 3)
                eng.reciprocal(rsc2[:, :], sc2[:, :]).then_inc(rsc2_r.sem, 1)
                wsr_r.before(eng, i, 0)
                for r in range(2):
                    eng.tensor_scalar(diag2[:, r, :], nm.ident[:, :], sc2[:, 2 + r:3 + r], None, ALU.mult).then_inc(dg2_r.sem, 1)
                q3_r.now(eng, i, 3)
                b2_r.before(eng, i, 0)
                eng.tensor_scalar(Q4[:, :, :], Q3[:, :, :], MAGIC + QMAX, MAGIC - QMAX, ALU.min, ALU.max).then_inc(q4_r.sem, 1)
                yy_r.now(eng, i, 0)
                ws_r.now(eng, i, 0)
                x_r.before(eng, i, 0)
                for h in range(TT):
                    eng.scalar_tensor_tensor(yd[:, h, :], GU[:, h * D:(h + 1) * D], sc2[:, h:h + 1], WS[:, :],
                                             ALU.mult, ALU.mult).then_inc(y_r.sem, 1)
                y_r.now(eng, i, 1)
                eng.tensor_tensor(nm.X[:, i, :, :], nm.X[:, i, :, :], yd[:, :, :], ALU.add).then_inc(x_r.sem, 1)


def sparse(nc, nm, w, dram):
    with ExitStack() as ctx:
        sb, ps = buffers(ctx, nc)
        H, A = sb("s_h", [P, 4, HALF]), sb("s_abs", [P, 4, HALF])
        SG = sb("s_silu", [P, 2, HALF])
        C = sb("s_wins", [P, 6, HALF], BF16)
        W1 = sb("s_sums1", [P, 4, HALF], BF16)
        W2 = sb("s_sums2", [P, 4, HALF], BF16)
        HS = sb("s_kept", [P, 4, HALF])
        HH, HL = (sb(f"s_kept_{n}", [P, 2, 4, HALF], F32R) for n in ("high", "low"))
        x = SplitX(nm, sb, "s")
        NB = 3
        GP, UP = [ps(f"s_gate{n}") for n in range(NB)], [ps(f"s_up{n}") for n in range(NB)]
        OUT = [ps(f"s_out{n}") for n in range(2)]
        NT, STEPS = HALF // P, 4
        g_ps, u_ps, sg_r, ab_r, h_r, c_r, w1_r, w2_r, hs_r, hh_r, hl_r, o_ps, x_added = (
            nm.sems.new(f"s_{n}") for n in ("gate_ps", "up_ps", "silu_r", "abs_r", "h_r", "wins_r", "sums1_r", "sums2_r",
                                            "kept_r", "high_r", "low_r", "down", "x_added"))
        block = ctx.enter_context(nc.Block())

        @block.gpsimd
        def _(eng):
            nm.sems.clear_stale(eng)
            nm.gpsimd(eng, 2)

        @block.tensor
        def _(eng):
            nm.tensor(eng, 2, OUT)

            def gates(q, j):
                u, at = 4 * q + j, (4 * (q % 2) + j) * P
                if u >= NB:
                    eng.wait_ge(sg_r, u - NB + 1)
                    eng.wait_ge(h_r, u - NB + 1)
                for bank, name, c in ((GP[u % NB], "f_gate", g_ps), (UP[u % NB], "f_up", u_ps)):
                    split_product(eng, bank[:, :], [
                        (w[name + "_high"][:, k, at:at + P], w[name + "_low"][:, k, at:at + P],
                         *x.half(k, q // 2)) for k in range(KD)]).then_inc(c, 1)

            def downs(q):
                for j in range(4):
                    eng.wait_ge(hl_r, 4 * q + j + 1)
                    if q == 0 and j == 0:
                        eng.wait_ge(nm.xnT_ready, 3 * B)
                    if q == 2 and j == 0:
                        eng.wait_ge(x_added, 2)
                    n = 4 * (q % 2) + j
                    for t in range(NT):
                        rows = slice(t * P, (t + 1) * P)
                        mm = split_product(eng, OUT[t // 2][:, (t % 2) * D:(t % 2 + 1) * D], [
                            (HH[:, q % 2, j, rows], HL[:, q % 2, j, rows], w["f_down_high"][:, n, :], w["f_down_low"][:, n, :])],
                            start=(n == 0 and t % 2 == 0), stop=(n == 7))
                mm.then_inc(o_ps, 1)

            for q in range(STEPS):
                eng.wait_ge(x.low_ready, q // 2 + 1)
                for j in range(4):
                    gates(q, j)
                if q:
                    downs(q - 1)
            downs(STEPS - 1)

        @block.scalar
        def _(eng):
            nm.scalar(eng, 2, OUT, after=x.scalar)

            def highs(q):
                for j in range(4):
                    eng.wait_ge(hs_r, 4 * q + j + 1)
                    if q >= 2:
                        eng.wait_ge(o_ps, q - 1)
                    eng.activation(HH[:, q % 2, j, :], HS[:, j, :], ACT.Copy).then_inc(hh_r, 1)

            for q in range(STEPS):
                for j in range(4):
                    u = 4 * q + j
                    eng.wait_ge(g_ps, u + 1)
                    if u >= 2:
                        eng.wait_ge(h_r, u - 1)
                    eng.activation(SG[:, u % 2, :], GP[u % NB][:, :], ACT.Silu).then_inc(sg_r, 1)
                    if q and j == 0:
                        highs(q - 1)
                    eng.wait_ge(h_r, u + 1)
                    if q:
                        eng.wait_ge(c_r, 6 * q)
                    eng.activation(A[:, j, :], H[:, j, :], ACT.Abs).then_inc(ab_r, 1)
            highs(STEPS - 1)

        @block.vector
        def _(eng):
            nm.vector(eng, 2)
            x.vector(eng)

            def lows(q, js):
                for j in js:
                    eng.wait_ge(hh_r, 4 * q + j + 1)
                    if q >= 2:
                        eng.wait_ge(o_ps, q - 1)
                    eng.tensor_tensor(HL[:, q % 2, j, :], HS[:, j, :], HH[:, q % 2, j, :].bitcast(F32),
                                      ALU.subtract).then_inc(hl_r, 1)

            def wins(q, a, b, n):
                eng.wait_ge(ab_r, 4 * q + b + 1)
                if q:
                    eng.wait_ge(w2_r, 4 * q)
                eng.tensor_tensor(C[:, n, :], A[:, a, :], A[:, b, :], ALU.is_ge).then_inc(c_r, 1)

            def add(i):
                eng.wait_ge(o_ps, 2 * i + 2)
                for n in range(2):
                    b = 2 * i + n
                    eng.tensor_tensor(nm.X[:, b, :, :], nm.X[:, b, :, :], OUT[n][:, :].rearrange("p (h f) -> p h f", h=TT),
                                      ALU.add).then_inc(x_added, 1)

            for q in range(STEPS):
                for j in range(4):
                    u = 4 * q + j
                    eng.wait_ge(sg_r, u + 1)
                    eng.wait_ge(u_ps, u + 1)
                    if q:
                        eng.wait_ge(hs_r, u - 3)
                    eng.tensor_tensor(H[:, j, :], SG[:, u % 2, :], UP[u % NB][:, :], ALU.mult).then_inc(h_r, 1)
                    if q and j < 2:
                        lows(q - 1, (2 * j, 2 * j + 1))
                    if q == 3 and j == 1:
                        add(0)
                    for a, n in ((), ((0, 0),), ((1, 5), (0, 2)), ((2, 1), (1, 3), (0, 4)))[j]:
                        wins(q, a, j, n)
                eng.wait_ge(c_r, 6 * q + 6)
                for j, (a, b) in enumerate(((0, 2), (5, 3), (2, 5), (4, 3))):
                    eng.tensor_tensor(W1[:, j, :], C[:, a, :], C[:, b, :], ALU.add).then_inc(w1_r, 1)
                for j, (a, b, op) in enumerate(((W1[:, 0, :], C[:, 4, :], ALU.add), (W1[:, 1, :], C[:, 0, :], ALU.subtract),
                                                (C[:, 1, :], W1[:, 2, :], ALU.subtract), (W1[:, 3, :], C[:, 1, :], ALU.add))):
                    eng.wait_ge(w1_r, 4 * q + j + 1)
                    eng.tensor_tensor(W2[:, j, :], a, b, op).then_inc(w2_r, 1)
                for j, (least, op) in enumerate(((2.0, ALU.is_ge), (1.0, ALU.is_ge), (0.0, ALU.is_ge), (1.0, ALU.is_le))):
                    eng.wait_ge(w2_r, 4 * q + j + 1)
                    if q:
                        eng.wait_ge(hl_r, 4 * q)
                    eng.scalar_tensor_tensor(HS[:, j, :], W2[:, j, :], least, H[:, j, :], op, ALU.mult).then_inc(hs_r, 1)
            lows(STEPS - 1, range(4))
            add(1)


def scan_inputs(nc, nm, w, dram, keep):
    with ExitStack() as ctx:
        sb, ps = buffers(ctx, nc)
        NT = B * TT
        sq = sb("m_square", [P, D])
        ss, ms, rms = sb("m_sum_sq", [P, NT]), sb("m_mean_sq", [P, NT]), sb("m_rms", [P, NT])
        XR = sb("m_xr", [P, B, TT, D])
        cin = sb("m_conv_in", [P, 2, 2, S + KC - 1])
        cv = sb("m_conv", [P, 2, 2, S])
        d1 = sb("m_d1T", [P, HALF])
        az, ez, lz = sb("m_abs_z", [P, HALF]), sb("m_exp_z", [P, KE, HALF]), sb("m_ln_z", [P, 2, HALF])
        bc = sb("m_bcT", [2 * NS, T])
        small = w["m_small"][0]
        norm_w, conv_b, b_d2 = small[:, 0:KD], small[:, KD:KD + KE], small[:, KD + KE:KD + 2 * KE]
        conv_w = small[:, KD + 4 * KE:KD + 4 * KE + KE * KC]
        a_log = small[:, KD + 4 * KE + KE * KC:]
        IN, SK = [ps(f"m_in{n}") for n in range(2)], [ps(f"m_skip{n}") for n in range(2)]
        D2 = [ps(f"m_d2_{n}") for n in range(2)]
        D1, BC = ps("m_d1_ps"), ps("m_bc_ps")
        sem = lambda n: nm.sems.new(n)
        sq_ready, ms_ready, rms_ready, xr_ready = sem("m_sq"), sem("m_ms"), sem("m_rms_r"), sem("m_xr_r")
        a_ready, padded, nw_ready, bc_out = sem("m_a"), sem("m_pad"), sem("m_nw"), sem("m_bc_out")
        (in_ps, sk_ps, d1_ps, d2_ps, bc_ps, cin_r, x2_r, gt_r, d1_r, bc_r, az_r, ez_r, lz_r, cv_r, tap_r, rz_r,
         dl_r, dx_r) = cs = counts(
            nm.sems, m_in_ps=4, m_sk_ps=4, m_d1p=1, m_d2p=4, m_bcp=1, m_cin_r=4, m_x2_r=4, m_gt_r=4, m_d1r=1,
            m_bc_r=1, m_az_r=4, m_ez_r=4, m_lz_r=4, m_cv_r=4, m_tap_r=12, m_rz_r=4, m_dl_r=4, m_dx_r=4)
        pe = [in_ps, sk_ps, d1_ps, d2_ps, bc_ps]
        act = [cin_r, x2_r, gt_r, d1_r, bc_r, az_r, ez_r, lz_r]
        pool = [dx_r]
        block = ctx.enter_context(nc.Block())

        def half(t, e, i):
            return t[:, e, bass.ds(i * HALF, HALF)]

        @block.sync
        def _(eng):
            for i in range(2):
                bc_r.now(eng, i, 0)
                at = slice(i * HALF, (i + 1) * HALF)
                eng.dma_start(keep.bc_dram[:, at], bc[:, at]).then_inc(bc_out, 16)
                eng.wait_ge(bc_out, 16 * (i + 1))
                if i == 0:
                    for nh in range(2):
                        keep.load_b(eng, 0, nh)
                        keep.load_c(eng, 0, nh)

        @block.gpsimd
        def _(eng):
            nm.sems.clear_stale(eng)
            for c in pool:
                c.credit(eng)
            eng.memset(cin[:, :, :, 0:KC - 1], 0.0).then_inc(padded, 1)
            nm.gpsimd(eng, 3)
            eng.wait_ge(sq_ready, NT)
            eng.tensor_scalar(ms[:, :], ss[:, :], 1.0 / D, EPS_LN, ALU.mult, ALU.add).then_inc(ms_ready, 1)
            eng.wait_ge(ms_ready, 1)
            eng.tensor_tensor(rms[:, :], ms[:, :], nm.mhalf[:, :], ALU.pow).then_inc(rms_ready, 1)
            eng.tensor_tensor(nm.X[:, :, :, :], nm.X[:, :, :, :], nm.XN[:, :, :, :], ALU.add)
            with eng.Fori(0, 2) as i:
                for e in range(KE):
                    dl_r.now(eng, i, e)
                    eng.tensor_tensor(half(keep.dx, e, i), half(keep.delta, e, i), half(keep.x2, e, i),
                                      ALU.mult).then_inc(dx_r.sem, 1)

        @block.tensor
        def _(eng):
            for c in pe:
                c.credit(eng)
            nm.tensor(eng, 3, IN, XR, xr_ready, TT)
            eng.wait_ge(nm.xnT_ready, 4 * B)
            for name in ("m_skip", "m_in", "m_d1", "m_d2", "m_bc"):
                eng.wait_ge(w[name][1], 16)
            with eng.Fori(0, 2) as i:
                for e in range(KE):
                    for bank, wt, out_c, used in ((IN[e % 2], w["m_in"][0], in_ps, cin_r), (SK[e % 2], w["m_skip"][0], sk_ps, gt_r)):
                        (used.now(eng, i, e - 2) if e >= 2 else used.before(eng, i, e + 2))
                        for k in range(KD):
                            mm = eng.matmul(bank[:, :], wt[:, k, e * P:(e + 1) * P], half(nm.xnT, k, i),
                                            start=(k == 0), stop=(k == KD - 1))
                        mm.then_inc(out_c.sem, 1)
                d1_r.before(eng, i, 0)
                for e in range(KE):
                    x2_r.now(eng, i, e)
                    mm = eng.matmul(D1[:, :], w["m_d1"][0][:, e, :], half(keep.x2, e, i), start=(e == 0), stop=(e == KE - 1))
                mm.then_inc(d1_ps.sem, 1)
                bc_r.before(eng, i, 0)
                for e in range(KE):
                    with fresh_addresses(nc):
                        mm = eng.matmul(BC[0:2 * NS, :], w["m_bc"][0][:, e, :], half(keep.x2, e, i), start=(e == 0),
                                        stop=(e == KE - 1))
                mm.then_inc(bc_ps.sem, 1)
                d1_r.now(eng, i, 0)
                for e in range(KE):
                    if e >= 2:
                        az_r.now(eng, i, e - 2)
                        rz_r.now(eng, i, e - 2)
                    else:
                        az_r.before(eng, i, e + 2)
                        rz_r.before(eng, i, e + 2)
                    eng.matmul(D2[e % 2][:, :], w["m_d2"][0][:, e * P:(e + 1) * P], d1[:, :], start=True,
                               stop=True).then_inc(d2_ps.sem, 1)

        @block.scalar
        def _(eng):
            for c in act:
                c.credit(eng)
            eng.wait_ge(w["m_small"][1], 16)
            for t in range(NT):
                eng.wait_ge(nm.xn_ready, 3 * NT + t + 1)
                if t:
                    eng.wait_ge(sq_ready, t)
                eng.activation(sq[:, :], nm.XN[:, t // TT, t % TT, :], ACT.Square,
                               accum_out=ss[:, t:t + 1]).then_inc(sq_ready, 1)
            eng.activation(keep.A[:, :], a_log, ACT.Exp).then_inc(a_ready, 1)
            nm.scalar(eng, 3, IN, norm_w)
            with eng.Fori(0, 2) as i:
                for e in range(KE):
                    in_ps.now(eng, i, e)
                    (cv_r.now(eng, i, e - 2) if e >= 2 else cv_r.before(eng, i, e + 2))
                    eng.activation(cin[:, e % 2, :, KC - 1:], IN[e % 2][:, :].rearrange("p (b t) -> p b t", b=2),
                                   ACT.Copy).then_inc(cin_r.sem, 1)
                    sk_ps.now(eng, i, e)
                    eng.activation(half(keep.gate, e, i), SK[e % 2][:, :], ACT.Silu).then_inc(gt_r.sem, 1)
                    if e:
                        cv_r.now(eng, i, e - 1)
                        eng.activation(half(keep.x2, e - 1, i), cv[:, (e - 1) % 2, :, :].rearrange("p b t -> p (b t)"),
                                       ACT.Silu, bias=conv_b[:, e - 1:e]).then_inc(x2_r.sem, 1)
                cv_r.now(eng, i, KE - 1)
                eng.activation(half(keep.x2, KE - 1, i), cv[:, (KE - 1) % 2, :, :].rearrange("p b t -> p (b t)"),
                               ACT.Silu, bias=conv_b[:, KE - 1:KE]).then_inc(x2_r.sem, 1)
                d1_ps.now(eng, i, 0)
                d2_ps.before(eng, i, 3)
                eng.activation(d1[:, :], D1[:, :], ACT.Copy).then_inc(d1_r.sem, 1)
                bc_ps.now(eng, i, 0)
                eng.activation(bc[:, bass.ds(i * HALF, HALF)], BC[0:2 * NS, :], ACT.Copy).then_inc(bc_r.sem, 1)
                for e in range(KE):
                    d2_ps.now(eng, i, e)
                    (ez_r.now(eng, i, e - 1) if e else ez_r.before(eng, i, KE - 1))
                    eng.activation(az[:, :], D2[e % 2][:, :], ACT.Abs, bias=b_d2[:, e:e + 1]).then_inc(az_r.sem, 1)
                    az_r.now(eng, i, e)
                    lz_r.before(eng, i, e)
                    eng.activation(ez[:, e, :], az[:, :], ACT.Exp, scale=-1.0).then_inc(ez_r.sem, 1)
                for e in range(KE):
                    ez_r.now(eng, i, e)
                    (dl_r.now(eng, i, e - 2) if e >= 2 else dl_r.before(eng, i, e + 2))
                    eng.activation(lz[:, e % 2, :], ez[:, e, :], ACT.Ln, bias=1.0).then_inc(lz_r.sem, 1)

        @block.vector
        def _(eng):
            for c in cs:
                if c not in pe + act + pool:
                    c.credit(eng)
            nm.vector(eng, 3)
            eng.wait_ge(rms_ready, 1)
            for t in range(NT):
                eng.tensor_scalar(XR[:, t // TT, t % TT, :], nm.XN[:, t // TT, t % TT, :], rms[:, t:t + 1], None,
                                  ALU.mult).then_inc(xr_ready, 1)
            eng.wait_ge(padded, 1)
            eng.wait_ge(a_ready, 1)
            eng.tensor_scalar(keep.A[:, :], keep.A[:, :], -1.0, None, ALU.mult).then_inc(a_ready, 1)

            def relu_z(i, e):
                d2_ps.now(eng, i, e)
                az_r.now(eng, i, e)
                eng.tensor_scalar(half(keep.delta, e, i), D2[e % 2][:, :], b_d2[:, e:e + 1], 0.0, ALU.add, ALU.max)\
                   .then_inc(rz_r.sem, 1)

            def delta(i, e):
                lz_r.now(eng, i, e)
                rz_r.now(eng, i, e)
                eng.tensor_tensor(half(keep.delta, e, i), half(keep.delta, e, i), lz[:, e % 2, :], ALU.add).then_inc(dl_r.sem, 1)

            with eng.Fori(0, 2) as i:
                for e in range(KE):
                    cin_r.now(eng, i, e)
                    (x2_r.now(eng, i, e - 2) if e >= 2 else x2_r.before(eng, i, e + 2))
                    eng.tensor_scalar(cv[:, e % 2, :, :], cin[:, e % 2, :, 0:S], conv_w[:, e * KC:e * KC + 1], None,
                                      ALU.mult).then_inc(tap_r.sem, 1)
                    for q in range(1, KC):
                        tap_r.now(eng, i, 3 * e + q - 1)
                        eng.scalar_tensor_tensor(cv[:, e % 2, :, :], cin[:, e % 2, :, q:q + S],
                                                 conv_w[:, e * KC + q:e * KC + q + 1], cv[:, e % 2, :, :],
                                                 ALU.mult, ALU.add).then_inc((cv_r if q == KC - 1 else tap_r).sem, 1)
                for e in range(KE):
                    relu_z(i, e)
                for e in range(KE):
                    delta(i, e)


class Keep:

    def __init__(self, ctx, nc):
        sb, _ = buffers(ctx, nc)
        self.x2, self.gate = sb("m_x2T", [P, KE, T]), sb("m_gateT", [P, KE, T])
        self.delta, self.dx = sb("m_deltaT", [P, KE, T]), sb("m_dxT", [P, KE, T])
        self.A = sb("m_A", [P, KE * NS])
        self.B, self.C = sb("m_B", [P, 2, NS // 2, S]), sb("m_C", [P, 2, NS // 2, S])
        self.b_in = [nc.alloc_semaphore(f"m_b_in{n}") for n in range(2)]
        self.c_in = [nc.alloc_semaphore(f"m_c_in{n}") for n in range(2)]
        self.bc_dram = nc.dram_tensor("bc_scratch", (2 * NS, T), F32, kind="Internal").ap()

    def rows(self, b, at):
        return self.bc_dram[at:at + NS // 2, bass.ds(b * S, S)][None, :, :].to_broadcast((P, NS // 2, S))

    def load_b(self, eng, b, nh):
        eng.dma_start(self.B[:, nh, :, :], self.rows(b, nh * NS // 2)).then_inc(self.b_in[nh], 16)

    def load_c(self, eng, b, nh):
        eng.dma_start(self.C[:, nh, :, :], self.rows(b, NS + nh * NS // 2)).then_inc(self.c_in[nh], 16)


def scan(nc, nm, w, dram, keep):
    with ExitStack() as ctx:
        sb, ps = buffers(ctx, nc)
        NH = NS // 2
        U = 2 * KE
        NB, ND = 4, 2
        Bb, Cb, b_in, c_in = keep.B, keep.C, keep.b_in, keep.c_in
        dec = sb("m_decay", [P, ND, NH, S])
        hb = sb("m_h", [P, NB, NH, S])
        y1, yT = sb("m_y1", [P, KE, S]), sb("m_yT", [P, KE, S])
        Y = ps("m_y_ps", 2)
        O = ps("m_out_ps")
        W_D = w["m_small"][0][:, KD + 2 * KE:KD + 3 * KE]
        zeroed = nm.sems.new("m_zeroed")
        (y_ps, dec_r, u_r, h_r, p_r) = counts(nm.sems, m_y_r=U, m_dec_r=U, m_u_r=U, m_h_r=U, m_p_r=U)
        (y1_r, yT_r, o_ps, x_r) = counts(nm.sems, m_y1_r=KE, m_yT_r=1, m_o_r=1, m_xadd=1)

        def batches(eng, body):
            body(0, False)
            with eng.Fori(1, B) as i:
                body(i, True)

        block = ctx.enter_context(nc.Block())

        @block.sync
        def _(eng):
            with eng.Fori(1, B) as i:
                for nh in range(2):
                    u_r.before(eng, i, KE * (nh + 1) - 1)
                    keep.load_b(eng, i, nh)
                    p_r.before(eng, i, KE * (nh + 1) - 1)
                    keep.load_c(eng, i, nh)

        @block.scalar
        def _(eng):
            dec_r.credit(eng)
            eng.wait_ge(zeroed, 1)
            with fresh_addresses(nc), eng.Fori(0, B) as i:
                for u in range(U):
                    nh, e = u // KE, u % KE
                    (h_r.now(eng, i, u - ND) if u >= ND else h_r.before(eng, i, U - ND + u))
                    for n in range(NH):
                        s = e * NS + nh * NH + n
                        a = eng.activation(dec[:, u % ND, n, 1:S], keep.delta[:, e, bass.ds(i * S + 1, S - 1)], ACT.Exp,
                                           scale=keep.A[:, s:s + 1])
                    a.then_inc(dec_r.sem, 1)

        @block.gpsimd
        def _(eng):
            nm.sems.clear_stale(eng)
            u_r.credit(eng)
            eng.memset(dec[:, :, :, 0:1], 0.0).then_inc(zeroed, 1)

            with fresh_addresses(nc), eng.Fori(0, B) as i:
                for u in range(U):
                    nh, e = u // KE, u % KE
                    if e == 0:
                        eng.wait_ge(b_in[nh], 16 * i + 16)
                    (y_ps.now(eng, i, u - NB) if u >= NB else y_ps.before(eng, i, U - NB + u))
                    eng.tensor_tensor(hb[:, u % NB, :, :], Bb[:, nh, :, :],
                                      keep.dx[:, e, bass.ds(i * S, S)][:, None, :].to_broadcast((P, NH, S)),
                                      ALU.mult).then_inc(u_r.sem, 1)

        @block.vector
        def _(eng):
            for c in (h_r, p_r):
                c.credit(eng)
            for c in (y1_r, yT_r, x_r):
                c.credit(eng, 2)
            flat = lambda t: t.rearrange("p n t -> p (n t)")

            def gated(i):
                yT_r.before(eng, i, 0)
                for e in range(KE):
                    y_ps.before(eng, i, KE + e | 1)
                    eng.scalar_tensor_tensor(y1[:, e, :], keep.x2[:, e, bass.ds((i - 1) * S, S)], W_D[:, e:e + 1],
                                             Y[:, e * S:(e + 1) * S], ALU.mult, ALU.add).then_inc(y1_r.sem, 1)
                y1_r.now(eng, i, KE - 1)
                o_ps.before(eng, i, 0)
                eng.tensor_tensor(yT[:, :, :], y1[:, :, :], keep.gate[:, :, bass.ds((i - 1) * S, S)], ALU.mult)\
                   .then_inc(yT_r.sem, 1)

            def add(i):
                o_ps.now(eng, i, 0)
                eng.tensor_tensor(nm.X[:, i - 1, :, :], nm.X[:, i - 1, :, :], O[:, :].rearrange("p (h f) -> p h f", h=TT),
                                  ALU.add).then_inc(x_r.sem, 1)

            def units(i, end_before):
                for u in range(U):
                    nh, e = u // KE, u % KE
                    dec_r.now(eng, i, u)
                    u_r.now(eng, i, u)
                    eng.tensor_tensor_scan(flat(hb[:, u % NB, :, :]), flat(dec[:, u % ND, :, :]), flat(hb[:, u % NB, :, :]),
                                           0.0, ALU.mult, ALU.add).then_inc(h_r.sem, 1)
                    if e == 0:
                        eng.wait_ge(c_in[nh], 16 * i + 16)
                    h_r.now(eng, i, u)
                    eng.tensor_tensor(hb[:, u % NB, :, :], hb[:, u % NB, :, :], Cb[:, nh, :, :], ALU.mult).then_inc(p_r.sem, 1)
                    if end_before and u == 0:
                        gated(i)
                    if end_before and u == 3:
                        add(i)

            batches(eng, units)
            gated(B)
            add(B)

        @block.tensor
        def _(eng):
            y_ps.credit(eng)
            o_ps.credit(eng, 2)
            eng.wait_ge(w["m_out"][1], 16)

            def out_product(i):
                yT_r.now(eng, i, 0)
                x_r.before(eng, i, 0)
                for h in range(TT):
                    for e in range(KE):
                        mm = eng.matmul(O[:, h * D:(h + 1) * D], yT[:, e, h * P:(h + 1) * P], w["m_out"][0][:, e, :],
                                        start=(e == 0), stop=(e == KE - 1))
                mm.then_inc(o_ps.sem, 1)

            def units(i, end_before):
                y1_r.now(eng, i, KE - 1)
                for u in range(U):
                    nh, e = u // KE, u % KE
                    p_r.now(eng, i, u)
                    for n in range(NH):
                        mm = eng.matmul(Y[:, e * S:(e + 1) * S], nm.ident[:, :], hb[:, u % NB, n, :],
                                        start=(nh == 0 and n == 0 and e % 2 == 0), stop=(nh == 1 and n == NH - 1),
                                        skip_group_check=True)
                    mm.then_inc(y_ps.sem, 1)
                    if end_before and u == 1:
                        out_product(i)

            batches(eng, units)
            out_product(B)


def selective_scan(nc, nm, w, dram):
    with ExitStack() as ctx:
        keep = Keep(ctx, nc)
        scan_inputs(nc, nm, w, dram, keep)
        nm.sems.next_phase()
        scan(nc, nm, w, dram, keep)


def context_attention(nc, nm, w, dram):
    with ExitStack() as ctx:
        sb, ps = buffers(ctx, nc)
        qT, kT = sb("c_qT", [P, S]), sb("c_kT", [P, S])
        nmax, sums, rs = sb("c_neg_max", [P, TT]), sb("c_sums", [P, TT]), sb("c_rsums", [P, TT])
        E, AT = sb("c_probs", [P, TT, S]), sb("c_probsT", [P, KD, S])
        AN = sb("c_probs_norm", [P, TT, S])
        xcur = sb("c_x", [P, KD, S])
        QP, KP, EP, TP, OP = (ps(f"c_{n}") for n in ("q", "k", "energy", "turned", "out"))
        L0, L1 = ps("c_ln0"), ps("c_ln1")
        (q_ps, k_ps, e_ps, t_ps, o_ps, q_sb, k_sb, ex, at_sb, mx, rs_r, an_r, x_r, xc_r) = cs = counts(
            nm.sems, c_q_ps=1, c_k_ps=1, c_e_ps=1, c_t_ps=1, c_o_ps=1, c_q_sb=1, c_k_sb=1, c_ex=2, c_at=1, c_mx=1,
            c_rs=1, c_an=2, c_xadd=1, c_xc=1)
        pe, act, pool = [q_ps, k_ps, e_ps, t_ps, o_ps], [q_sb, k_sb, ex, at_sb], [xc_r]
        qk = w["x_qk"][0]
        block = ctx.enter_context(nc.Block())

        @block.gpsimd
        def _(eng):
            nm.sems.clear_stale(eng)
            for c in pool:
                c.credit(eng)
            nm.gpsimd(eng, 4)
            eng.wait_ge(nm.xnT_ready, 5 * B)
            with eng.Fori(0, B) as i:
                o_ps.before(eng, i, 0)
                eng.tensor_copy(xcur[:, :, :], nm.xnT[:, :, bass.ds(i * S, S)]).then_inc(xc_r.sem, 1)

        @block.tensor
        def _(eng):
            for c in pe:
                c.credit(eng)
            nm.tensor(eng, 4, (L0, L1))
            eng.wait_ge(w["ctxT"][1], 16)
            eng.wait_ge(w["x_qk"][1], 16)
            with eng.Fori(0, B) as i:
                q_sb.before(eng, i, 0)
                eng.matmul(QP[:, 0:S], qk[:, 0:P], w["ctxT"][0][:, i, :], start=True, stop=True).then_inc(q_ps.sem, 1)
                k_sb.before(eng, i, 0)
                eng.matmul(KP[:, 0:S], qk[:, P:2 * P], w["ctxT"][0][:, i, :], start=True, stop=True).then_inc(k_ps.sem, 1)
                q_sb.now(eng, i, 0)
                k_sb.now(eng, i, 0)
                ex.before(eng, i, 1)
                for h in range(TT):
                    mm = eng.matmul(EP[:, h * S:(h + 1) * S], qT[:, h * P:(h + 1) * P], kT[:, :], start=True, stop=True)
                mm.then_inc(e_ps.sem, 1)
                an_r.now(eng, i, 1)
                at_sb.before(eng, i, 0)
                for h in range(TT):
                    for k in range(KD):
                        mm = eng.transpose(TP[:, k * S + h * P:k * S + (h + 1) * P], AN[:, h, k * P:(k + 1) * P], nm.ident[:, :])
                mm.then_inc(t_ps.sem, 1)
                at_sb.now(eng, i, 0)
                xc_r.now(eng, i, 0)
                x_r.before(eng, i, 0)
                for h in range(TT):
                    for k in range(KD):
                        mm = eng.matmul(OP[:, h * S:(h + 1) * S], xcur[:, k, h * P:(h + 1) * P], AT[:, k, :],
                                        start=(k == 0), stop=(k == KD - 1))
                mm.then_inc(o_ps.sem, 1)

        @block.scalar
        def _(eng):
            for c in act:
                c.credit(eng)
            nm.scalar(eng, 4, (L0, L1))
            with eng.Fori(0, B) as i:
                e_ps.before(eng, i, 0)
                q_ps.now(eng, i, 0)
                eng.activation(qT[:, :], QP[:, 0:S], ACT.Identity, bias=qk[:, 2 * P:2 * P + 1]).then_inc(q_sb.sem, 1)
                k_ps.now(eng, i, 0)
                eng.activation(kT[:, :], KP[:, 0:S], ACT.Identity, bias=qk[:, 2 * P + 1:2 * P + 2]).then_inc(k_sb.sem, 1)
                mx.now(eng, i, 0)
                an_r.before(eng, i, 1)
                for h in range(TT):
                    eng.activation(E[:, h, :], EP[:, h * S:(h + 1) * S], ACT.Exp, bias=nmax[:, h:h + 1],
                                   accum_out=sums[:, h:h + 1]).then_inc(ex.sem, 1)
                t_ps.now(eng, i, 0)
                o_ps.before(eng, i, 0)
                eng.activation(AT[:, :, :], TP[:, :].rearrange("p (k t) -> p k t", k=KD), ACT.Copy).then_inc(at_sb.sem, 1)

        @block.vector
        def _(eng):
            for c in cs:
                if c not in pe + act + pool:
                    c.credit(eng)
            nm.vector(eng, 4)
            with eng.Fori(0, B) as i:
                e_ps.now(eng, i, 0)
                ex.before(eng, i, 1)
                eng.tensor_reduce(nmax[:, :], EP[:, :].rearrange("p (h t) -> p h t", h=TT), AX.X, ALU.max,
                                  negate=True).then_inc(mx.sem, 1)
                ex.now(eng, i, 1)
                an_r.before(eng, i, 1)
                eng.reciprocal(rs[:, :], sums[:, :]).then_inc(rs_r.sem, 1)
                rs_r.now(eng, i, 0)
                t_ps.before(eng, i, 0)
                for h in range(TT):
                    eng.tensor_scalar(AN[:, h, :], E[:, h, :], rs[:, h:h + 1], None, ALU.mult).then_inc(an_r.sem, 1)
                o_ps.now(eng, i, 0)
                eng.tensor_tensor(nm.X[:, i, :, :], nm.X[:, i, :, :], OP[:, :].rearrange("p (h f) -> p h f", h=TT),
                                  ALU.add).then_inc(x_r.sem, 1)


def experts(nc, nm, w, dram, out):
    with ExitStack() as ctx:
        sb, ps = buffers(ctx, nc)
        NT, NR, NW = B * TT, NX + 1, NX + 4
        nmax, tops = sb("e_neg_max", [P, NT]), sb("e_tops", [P, NT, 8])
        EV, REST = sb("e_exp", [P, NT, NW]), sb("e_rest", [P, NT, NW])
        tot, rtot = sb("e_total", [P, NT]), sb("e_rtotal", [P, NT])
        SH0, SH = sb("e_share0", [P, NT, NX]), sb("e_share", [P, NT, NR])
        SHT = sb("e_shareT", [NR, T])
        RING = 3
        W = sb("e_weights", [P, RING, 3 * KD * P])
        WH, WL = (sb(f"e_weights_{n}", [P, RING, 3 * KD * P], F32R) for n in ("high", "low"))
        x = SplitX(nm, sb, "e")
        AH, AL = (sb(f"e_act_{n}", [P, 2, HALF], F32R) for n in ("high", "low"))
        CB = sb("e_share_rows", [P, RING, T])
        SG = sb("e_silu", [P, 2, HALF])
        GU = sb("e_gated", [P, 2, HALF])
        AC = sb("e_act", [P, 2, HALF])
        GP, UP = [ps(f"e_gate{n}") for n in range(2)], [ps(f"e_up{n}") for n in range(2)]
        OUT = [ps(f"e_out{n}") for n in range(4)]
        sem = lambda n: nm.sems.new(n)
        lg_r, nmx_r, ev_r, sg_r, top_r, cut_r, rest_r = (sem(f"e_{n}") for n in ("lg", "nmx", "ev", "sgm", "top", "cut", "rest"))
        sh0_r, tot_r, rtot_r, sh_r, sht_ps, sht_r, sht_out, done, stored = (
            sem(f"e_{n}") for n in ("sh0", "tot", "rtot", "sh", "shtp", "sht", "shtout", "done", "stored"))
        w_in = [sem(f"e_w_in{n}") for n in range(RING)]
        c_in = [[sem(f"e_c_in{n}{a}") for a in range(2)] for n in range(RING)]
        (g_ps, u_ps, dn, si, gu_r, ac_r, wh_r, wl_r, ah_r, al_r) = cs = counts(
            nm.sems, e_g_ps=6, e_u_ps=6, e_dn=6, e_si=6, e_gu=6, e_ac=6, e_wh=3, e_wl=3, e_ah=6, e_al=6)
        pe, act, pool = [g_ps, u_ps, dn], [si, wh_r, ah_r], [ac_r]
        share_dram = nc.dram_tensor("share_scratch", (NR, T), F32, kind="Internal").ap()
        HT = HALF // P
        PASSES = 1 + NX * FX // P // RING
        LAST = PASSES

        def passes(eng, body):
            body(0, RING, True, False)
            with eng.Fori(1, PASSES) as i:
                body(i, RING, False, False)
            body(LAST, 1, False, True)

        block = ctx.enter_context(nc.Block())

        def owners(i, r):
            if i is None:
                return [(a * P // 2, P // 2, NX) for a in range(2)]
            cut, e = FX - r * (P - FX), (RING + 1) * (i - 1) + r
            return [(0, cut, e), (cut, P - cut, e + 1)]

        @block.sync
        def _(eng):
            def weights_of(i, r):
                eng.dma_start(W[:, r, :], dram["experts"][bass.ds(i * RING + r, 1)].rearrange("a p n -> (a p) n"))\
                   .then_inc(w_in[r], 16)

            for r in range(RING):
                weights_of(0, r)
            eng.wait_ge(sht_r, 2)
            eng.dma_start(share_dram, SHT[:, :]).then_inc(sht_out, 16)
            eng.wait_ge(sht_out, 16)

            def loads(i, slots, first, last):
                for r in range(slots):
                    if not first:
                        wl_r.before(eng, i, r)
                        weights_of(i, r)
                    for a, (p, n, e) in enumerate(owners(None if first or last else i, r)):
                        if not first:
                            ac_r.before(eng, i, 2 * r + 1)
                        eng.dma_start(CB[p:p + n, r, :], share_dram[bass.ds(e, 1), :].to_broadcast((n, T)))\
                           .then_inc(c_in[r][a], 16)

            passes(eng, loads)
            for b in range(B):
                eng.wait_ge(done, b + 1)
                eng.dma_start(out[b].rearrange("(h p) f -> p h f", p=P), nm.X[:, b, :, :]).then_inc(stored, 16)
            eng.wait_ge(stored, 16 * B)

        @block.gpsimd
        def _(eng):
            nm.sems.clear_stale(eng)
            for c in pool:
                c.credit(eng)
            nm.gpsimd(eng, 5)
            eng.memset(EV[:, :, NX:NW], -1.0).then_inc(cut_r, 1)

            def share(i, slots, first, last):
                for r in range(slots):
                    eng.wait_ge(c_in[r][0], 16 * i + 16)
                    eng.wait_ge(c_in[r][1], 16 * i + 16)
                    for h in range(2):
                        u = 2 * r + h
                        gu_r.now(eng, i, u)
                        (al_r.now(eng, i, u - 2) if u >= 2 else al_r.before(eng, i, 4 + u))
                        eng.tensor_tensor(AC[:, h, :], GU[:, h, :], CB[:, r, h * HALF:(h + 1) * HALF], ALU.mult).then_inc(ac_r.sem, 1)

            passes(eng, share)

        @block.tensor
        def _(eng):
            for c in pe:
                c.credit(eng)
            nm.tensor(eng, 5, GP)
            eng.wait_ge(nm.xnT_ready, 6 * B)
            eng.wait_ge(w["router"][1], 16)
            for t in range(NT):
                for k in range(KD):
                    mm = eng.matmul(OUT[0][:, t * 64:t * 64 + NR], nm.xnT[:, k, t * P:(t + 1) * P], w["router"][0][:, k, :],
                                    start=(k == 0), stop=(k == KD - 1))
            mm.then_inc(lg_r, 1)
            eng.wait_ge(x.low_ready, 2)

            def turn_shares():
                eng.wait_ge(sh_r, 2)
                for t in range(NT):
                    mm = eng.transpose(OUT[2 + t // 4][0:NR, (t % 4) * P:(t % 4 + 1) * P], SH[:, t, :], nm.ident[:, :])
                mm.then_inc(sht_ps, 1)

            def down(r, h, ready, start=False, stop=False):
                ready()
                at = slice(2 * KD * P, None)
                for t in range(HT):
                    n = h * HT + t
                    rows = slice(t * P, (t + 1) * P)
                    mm = split_product(eng, OUT[n // 2][:, (n % 2) * D:(n % 2 + 1) * D],
                                       [(AH[:, h, rows], AL[:, h, rows], WH[:, r, at], WL[:, r, at])],
                                       start=(start and n % 2 == 0), stop=stop)
                mm.then_inc(dn.sem, 1)

            def chunks(i, slots, first, last):
                for u in range(2 * slots):
                    r, h = u // 2, u % 2
                    if h == 0:
                        wl_r.now(eng, i, r)
                    if u >= 2:
                        si.now(eng, i, u - 2)
                        gu_r.now(eng, i, u - 2)
                    else:
                        si.before(eng, i, 4 + u)
                        gu_r.before(eng, i, 4 + u)
                    for bank, at, cnt in ((GP[h], 0, g_ps), (UP[h], KD * P, u_ps)):
                        cols = lambda k: slice(at + k * P, at + (k + 1) * P)
                        split_product(eng, bank[:, :], [(WH[:, r, cols(k)], WL[:, r, cols(k)], *x.half(k, h))
                                                        for k in range(KD)]).then_inc(cnt.sem, 1)
                    if first and u == 1:
                        turn_shares()
                    if first and u == 2:
                        eng.wait_ge(sht_r, 2)
                    if u >= 2:
                        down(r - 1, h, lambda: al_r.now(eng, i, u - 2), first and r == 1)
                    elif not first:
                        down(RING - 1, h, lambda: al_r.before(eng, i, 4 + u))

            passes(eng, chunks)
            for h in range(2):
                down(0, h, lambda: al_r.now(eng, LAST, h), stop=True)

        @block.scalar
        def _(eng):
            for c in act:
                c.credit(eng)
            def high_weights(i, r, first):
                if r == RING:
                    dn.now(eng, i, 1)
                elif not first:
                    dn.before(eng, i, 2 * r + 1)
                eng.wait_ge(w_in[r % RING], 16 * (i + r // RING) + 16)
                eng.activation(WH[:, r % RING, :], W[:, r % RING, :], ACT.Copy).then_inc(wh_r.sem, 1)

            nm.scalar(eng, 5, GP, after=x.scalar)
            high_weights(0, 0, True)
            eng.wait_ge(nmx_r, 1)
            eng.wait_ge(cut_r, 1)
            lg = OUT[0][:, :].rearrange("p (t c) -> p t c", c=64)
            for t in range(NT):
                eng.activation(EV[:, t, 0:NX], lg[:, t, 0:NX], ACT.Exp, bias=nmax[:, t:t + 1]).then_inc(ev_r, 1)
            eng.activation(SH[:, :, NX], lg[:, :, NX], ACT.Sigmoid).then_inc(sh_r, 1)
            for n in range(2):
                eng.wait_ge(sht_ps, 1)
                eng.activation(SHT[:, n * HALF:(n + 1) * HALF], OUT[2 + n][0:NR, :], ACT.Copy).then_inc(sht_r, 1)

            def high(i, u, ac, free):
                ac()
                free()
                eng.activation(AH[:, u % 2, :], AC[:, u % 2, :], ACT.Copy).then_inc(ah_r.sem, 1)

            def silus(i, slots, first, last):
                for u in range(2 * slots):
                    if u % 2 == 0 and not last:
                        high_weights(i, u // 2 + 1, first)
                    g_ps.now(eng, i, u)
                    (gu_r.now(eng, i, u - 2) if u >= 2 else gu_r.before(eng, i, 4 + u))
                    eng.activation(SG[:, u % 2, :], GP[u % 2][:, :], ACT.Silu).then_inc(si.sem, 1)
                    if u:
                        high(i, u - 1, lambda: ac_r.now(eng, i, u - 1),
                             lambda: dn.now(eng, i, u - 3) if u >= 3 else dn.before(eng, i, u + 3))
                    elif not first:
                        high(i, 5, lambda: ac_r.before(eng, i, 5), lambda: dn.before(eng, i, 3))

            passes(eng, silus)
            high(LAST, 1, lambda: ac_r.now(eng, LAST, 1), lambda: dn.before(eng, LAST, 5))

        @block.vector
        def _(eng):
            for c in cs:
                if c not in pe + act + pool:
                    c.credit(eng)
            def low_weights(i, r, first):
                wh_r.now(eng, i, r)
                if r == RING:
                    dn.now(eng, i, 1)
                elif not first:
                    dn.before(eng, i, 2 * r + 1)
                eng.tensor_tensor(WL[:, r % RING, :], W[:, r % RING, :], WH[:, r % RING, :].bitcast(F32), ALU.subtract)\
                   .then_inc(wl_r.sem, 1)

            nm.vector(eng, 5)
            x.vector(eng)
            low_weights(0, 0, True)
            eng.wait_ge(lg_r, 1)
            lg = OUT[0][:, :].rearrange("p (t c) -> p t c", c=64)
            eng.tensor_reduce(nmax[:, :], lg[:, :, 0:NX], AX.X, ALU.max, negate=True).then_inc(nmx_r, 1)
            for t in range(NT):
                eng.wait_ge(ev_r, t + 1)
                eng.max(tops[:, t, :], EV[:, t, 0:NX]).then_inc(top_r, 1)
            eng.wait_ge(top_r, NT)
            eng.memset(tops[:, :, 4:8], -1.0).then_inc(cut_r, 1)
            eng.wait_ge(cut_r, 2)
            for t in range(NT):
                eng.match_replace(REST[:, t, :], tops[:, t, :], EV[:, t, :], 0.0).then_inc(rest_r, 1)
            eng.wait_ge(rest_r, NT)
            eng.tensor_tensor(SH0[:, :, :], EV[:, :, 0:NX], REST[:, :, 0:NX], ALU.subtract).then_inc(sh0_r, 1)
            eng.wait_ge(sh0_r, 1)
            eng.tensor_reduce(tot[:, :], SH0[:, :, :], AX.X, ALU.add).then_inc(tot_r, 1)
            eng.wait_ge(tot_r, 1)
            eng.reciprocal(rtot[:, :], tot[:, :]).then_inc(rtot_r, 1)
            eng.wait_ge(rtot_r, 1)
            eng.tensor_tensor(SH[:, :, 0:NX], SH0[:, :, :], rtot[:, :, None].to_broadcast((P, NT, NX)), ALU.mult).then_inc(sh_r, 1)

            def low(i, u, ah, free):
                ah()
                free()
                eng.tensor_tensor(AL[:, u % 2, :], AC[:, u % 2, :], AH[:, u % 2, :].bitcast(F32), ALU.subtract)\
                   .then_inc(al_r.sem, 1)

            def gated(i, slots, first, last):
                for u in range(2 * slots):
                    if u % 2 == 0 and not last:
                        low_weights(i, u // 2 + 1, first)
                    si.now(eng, i, u)
                    u_ps.now(eng, i, u)
                    (ac_r.now(eng, i, u - 2) if u >= 2 else ac_r.before(eng, i, 4 + u))
                    eng.tensor_tensor(GU[:, u % 2, :], SG[:, u % 2, :], UP[u % 2][:, :], ALU.mult).then_inc(gu_r.sem, 1)
                    if u:
                        low(i, u - 1, lambda: ah_r.now(eng, i, u - 1),
                            lambda: dn.now(eng, i, u - 3) if u >= 3 else dn.before(eng, i, u + 3))
                    elif not first:
                        low(i, 5, lambda: ah_r.before(eng, i, 5), lambda: dn.before(eng, i, 3))

            passes(eng, gated)
            low(LAST, 1, lambda: ah_r.now(eng, LAST, 1), lambda: dn.before(eng, LAST, 5))
            for b in range(B):
                dn.now(eng, LAST, b // 2)
                eng.tensor_tensor(nm.X[:, b, :, :], nm.X[:, b, :, :], OUT[b][:, :].rearrange("p (h f) -> p h f", h=TT),
                                  ALU.add).then_inc(done, 1)


def build(nc, dram, out, upto=99):
    with ExitStack() as ctx:
        nm = Norm(ctx, nc)
        late = weights(ctx, nc, LATE)
        with ExitStack() as parts:
            sb, _ = buffers(parts, nc)
            split = {f"{name}_{n}": sb(f"{name}_{n}", shape, F32R)
                     for name, shape in EARLY if name in SPLIT for n in ("high", "low")}
            with ExitStack() as first:
                w = weights(first, nc, EARLY) | late
                attention(nc, nm, w, split, dram)
                nm.sems.next_phase()
                if upto > 1:
                    quantised(nc, nm, w, split, dram)
                    nm.sems.next_phase()
            if upto > 2:
                sparse(nc, nm, split, dram)
                nm.sems.next_phase()
        for phase in PHASES[:max(upto - 3, 0)]:
            phase(nc, nm, late, dram, *([out] if phase is experts else []))
            nm.sems.next_phase()


PHASES = (selective_scan, context_attention, experts)


def layout(i):
    c = np.ascontiguousarray

    def tiles(a):
        return c(a.reshape(-1, P, a.shape[-1]).transpose(1, 0, 2))

    def cols(a):
        return a.reshape(-1, P).T

    low_rows = np.stack([np.arange(P) // (2 * HD) % 2, np.arange(P) // HD % 2], axis=1)
    out = {
        "part_masks": np.where(low_rows, -1, 0).astype(np.float32),
        "x": c(i["x"].reshape(B, TT, P, D).transpose(0, 2, 1, 3)),
        "wq": tiles(i["L0_attn_Wq"].T), "wk": tiles(i["L0_attn_Wk"].T),
        "wv": tiles(i["L0_attn_Wv"].T), "wo": tiles(i["L0_attn_Wo"].T),
        "fsT": c(i["fside_BxS2xS2_0"].transpose(0, 2, 1).reshape(B, KD, P, D).transpose(2, 0, 1, 3)),
        "ctxT": c(i["ctx_1024"].transpose(2, 0, 1)),
        "f_gate": tiles(i["L0_ffn_w_gate"].reshape(D, 2, P, 4).transpose(0, 1, 3, 2).reshape(D, FF)),
        "f_up": tiles(i["L0_ffn_w_up"].reshape(D, 2, P, 4).transpose(0, 1, 3, 2).reshape(D, FF)),
        "f_down": c(i["L0_ffn_w_down"].reshape(2, P, 4, D).transpose(1, 0, 2, 3).reshape(P, 8, D)),
        "m_small": c(np.concatenate([
            cols(i["L1_attn_norm_w"]), cols(i["L1_attn_conv_b"]), cols(i["L1_attn_b_d2"]), cols(i["L1_attn_W_D"]),
            np.zeros((P, KE), np.float32),
            i["L1_attn_conv_w"].reshape(KE, P, KC).transpose(1, 0, 2).reshape(P, KE * KC),
            i["L1_attn_A_log"].reshape(KE, P, NS).transpose(1, 0, 2).reshape(P, KE * NS)], axis=1)),
        "m_skip": tiles(i["L1_attn_W_skip"].T), "m_in": tiles(i["L1_attn_W_in"].T),
        "m_d1": tiles(i["L1_attn_W_d1"].T), "m_d2": c(i["L1_attn_W_d2"].T),
        "m_bc": tiles(np.concatenate([i["L1_attn_W_Bm"], i["L1_attn_W_Cm"]], axis=0).T),
        "m_out": tiles(i["L1_attn_W_out"].T),
        "x_qk": c(np.concatenate([i["L1_xattn_Wq"].T, i["L1_xattn_Wk"].T, i["L1_xattn_bq"][:, None],
                                  i["L1_xattn_bk"][:, None]], axis=1)),
        "router": tiles(np.concatenate([i["L1_ffn_router_weight"].T, i["L1_ffn_sgate_w"]], axis=1)),
    }

    def experts(w, shared):
        flat = np.concatenate([shared, w.transpose(1, 0, 2).reshape(D, NX * FX)], axis=1)
        return flat.reshape(KD, P, NCH, P).transpose(2, 1, 0, 3)

    gate = experts(i["L1_ffn_w_gate"], i["L1_ffn_sw_gate"])
    up = experts(i["L1_ffn_w_up"], i["L1_ffn_sw_up"])
    down = np.concatenate([i["L1_ffn_sw_down"], i["L1_ffn_w_down"].reshape(NX * FX, D)], axis=0).reshape(NCH, P, 1, D)
    order = [0, 1, 2, *range(SCH, NCH), SCH - 1]
    out["experts"] = c(np.concatenate([gate.reshape(NCH, P, 256), up.reshape(NCH, P, 256),
                                       down.reshape(NCH, P, 256)], axis=2)[order])
    return out


def kernel(**inputs):
    import concourse.bacc as bacc
    from concourse.bass_utils import run_bass_kernel_spmd as run

    arrays = layout({k: np.asarray(v) for k, v in inputs.items()})
    nc = bacc.Bacc("TRN2", target_bir_lowering=False, num_devices=1)
    dram = {n: nc.dram_tensor(f"in_{n}", a.shape, mybir.dt.from_np(a.dtype), kind="ExternalInput").ap()
            for n, a in arrays.items()}
    out = nc.dram_tensor("out_x", (B, S, D), F32, kind="ExternalOutput").ap()
    build(nc, dram, out)
    r = run(nc, [{f"in_{n}": a for n, a in arrays.items()}], core_ids=[0])
    return r.results[0]["out_x"]
```

```python
from contextlib import ExitStack, contextmanager

import numpy as np
import concourse.bass as bass
from concourse import mybir

F32 = mybir.dt.float32
BF16 = mybir.dt.bfloat16
F32R = mybir.dt.float32r
ALU = mybir.AluOpType
ACT = mybir.ActivationFunctionType
AX = mybir.AxisListType

P = 128
B, S, D = 4, 256, 256
TT = S // P
KD = D // P
T = B * S
HEADS, HD, HP = 16, 16, 32
HG = HEADS * HP // P
I0 = D // 2
FF = 1024
EI, NS, R, KC = 512, 16, 128, 4
KE = EI // P
NX, FX, FSH = 32, 96, 512
NCH = (NX * FX + FSH) // P
SCH = FSH // P
HALF = T // 2
EPS_LN = 1e-5
EPS_Q = 1e-6
QMAX = 127.0
MAGIC = 12582912.0
ROUNDS = 6


@contextmanager
def fresh_addresses(nc):
    nc.disable_value_cache = True
    yield
    nc.disable_value_cache = False


class Count:

    def __init__(self, sem, per, lanes=1):
        self.sem, self.steps, self.per = sem, per, per * lanes

    def credit(self, eng, passes=1):
        eng.sem_inc(self.sem, passes * self.per)

    def now(self, eng, i, k, lane=0):
        eng.wait_ge(self.sem, (i + 1) * self.per + lane * self.steps + k + 1)

    def before(self, eng, i, k, lane=0):
        eng.wait_ge(self.sem, i * self.per + lane * self.steps + k + 1)

    def of(self, eng, b, k):
        eng.wait_ge(self.sem, b * self.per + k + 1)


def counts(sems, lanes=1, **per):
    return [Count(sems.new(name), n, lanes) for name, n in per.items()]


def buffers(ctx, nc):
    def sb(name, shape, dt=F32):
        return ctx.enter_context(nc.sbuf_tensor(name, shape, dt))

    def ps(name, banks=1):
        return ctx.enter_context(nc.psum_tensor(name, [P, 512 * banks], F32))

    return sb, ps


class Semaphores:

    def __init__(self, nc):
        self.nc, self.used, self.stale, self.cleared = nc, [], [], []

    def new(self, name):
        self.used.append(self.nc.alloc_semaphore(name))
        return self.used[-1]

    def clear_stale(self, eng):
        for sem in self.stale:
            eng.sem_clear(sem)
        self.cleared, self.stale = self.stale, []

    def next_phase(self):
        for sem in self.cleared:
            self.nc.release_semaphore(sem)
        self.cleared, self.stale, self.used = [], self.stale + self.used, []


class Norm:

    def __init__(self, ctx, nc):
        sb, _ = buffers(ctx, nc)
        self.nc, self.sems = nc, Semaphores(nc)
        self.X = sb("X", [P, B, TT, D])
        self.XN = sb("XN", [P, B, TT, D])
        self.xnT = sb("xnT", [P, KD, T])
        self.stats = sb("ln_stats", [P, B * TT, 6])
        self.mv = sb("ln_mean_var", [P, B * TT, 2])
        self.ve = sb("ln_var_eps", [P, B * TT])
        self.rstd = sb("ln_rstd", [P, B * TT])
        self.mhalf = sb("minus_half", [P, B * TT])
        self.half = sb("plus_half", [P, B * TT])
        self.warmed = sb("table_results", [P, 4])
        self.warm = 0
        self.ident = sb("identity", [P, P])
        self.ones = sb("ones", [P, P])
        sem = lambda n: nc.alloc_semaphore(n)
        self.x_loaded = [sem(f"x{b}_loaded") for b in range(B)]
        self.consts = sem("consts")
        self.stats_ready = sem("ln_stats_ready")
        self.mv_ready = sem("ln_mv_ready")
        self.ve_ready = sem("ln_ve_ready")
        self.rstd_ready = sem("ln_rstd_ready")
        self.xn_ready = sem("ln_xn_ready")
        self.turned = sem("ln_turned")
        self.xnT_ready = sem("ln_xnT_ready")

    def statistics(self, eng, r, b):
        with fresh_addresses(self.nc):
            for h in range(TT):
                eng.bn_stats(self.stats[:, b * TT + h, :], self.X[:, b, h, :]).then_inc(self.stats_ready, 1)

    def vector(self, eng, r, beside=None):
        n = B * TT
        if r == 0:
            for b in range(B):
                eng.wait_ge(self.x_loaded[b], 16)
                self.statistics(eng, r, b)
        for t in range(n):
            eng.wait_ge(self.stats_ready, r * n + t + 1)
            eng.bn_aggr(self.mv[:, t, :], self.stats[:, t, :]).then_inc(self.mv_ready, 1)
        if beside is not None:
            beside()
        eng.wait_ge(self.rstd_ready, r + 1)
        for t in range(n):
            eng.tensor_scalar(self.XN[:, t // TT, t % TT, :], self.X[:, t // TT, t % TT, :],
                              self.mv[:, t, 0:1], self.rstd[:, t:t + 1],
                              ALU.subtract, ALU.mult).then_inc(self.xn_ready, 1)

    def gpsimd(self, eng, r):
        if r == 0:
            eng.wait_ge(self.consts, 5)
        eng.wait_ge(self.mv_ready, (r + 1) * B * TT)
        eng.tensor_scalar(self.ve[:, :], self.mv[:, :, 1], EPS_LN, None, ALU.add).then_inc(self.ve_ready, 1)
        eng.wait_ge(self.ve_ready, r + 1)
        eng.tensor_tensor(self.rstd[:, :], self.ve[:, :], self.mhalf[:, :], ALU.pow).then_inc(self.rstd_ready, 1)

    def load_table(self, eng, function):
        self.warm += 1
        eng.activation(self.warmed[:, self.warm - 1:self.warm], self.ones[:, 0:1], function)

    def tensor(self, eng, r, banks, src=None, ready=None, per=1):
        src = self.XN if src is None else src
        if r == 0:
            eng.wait_ge(self.consts, 5)
        for b in range(B):
            if ready is None:
                eng.wait_ge(self.xn_ready, r * B * TT + TT * (b + 1))
            else:
                eng.wait_ge(ready, per * (b + 1))
            if b >= 2:
                eng.wait_ge(self.xnT_ready, r * B + b - 1)
            for h in range(TT):
                for k in range(KD):
                    mm = eng.transpose(banks[b % 2][:, k * S + h * P:k * S + (h + 1) * P],
                                       src[:, b, h, k * P:(k + 1) * P], self.ident[:, :])
            mm.then_inc(self.turned, 1)

    def scalar(self, eng, r, banks, scale=None, after=None):
        for b in range(B):
            eng.wait_ge(self.turned, r * B + b + 1)
            if scale is None:
                mm = eng.activation(self.xnT[:, :, b * S:(b + 1) * S],
                                    banks[b % 2][:, :].rearrange("p (k t) -> p k t", k=KD), ACT.Copy)
            else:
                for k in range(KD):
                    mm = eng.activation(self.xnT[:, k, b * S:(b + 1) * S],
                                        banks[b % 2][:, k * S:(k + 1) * S], ACT.Copy, scale=scale[:, k:k + 1])
            mm.then_inc(self.xnT_ready, 1)
            if after is not None:
                after(eng, r, b)


def split_product(eng, out, terms, start=True, stop=True):
    parts = [(a, b) for sh, sl, mh, ml in terms for a, b in ((sh, mh), (sh, ml), (sl, mh))]
    for s, (a, b) in enumerate(parts):
        mm = eng.matmul(out, a, b, start=(start and s == 0), stop=(stop and s == len(parts) - 1), skip_group_check=True)
    return mm


class SplitX:

    def __init__(self, nm, sb, name):
        self.nm = nm
        self.high, self.low = (sb(f"{name}_x_{n}", [P, KD, T], F32R) for n in ("high", "low"))
        self.high_ready, self.low_ready = (nm.sems.new(f"{name}_x_{n}_ready") for n in ("high", "low"))

    def half(self, k, i):
        return tuple(x[:, k, i * HALF:(i + 1) * HALF] for x in (self.high, self.low))

    def scalar(self, eng, r, b):
        if b % 2:
            at = slice((b - 1) * S, (b + 1) * S)
            eng.wait_ge(self.nm.xnT_ready, r * B + b + 1)
            eng.activation(self.high[:, :, at], self.nm.xnT[:, :, at], ACT.Copy).then_inc(self.high_ready, 1)

    def vector(self, eng):
        for i in range(2):
            at = slice(i * HALF, (i + 1) * HALF)
            eng.wait_ge(self.high_ready, i + 1)
            eng.tensor_tensor(self.low[:, :, at], self.nm.xnT[:, :, at], self.high[:, :, at].bitcast(F32),
                              ALU.subtract).then_inc(self.low_ready, 1)


SPLIT = ("f_gate", "f_up", "f_down")


EARLY = (
    ("wq", [P, KD, D]), ("wk", [P, KD, D]), ("wv", [P, KD, D]), ("wo", [P, KD, D]), ("fsT", [P, B, KD, D]),
    ("f_gate", [P, KD, FF]), ("f_up", [P, KD, FF]), ("f_down", [P, FF // P, D]),
)
LATE = (
    ("ctxT", [P, B, S]), ("m_small", [P, KD + 8 * KE + KE * NS]),
    ("m_skip", [P, KD, EI]), ("m_in", [P, KD, EI]), ("m_d1", [P, KE, R]), ("m_d2", [P, EI]),
    ("m_bc", [P, KE, 2 * NS]), ("m_out", [P, KE, D]),
    ("x_qk", [P, 2 * P + 2]), ("router", [P, KD, NX + 1]),
)


def weights(ctx, nc, shapes):
    sb, _ = buffers(ctx, nc)
    return {n: (sb(n, shape), nc.alloc_semaphore(f"{n}_loaded")) for n, shape in shapes}


def load_weights(eng, w, dram):
    for name, (tile, sem) in w.items():
        eng.dma_start(tile[(slice(None),) * len(tile.shape)], dram[name]).then_inc(sem, 16)


def attention(nc, nm, w, split, dram):
    with ExitStack() as ctx:
        sb, ps = buffers(ctx, nc)
        masks = sb("a_part_masks", [P, 2])
        wide = {"wq": (split["f_gate_high"], split["f_gate_low"]), "wk": (split["f_up_high"], split["f_up_low"])}
        xcur = sb("a_x", [P, KD, S])
        x = SplitX(nm, sb, "a")
        PAIRS = HEADS // 2
        qS, kS = sb("a_q_parts", [P, PAIRS, S], F32R), sb("a_k_parts", [P, PAIRS, S], F32R)
        V1 = sb("a_v_ones", [P, TT, HEADS, HP])
        PR = sb("a_probs", [P, 2, 4, TT, S])
        PT = sb("a_probsT", [P, 2, TT, S])
        nmax = sb("a_neg_max", [P, HEADS, TT])
        aT = sb("a_outT", [P, S])
        rden = sb("a_rden", [P, TT, 4])
        aN = nm.XN[:, 0, :, :]
        xoT = sb("a_xoT", [P, KD, S])
        SC = [ps(f"a_scores{j}") for j in range(4)]
        PTp = [ps(f"a_probsT_ps{j}") for j in range(2)]
        M0, M1 = ps("a_m0"), ps("a_m1")
        wq_scaled = nm.sems.new("a_wq_scaled")
        xcur_ready = nm.sems.new("a_x_ready")
        masks_in, v_ones = nm.sems.new("a_masks_in"), nm.sems.new("a_v_ones")
        w_high, w_low = ({e: nm.sems.new(f"a_{e}_{n}") for e in ("wq", "wk")} for n in ("high", "low"))
        PROJ = 2 * HG
        (proj_ps, proj_high, proj_sb, v_sb, sc_ps, mx, ex) = counts(
            nm.sems, a_proj_ps=PROJ + 1, a_proj_high=PROJ, a_proj_sb=PROJ, a_v_sb=1, a_sc_ps=16, a_mx=16, a_ex=32)
        (pt_ps, pt_sb, pv_ps, aT_sb, at_ps, rd, nrm, xoT_ps, xoT_sb, o_ps, x_added) = counts(
            nm.sems, a_pt_ps=16, a_pt_sb=16, a_pv_ps=16, a_aT_sb=4, a_at_ps=4, a_rd=4, a_nrm=4, a_xoT_ps=1, a_xoT_sb=1,
            a_o_ps=1, a_x_added=1)
        block = ctx.enter_context(nc.Block())

        def once(name, k):
            return w[name][0][:, k, :].rearrange("p (h c) -> p h c", c=HD)[:, :, None, :].to_broadcast((P, HEADS, 4, HD))

        def four(tile, k):
            return tile[:, k, :].rearrange("p (h r c) -> p h r c", r=4, c=HD)

        def widen_low(eng, name):
            high, low = wide[name]
            for k in range(KD):
                eng.wait_ge(w_high[name], k + 1)
                eng.tensor_tensor(four(low, k), once(name, k), four(high, k).bitcast(F32), ALU.subtract).then_inc(w_low[name], 1)

        def batches(eng, body):
            with eng.Fori(0, B - 1) as i:
                body(i, True)
            body(B - 1, False)

        @block.sync
        def _(eng):
            for b in range(B):
                eng.dma_start(nm.X[:, b, :, :], dram["x"][b]).then_inc(nm.x_loaded[b], 16)
            eng.dma_start(masks[:, :], dram["part_masks"]).then_inc(masks_in, 16)
            load_weights(eng, w, dram)

        @block.gpsimd
        def _(eng):
            nm.sems.clear_stale(eng)
            eng.memset(nm.mhalf[:, :], -0.5).then_inc(nm.consts, 1)
            eng.memset(nm.half[:, :], 0.5).then_inc(nm.consts, 1)
            eng.memset(nm.ones[:, :], 1.0).then_inc(nm.consts, 1)
            eng.memset(nm.ident[:, :], 0.0).then_inc(nm.consts, 1)
            eng.wait_ge(nm.consts, 4)
            eng.affine_select(out=nm.ident[:, :], in_=nm.ident[:, :], compare_op=ALU.not_equal, fill=1.0,
                              base=0, pattern=[[-1, P]], channel_multiplier=1).then_inc(nm.consts, 1)
            eng.memset(V1[:, :, :, :], 1.0).then_inc(v_ones, 1)
            nm.gpsimd(eng, 0)
            widen_low(eng, "wq")
            eng.wait_ge(nm.xnT_ready, B)
            with eng.Fori(0, B - 1) as i:
                proj_ps.of(eng, i, PROJ)
                eng.tensor_copy(xcur[:, :, :], nm.xnT[:, :, bass.ds((i + 1) * S, S)]).then_inc(xcur_ready, 1)

        @block.tensor
        def _(eng):
            for c in (pt_ps, pv_ps, at_ps, xoT_ps, o_ps):
                c.credit(eng)
            nm.tensor(eng, 0, PTp)

            def project(b, n, bank):
                g, name = n // 2, ("wq", "wk")[n % 2]
                for a in range(2):
                    at = slice((2 * g + a) * P, (2 * g + a + 1) * P)
                    mm = split_product(eng, bank[:, a * S:(a + 1) * S], [
                        (wide[name][0][:, k, at], wide[name][1][:, k, at],
                         x.high[:, k, bass.ds(b * S, S)], x.low[:, k, bass.ds(b * S, S)]) for k in range(KD)])
                mm.then_inc(proj_ps.sem, 1)

            def project_v(x_of_batch):
                for h in range(TT):
                    for k in range(KD):
                        mm = eng.matmul(M0[:, h * D:(h + 1) * D], x_of_batch[:, k, h * P:(h + 1) * P], w["wv"][0][:, k, :],
                                        start=(k == 0), stop=(k == KD - 1))
                mm.then_inc(proj_ps.sem, 1)

            def scores(g, j):
                rows, pair = slice(4 * HD * (j % 2), 4 * HD * (j % 2 + 1)), 2 * g + j // 2
                for h in range(TT):
                    mm = eng.matmul(SC[j][:, h * S:(h + 1) * S], qS[rows, pair, h * P:(h + 1) * P],
                                    kS[rows, pair, :], start=True, stop=True)
                mm.then_inc(sc_ps.sem, 1)

            def turn(i, g, j, more):
                u = 4 * g + j
                ex.of(eng, i, 8 * g + 2 * j + 1)
                if g < HG - 1:
                    proj_sb.of(eng, i, 2 * g + 3)
                    scores(g + 1, j)
                elif more:
                    proj_sb.of(eng, i + 1, 1)
                    scores(0, j)
                (pt_sb.now(eng, i, u - 2) if u >= 2 else pt_sb.before(eng, i, 14 + u))
                for c in range(TT):
                    for h in range(TT):
                        mm = eng.transpose(PTp[j % 2][:, c * S + h * P:c * S + (h + 1) * P],
                                           PR[:, g % 2, j, h, c * P:(c + 1) * P], nm.ident[:, :])
                mm.then_inc(pt_ps.sem, 1)

            def values(i, g, j):
                pt_sb.now(eng, i, 4 * g + j)
                if j == 0:
                    (nrm.now(eng, i, g - 1) if g else x_added.before(eng, i, 0))
                if g == 0 and j == 0:
                    v_sb.of(eng, i, 0)
                for c in range(TT):
                    mm = eng.matmul(M1[HP * j:HP * (j + 1), 0:S], V1[:, c, 4 * g + j, :], PT[:, j % 2, c, :],
                                    start=(c == 0), stop=(c == TT - 1))
                mm.then_inc(pv_ps.sem, 1)

            def turn_back(i, g):
                aT_sb.now(eng, i, g)
                for h in range(TT):
                    mm = eng.transpose(M1[:, h * P:(h + 1) * P], aT[:, h * P:(h + 1) * P], nm.ident[:, :])
                mm.then_inc(at_ps.sem, 1)

            banks = (M0, M1, *PTp)
            eng.wait_ge(x.low_ready, 1)
            eng.wait_ge(w_low["wq"], KD)
            eng.wait_ge(w_low["wk"], KD)
            for n in range(PROJ):
                if n >= len(banks):
                    proj_sb.of(eng, 0, n - len(banks))
                elif n == 2:
                    eng.wait_ge(nm.xnT_ready, B)
                project(0, n, banks[n % len(banks)])
                if n == 3:
                    proj_sb.of(eng, 0, 1)
                    for j in range(4):
                        scores(0, j)
            proj_sb.of(eng, 0, PROJ - len(banks))
            eng.wait_ge(w["wv"][1], 16)
            project_v(nm.xnT)
            proj_sb.of(eng, 0, PROJ - 1)
            eng.wait_ge(x.low_ready, 2)

            def batch(i, more):
                def next_projection(n):
                    if more:
                        (proj_sb.of(eng, i + 1, n - 1) if n else v_sb.of(eng, i, 0))
                        project(i + 1, n, M0)

                for g in range(HG):
                    turn(i, g, 0, more)
                    if g:
                        turn_back(i, g - 1)
                    next_projection(2 * g)
                    turn(i, g, 1, more)
                    values(i, g, 0)
                    turn(i, g, 2, more)
                    values(i, g, 1)
                    turn(i, g, 3, more)
                    next_projection(2 * g + 1)
                    values(i, g, 2)
                    values(i, g, 3)
                if more:
                    proj_sb.of(eng, i + 1, PROJ - 1)
                    eng.wait_ge(xcur_ready, i + 1)
                    project_v(xcur)
                turn_back(i, HG - 1)
                nrm.now(eng, i, HG - 1)
                for h in range(TT):
                    for k in range(KD):
                        mm = eng.transpose(M1[:, k * S + h * P:k * S + (h + 1) * P], aN[:, h, k * P:(k + 1) * P],
                                           nm.ident[:, :])
                mm.then_inc(xoT_ps.sem, 1)
                xoT_sb.now(eng, i, 0)
                for h in range(TT):
                    for k in range(KD):
                        mm = eng.matmul(M1[:, h * D:(h + 1) * D], xoT[:, k, h * P:(h + 1) * P], w["wo"][0][:, k, :],
                                        start=(k == 0), stop=(k == KD - 1))
                mm.then_inc(o_ps.sem, 1)

            eng.wait_ge(w["wo"][1], 16)
            batches(eng, batch)

        @block.vector
        def _(eng):
            for c in (pt_sb, rd, nrm, x_added):
                c.credit(eng)
            nm.vector(eng, 0)
            widen_low(eng, "wk")
            x.vector(eng)
            eng.wait_ge(masks_in, 16)

            def parts(b, n, bank):
                proj_high.of(eng, b, n)
                tile = (qS, kS)[n % 2][:, n // 2 * 2:n // 2 * 2 + 2, :]
                eng.scalar_tensor_tensor(tile, tile.bitcast(F32), masks[:, n % 2:n % 2 + 1],
                                         bank[:, :].rearrange("p (a t) -> p a t", a=2), ALU.mult, ALU.add).then_inc(proj_sb.sem, 1)

            def maxima(b, g, j):
                h4 = 4 * g + j
                sc_ps.of(eng, b, h4)
                eng.tensor_reduce(nmax[:, h4, :], SC[j][:, :].rearrange("p (h t) -> p h t", h=TT),
                                  AX.X, ALU.max, negate=True).then_inc(mx.sem, 1)

            def keep_probsT(i, g, j):
                u = 4 * g + j
                pt_ps.now(eng, i, u)
                (pv_ps.now(eng, i, u - 2) if u >= 2 else pv_ps.before(eng, i, 14 + u))
                eng.tensor_copy(PT[:, j % 2, :, :], PTp[j % 2][:, :].rearrange("p (c t) -> p c t", c=TT)).then_inc(pt_sb.sem, 1)

            def normalise(i, g):
                at_ps.now(eng, i, g)
                view = M1[:, 0:TT * P].rearrange("p (h j c) -> p h j c", h=TT, j=4)
                (nrm.now(eng, i, g - 1) if g else nrm.before(eng, i, HG - 1))
                eng.reciprocal(rden[:, :, :], view[:, :, :, HD]).then_inc(rd.sem, 1)
                rd.now(eng, i, g)
                xoT_ps.before(eng, i, 0)
                for h in range(TT):
                    op = eng.tensor_tensor(
                        aN[:, h, g * 4 * HD:(g + 1) * 4 * HD].rearrange("p (j c) -> p j c", j=4),
                        view[:, h, :, 0:HD], rden[:, h, :, None].to_broadcast((P, 4, HD)), ALU.mult)
                op.then_inc(nrm.sem, 1)

            banks = (M0, M1, *PTp)
            for n in range(PROJ):
                parts(0, n, banks[n % len(banks)])
                if n == 3:
                    for j in range(4):
                        maxima(0, 0, j)

            def batch(i, more):
                for g in range(HG):
                    for j in range(4):
                        if g < HG - 1:
                            maxima(i, g + 1, j)
                        elif more:
                            maxima(i + 1, 0, j)
                        keep_probsT(i, g, j)
                        if j == 0 and g:
                            normalise(i, g - 1)
                        if j % 2 and more:
                            parts(i + 1, 2 * g + j // 2, M0)
                normalise(i, HG - 1)
                o_ps.now(eng, i, 0)
                eng.tensor_tensor(nm.X[:, i, :, :], nm.X[:, i, :, :],
                                  M1[:, :].rearrange("p (h f) -> p h f", h=TT), ALU.add).then_inc(x_added.sem, 1)
                x_added.now(eng, i, 0)
                nm.statistics(eng, 1, i)

            batches(eng, batch)

        @block.scalar
        def _(eng):
            for c in (aT_sb, xoT_sb):
                c.credit(eng)
            wq, loaded = w["wq"]
            eng.wait_ge(loaded, 16)
            eng.activation(wq[:, :, :], wq[:, :, :], ACT.Copy, scale=HD ** -0.5).then_inc(wq_scaled, 1)
            eng.wait_ge(wq_scaled, 1)
            for name in ("wq", "wk"):
                eng.wait_ge(w[name][1], 16)
                for k in range(KD):
                    eng.activation(four(wide[name][0], k), once(name, k), ACT.Copy).then_inc(w_high[name], 1)
            nm.scalar(eng, 0, PTp, after=x.scalar)

            def high(b, n, bank, free):
                proj_ps.of(eng, b, n)
                free()
                eng.activation((qS, kS)[n % 2][:, n // 2 * 2:n // 2 * 2 + 2, :],
                               bank[:, :].rearrange("p (a t) -> p a t", a=2), ACT.Copy).then_inc(proj_high.sem, 1)

            def keep_v(b, free):
                proj_ps.of(eng, b, PROJ)
                free()
                eng.activation(V1[:, :, :, 0:HD], M0[:, :].rearrange("p (h n c) -> p h n c", h=TT, c=HD),
                               ACT.Copy).then_inc(v_sb.sem, 1)

            def exps(b, g, j, free):
                mx.of(eng, b, 4 * g + j)
                free(j)
                for h in range(TT):
                    eng.activation(PR[:, g % 2, j, h, :], SC[j][:, h * S:(h + 1) * S], ACT.Exp,
                                   bias=nmax[:, 4 * g + j, h:h + 1]).then_inc(ex.sem, 1)

            def keep_outT(i, g):
                pv_ps.now(eng, i, 4 * g + 3)
                (at_ps.now(eng, i, g - 1) if g else at_ps.before(eng, i, HG - 1))
                eng.activation(aT[:, :], M1[:, 0:S], ACT.Copy).then_inc(aT_sb.sem, 1)

            banks = (M0, M1, *PTp)
            for n in range(PROJ):
                high(0, n, banks[n % len(banks)], lambda: None)
                if n == 3:
                    for j in range(4):
                        exps(0, 0, j, lambda j: None)
            eng.wait_ge(v_ones, 1)
            keep_v(0, lambda: None)

            def batch(i, more):
                for g in range(HG):
                    used = lambda: sc_ps.of(eng, i, 4 * g + 3)
                    turned = lambda j: (pt_ps.now(eng, i, 4 * (g - 1) + j) if g else pt_ps.before(eng, i, 12 + j))
                    if more:
                        high(i + 1, 2 * g, M0, used)
                    for j in range(4):
                        if g < HG - 1:
                            exps(i, g + 1, j, turned)
                        elif more:
                            exps(i + 1, 0, j, turned)
                        if j == 2 and more:
                            high(i + 1, 2 * g + 1, M0, used)
                    keep_outT(i, g)
                if more:
                    keep_v(i + 1, lambda: pv_ps.now(eng, i, 15))
                xoT_ps.now(eng, i, 0)
                o_ps.before(eng, i, 0)
                eng.activation(xoT[:, :, :], M1[:, :].rearrange("p (k t) -> p k t", k=KD), ACT.Copy).then_inc(xoT_sb.sem, 1)

            batches(eng, batch)


def quantised(nc, nm, w, split, dram):
    with ExitStack() as ctx:
        sb, ps = buffers(ctx, nc)
        NL = 2
        lane = lambda name, *shape, dt=F32: sb(f"q_{name}", [P, NL, *shape], dt)
        am, amf = lane("amax", 5), lane("amax_floor", 5)
        rw = lane("recip_w", 3)
        ratio, root = lane("ratio", 2), lane("root", 2)
        s1, rs1 = lane("s1", 2), lane("rs1", 2)
        OP = lane("scaled", 4, S)
        ra, sc, rsc = lane("row_amax", 4), lane("scale", 4), lane("rscale", 4)
        Q1, Q2 = lane("shifted", 4, S), lane("clipped", 4, S)
        QT = lane("turned", 4, S, dt=BF16)
        diag = lane("diag", 2, P)
        XS = lane("x_scale_row", S)
        gd, ud, sg, aa = (lane(n, S) for n in ("gate", "up", "silu", "act"))
        am2, amf2 = lane("amax2", 1), lane("amax2_floor", 1)
        ratio2, root2 = lane("ratio2", 1), lane("root2", 1)
        s2, rs2 = lane("s2", 1), lane("rs2", 1)
        OP2 = lane("scaled2", 2, S)
        ra2, sc2, rsc2 = lane("row_amax2", 4), lane("scale2", 4), lane("rscale2", 4)
        Q3, Q4 = lane("shifted2", 4, P), lane("clipped2", 4, P)
        QT2 = lane("turned2", 4, P, dt=BF16)
        diag2 = lane("diag2", 2, P)
        WS = lane("w_scale_row", S)
        yd = lane("y", TT, D)
        K = [[ps(f"q_k{l}{n}") for n in range(2)] for l in range(NL)]
        RW = [ps(f"q_rows{l}") for l in range(NL)]
        (am_r, amf_r, rw_r, rt_r, root_r, s_r, rs_r, op_r, ra_r, sc_r, rsc_r, q2_r, dg_r, gd_r, ud_r, aa_r,
         am2_r, amf2_r, rt2_r, s2_r, rs2_r, op2_r, ra2_r, sc2_r, rsc2_r, q4_r, dg2_r, y_r, x_r,
         root2_r, tp_r, tb_r, xsr_r, gu_r, t2_r, b2_r, wsr_r, yy_r,
         q1_r, qt_r, xs_r, sg_r, q3_r, qt2_r, ws_r) = cs = counts(
            nm.sems, NL, q_am=3, q_amf=1, q_rw=1, q_rt=1, q_root_r=1, q_s=1, q_rs=1, q_op=4, q_ra=2, q_sc=1, q_rsc=1,
            q_q2=1, q_dg=2, q_gd=1, q_ud=1, q_aa=1, q_am2=1, q_amf2=1, q_rt2=1, q_s2r=1, q_rs2r=1, q_op2=2,
            q_ra2=1, q_sc2=1, q_rsc2=1, q_q4=1, q_dg2=2, q_yr=2, q_xr=1, q_root2r=1, q_tp_r=2, q_tb_r=2, q_xsr=1,
            q_gu_r=2, q_t2r=1, q_b2r=1, q_wsr=1, q_yyr=1, q_q1=4, q_qt=2, q_xs=1, q_sgr=1, q_q3=4, q_qt2=1, q_wsr2=1)
        w_high = {name: nm.sems.new(f"q_{name}_high") for name in SPLIT}
        pool = [root_r, root2_r]
        pe = [tp_r, tb_r, xsr_r, gu_r, t2_r, b2_r, wsr_r, yy_r]
        act = [q1_r, qt_r, xs_r, sg_r, q3_r, qt2_r, ws_r]
        PASSES = B // NL
        lanes = range(NL)
        block = ctx.enter_context(nc.Block())

        @block.gpsimd
        def _(eng):
            for c in pool:
                c.credit(eng)
            for name in SPLIT:
                eng.wait_ge(w[name][1], 16)
            nm.gpsimd(eng, 1)

            def split_share(i, name):
                tiles = w[name][0], split[f"{name}_high"], split[f"{name}_low"]
                if name == "f_down":
                    n = FF // P // PASSES
                    tile, high, low = (a[:, bass.ds(i * n, n), :] for a in tiles)
                else:
                    n = FF // PASSES
                    tile, high, low = (a[:, :, bass.ds(i * n, n)] for a in tiles)
                eng.tensor_copy(high, tile).then_inc(w_high[name], 1)
                eng.wait_ge(w_high[name], i + 1)
                eng.tensor_tensor(low, tile, high.bitcast(F32), ALU.subtract)

            with fresh_addresses(nc), eng.Fori(0, PASSES) as i:
                for l in lanes:
                    rt_r.now(eng, i, 0, l)
                    eng.tensor_tensor(root[:, l, :], ratio[:, l, :], nm.half[:, 0:2], ALU.pow).then_inc(root_r.sem, 1)
                split_share(i, "f_gate")
                split_share(i, "f_up")
                for l in lanes:
                    rt2_r.now(eng, i, 0, l)
                    eng.tensor_tensor(root2[:, l, :], ratio2[:, l, :], nm.half[:, 0:1], ALU.pow).then_inc(root2_r.sem, 1)
                split_share(i, "f_down")
            nm.sems.clear_stale(eng)

        @block.tensor
        def _(eng):
            for c in pe:
                c.credit(eng)
            nm.tensor(eng, 1, K[0])
            eng.wait_ge(nm.xnT_ready, 2 * B)
            with eng.Fori(0, PASSES) as i:
                for l in lanes:
                    for o in range(2):
                        op_r.now(eng, i, 2 * o + 1, l)
                        (y_r.before(eng, i, 1, l) if o else qt2_r.before(eng, i, 0, l))
                        for r in range(2):
                            for k in range(KD):
                                mm = eng.transpose(K[l][o][:, r * D + k * P:r * D + (k + 1) * P],
                                                   OP[:, l, 2 * o + k, r * P:(r + 1) * P], nm.ident[:, :])
                        mm.then_inc(tp_r.sem, 1)
                for l in lanes:
                    dg_r.now(eng, i, 1, l)
                    ws_r.before(eng, i, 0, l)
                    for r in range(2):
                        mm = eng.matmul(RW[l][:, r * P:(r + 1) * P], nm.ones[:, :], diag[:, l, r, :], start=True, stop=True)
                    mm.then_inc(xsr_r.sem, 1)
                for l in lanes:
                    q2_r.now(eng, i, 0, l)
                    for o in range(2):
                        for r in range(2):
                            for k in range(KD):
                                mm = eng.transpose(K[l][o][:, k * S + r * P:k * S + (r + 1) * P],
                                                   Q2[:, l, 2 * o + r, k * P:(k + 1) * P], nm.ident[:, :])
                        mm.then_inc(tb_r.sem, 1)
                for l in lanes:
                    qt_r.now(eng, i, 1, l)
                    for o in range(2):
                        for k in range(KD):
                            mm = eng.matmul(K[l][1][:, o * S:(o + 1) * S], QT[:, l, 2 + k, o * P:(o + 1) * P], QT[:, l, k, :],
                                            start=(k == 0), stop=(k == KD - 1))
                        mm.then_inc(gu_r.sem, 1)
                for l in lanes:
                    op2_r.now(eng, i, 1, l)
                    for o in range(2):
                        for r in range(2):
                            mm = eng.transpose(K[l][0][:, (2 * o + r) * P:(2 * o + r + 1) * P], OP2[:, l, o, r * P:(r + 1) * P],
                                               nm.ident[:, :])
                    mm.then_inc(t2_r.sem, 1)
                for l in lanes:
                    dg2_r.now(eng, i, 1, l)
                    xs_r.now(eng, i, 0, l)
                    for r in range(2):
                        mm = eng.matmul(RW[l][:, S + r * P:S + (r + 1) * P], nm.ones[:, :], diag2[:, l, r, :],
                                        start=True, stop=True)
                    mm.then_inc(wsr_r.sem, 1)
                for l in lanes:
                    q4_r.now(eng, i, 0, l)
                    for r in range(4):
                        mm = eng.transpose(K[l][0][:, r * P:(r + 1) * P], Q4[:, l, r, :], nm.ident[:, :])
                    mm.then_inc(b2_r.sem, 1)
                for l in lanes:
                    qt2_r.now(eng, i, 0, l)
                    ud_r.now(eng, i, 0, l)
                    for h in range(TT):
                        mm = eng.matmul(K[l][1][:, h * D:(h + 1) * D], QT2[:, l, h, :], QT2[:, l, 2:4, :], start=True, stop=True)
                    mm.then_inc(yy_r.sem, 1)

        @block.scalar
        def _(eng):
            for c in act:
                c.credit(eng)
            nm.scalar(eng, 1, K[0])
            nm.load_table(eng, ACT.Silu)
            with eng.Fori(0, PASSES) as i:
                for l in lanes:
                    rsc_r.now(eng, i, 0, l)
                    q2_r.before(eng, i, 0, l)
                    for r in range(4):
                        tp_r.now(eng, i, r // 2, l)
                        eng.activation(Q1[:, l, r, :], K[l][r // 2][:, r % 2 * D:(r % 2 + 1) * D], ACT.Copy,
                                       bias=MAGIC, scale=rsc[:, l, r:r + 1]).then_inc(q1_r.sem, 1)
                for l in lanes:
                    xsr_r.now(eng, i, 0, l)
                    ud_r.before(eng, i, 0, l)
                    eng.activation(XS[:, l, :], RW[l][:, 0:S], ACT.Copy).then_inc(xs_r.sem, 1)
                for l in lanes:
                    gu_r.before(eng, i, 1, l)
                    for o in range(2):
                        tb_r.now(eng, i, o, l)
                        eng.activation(QT[:, l, 2 * o:2 * o + 2, :], K[l][o][:, :].rearrange("p (k t) -> p k t", k=2),
                                       ACT.Copy, bias=-MAGIC).then_inc(qt_r.sem, 1)
                for l in lanes:
                    gd_r.now(eng, i, 0, l)
                    aa_r.before(eng, i, 0, l)
                    eng.activation(sg[:, l, :], gd[:, l, :], ACT.Silu).then_inc(sg_r.sem, 1)
                for l in lanes:
                    rsc2_r.now(eng, i, 0, l)
                    t2_r.now(eng, i, 0, l)
                    q4_r.before(eng, i, 0, l)
                    for r in range(4):
                        eng.activation(Q3[:, l, r, :], K[l][0][:, r * P:(r + 1) * P], ACT.Copy, bias=MAGIC,
                                       scale=rsc2[:, l, r:r + 1]).then_inc(q3_r.sem, 1)
                for l in lanes:
                    wsr_r.now(eng, i, 0, l)
                    y_r.before(eng, i, 1, l)
                    eng.activation(WS[:, l, :], RW[l][:, S:2 * S], ACT.Copy).then_inc(ws_r.sem, 1)
                for l in lanes:
                    b2_r.now(eng, i, 0, l)
                    yy_r.before(eng, i, 0, l)
                    eng.activation(QT2[:, l, :, :], K[l][0][:, :].rearrange("p (r t) -> p r t", r=4), ACT.Copy,
                                   bias=-MAGIC).then_inc(qt2_r.sem, 1)

        @block.vector
        def _(eng):
            for c in cs:
                if c not in pool + pe + act:
                    c.credit(eng)
            nm.vector(eng, 1)
            eng.wait_ge(nm.xnT_ready, 2 * B)
            eng.wait_ge(w["fsT"][1], 16)
            eng.wait_ge(w["ctxT"][1], 16)
            fsT, ctxT = w["fsT"][0], w["ctxT"][0]
            with eng.Fori(0, PASSES) as i:
                for l in lanes:
                    b = NL * i + l
                    amf_r.before(eng, i, 0, l)
                    for at, channels in ((slice(0, 2), nm.xnT[:, :, bass.ds(b * S, S)]), (slice(2, 4), fsT[:, b, :, :]),
                                         (slice(4, 5), ctxT[:, b, :])):
                        eng.tensor_reduce(am[:, l, at], channels, AX.X, ALU.max, apply_absolute_value=True).then_inc(am_r.sem, 1)
                for l in lanes:
                    am_r.now(eng, i, 2, l)
                    rt2_r.before(eng, i, 0, l)
                    eng.tensor_scalar(amf[:, l, :], am[:, l, :], EPS_Q, None, ALU.max).then_inc(amf_r.sem, 1)
                for l in lanes:
                    amf_r.now(eng, i, 0, l)
                    eng.reciprocal(rw[:, l, :], amf[:, l, 2:5]).then_inc(rw_r.sem, 1)
                for l in lanes:
                    rw_r.now(eng, i, 0, l)
                    root_r.before(eng, i, 0, l)
                    eng.tensor_tensor(ratio[:, l, :], amf[:, l, 0:2], rw[:, l, 0:2], ALU.mult).then_inc(rt_r.sem, 1)
                for l in lanes:
                    root_r.now(eng, i, 0, l)
                    op_r.before(eng, i, 3, l)
                    eng.tensor_scalar(s1[:, l, :], root[:, l, :], EPS_Q, None, ALU.max).then_inc(s_r.sem, 1)
                for l in lanes:
                    s_r.now(eng, i, 0, l)
                    eng.reciprocal(rs1[:, l, :], s1[:, l, :]).then_inc(rs_r.sem, 1)
                for l in lanes:
                    b = NL * i + l
                    rs_r.now(eng, i, 0, l)
                    tp_r.before(eng, i, 1, l)
                    for k in range(KD):
                        eng.tensor_scalar(OP[:, l, k, :], nm.xnT[:, k, bass.ds(b * S, S)], rs1[:, l, k:k + 1], None,
                                          ALU.mult).then_inc(op_r.sem, 1)
                    for k in range(KD):
                        eng.tensor_scalar(OP[:, l, 2 + k, :], fsT[:, b, k, :], s1[:, l, k:k + 1], None,
                                          ALU.mult).then_inc(op_r.sem, 1)
                for l in lanes:
                    sc_r.before(eng, i, 0, l)
                    for o in range(2):
                        tp_r.now(eng, i, o, l)
                        eng.tensor_reduce(ra[:, l, 2 * o:2 * o + 2], K[l][o][:, :].rearrange("p (r f) -> p r f", r=2),
                                          AX.X, ALU.max, apply_absolute_value=True).then_inc(ra_r.sem, 1)
                for l in lanes:
                    ra_r.now(eng, i, 1, l)
                    dg_r.before(eng, i, 1, l)
                    ud_r.before(eng, i, 0, l)
                    eng.tensor_scalar(sc[:, l, :], ra[:, l, :], EPS_Q, 1.0 / QMAX, ALU.max, ALU.mult).then_inc(sc_r.sem, 1)
                for l in lanes:
                    sc_r.now(eng, i, 0, l)
                    q1_r.before(eng, i, 3, l)
                    eng.reciprocal(rsc[:, l, :], sc[:, l, :]).then_inc(rsc_r.sem, 1)
                for l in lanes:
                    xsr_r.before(eng, i, 0, l)
                    for r in range(2):
                        eng.tensor_scalar(diag[:, l, r, :], nm.ident[:, :], sc[:, l, r:r + 1], None, ALU.mult).then_inc(dg_r.sem, 1)
                for l in lanes:
                    q1_r.now(eng, i, 3, l)
                    tb_r.before(eng, i, 1, l)
                    eng.tensor_scalar(Q2[:, l, :, :], Q1[:, l, :, :], MAGIC + QMAX, MAGIC - QMAX, ALU.min, ALU.max).then_inc(q2_r.sem, 1)
                for l in lanes:
                    xs_r.now(eng, i, 0, l)
                    gu_r.now(eng, i, 1, l)
                    sg_r.before(eng, i, 0, l)
                    aa_r.before(eng, i, 0, l)
                    eng.scalar_tensor_tensor(gd[:, l, :], K[l][1][:, 0:S], sc[:, l, 2:3], XS[:, l, :],
                                             ALU.mult, ALU.mult).then_inc(gd_r.sem, 1)
                    eng.scalar_tensor_tensor(ud[:, l, :], K[l][1][:, S:2 * S], sc[:, l, 3:4], XS[:, l, :],
                                             ALU.mult, ALU.mult).then_inc(ud_r.sem, 1)
                for l in lanes:
                    sg_r.now(eng, i, 0, l)
                    ud_r.now(eng, i, 0, l)
                    op2_r.before(eng, i, 1, l)
                    am2_r.before(eng, i, 0, l)
                    eng.tensor_tensor(aa[:, l, :], sg[:, l, :], ud[:, l, :], ALU.mult).then_inc(aa_r.sem, 1)
                for l in lanes:
                    aa_r.now(eng, i, 0, l)
                    amf2_r.before(eng, i, 0, l)
                    eng.tensor_reduce(am2[:, l, :], aa[:, l, :], AX.X, ALU.max, apply_absolute_value=True).then_inc(am2_r.sem, 1)
                for l in lanes:
                    am2_r.now(eng, i, 0, l)
                    eng.tensor_scalar(amf2[:, l, :], am2[:, l, :], EPS_Q, None, ALU.max).then_inc(amf2_r.sem, 1)
                for l in lanes:
                    amf2_r.now(eng, i, 0, l)
                    root2_r.before(eng, i, 0, l)
                    eng.tensor_tensor(ratio2[:, l, :], amf2[:, l, :], rw[:, l, 2:3], ALU.mult).then_inc(rt2_r.sem, 1)
                for l in lanes:
                    root2_r.now(eng, i, 0, l)
                    op2_r.before(eng, i, 1, l)
                    eng.tensor_scalar(s2[:, l, :], root2[:, l, :], EPS_Q, None, ALU.max).then_inc(s2_r.sem, 1)
                for l in lanes:
                    s2_r.now(eng, i, 0, l)
                    eng.reciprocal(rs2[:, l, :], s2[:, l, :]).then_inc(rs2_r.sem, 1)
                for l in lanes:
                    rs2_r.now(eng, i, 0, l)
                    t2_r.before(eng, i, 0, l)
                    eng.tensor_scalar(OP2[:, l, 0, :], aa[:, l, :], rs2[:, l, 0:1], None, ALU.mult).then_inc(op2_r.sem, 1)
                    eng.tensor_scalar(OP2[:, l, 1, :], ctxT[:, NL * i + l, :], s2[:, l, 0:1], None, ALU.mult).then_inc(op2_r.sem, 1)
                for l in lanes:
                    t2_r.now(eng, i, 0, l)
                    sc2_r.before(eng, i, 0, l)
                    eng.tensor_reduce(ra2[:, l, :], K[l][0][:, :].rearrange("p (r f) -> p r f", r=4), AX.X, ALU.max,
                                      apply_absolute_value=True).then_inc(ra2_r.sem, 1)
                for l in lanes:
                    ra2_r.now(eng, i, 0, l)
                    y_r.before(eng, i, 1, l)
                    eng.tensor_scalar(sc2[:, l, :], ra2[:, l, :], EPS_Q, 1.0 / QMAX, ALU.max, ALU.mult).then_inc(sc2_r.sem, 1)
                for l in lanes:
                    sc2_r.now(eng, i, 0, l)
                    q3_r.before(eng, i, 3, l)
                    eng.reciprocal(rsc2[:, l, :], sc2[:, l, :]).then_inc(rsc2_r.sem, 1)
                for l in lanes:
                    wsr_r.before(eng, i, 0, l)
                    for r in range(2):
                        eng.tensor_scalar(diag2[:, l, r, :], nm.ident[:, :], sc2[:, l, 2 + r:3 + r], None,
                                          ALU.mult).then_inc(dg2_r.sem, 1)
                for l in lanes:
                    q3_r.now(eng, i, 3, l)
                    b2_r.before(eng, i, 0, l)
                    eng.tensor_scalar(Q4[:, l, :, :], Q3[:, l, :, :], MAGIC + QMAX, MAGIC - QMAX, ALU.min, ALU.max).then_inc(q4_r.sem, 1)
                for l in lanes:
                    yy_r.now(eng, i, 0, l)
                    ws_r.now(eng, i, 0, l)
                    x_r.before(eng, i, 0, l)
                    for h in range(TT):
                        eng.scalar_tensor_tensor(yd[:, l, h, :], K[l][1][:, h * D:(h + 1) * D], sc2[:, l, h:h + 1], WS[:, l, :],
                                                 ALU.mult, ALU.mult).then_inc(y_r.sem, 1)
                for l in lanes:
                    b = NL * i + l
                    y_r.now(eng, i, 1, l)
                    eng.tensor_tensor(nm.X[:, b, :, :], nm.X[:, b, :, :], yd[:, l, :, :], ALU.add).then_inc(x_r.sem, 1)
                    x_r.now(eng, i, 0, l)
                    nm.statistics(eng, 2, b)


def sparse(nc, nm, w, dram):
    with ExitStack() as ctx:
        sb, ps = buffers(ctx, nc)
        H, A = sb("s_h", [P, 4, HALF]), sb("s_abs", [P, 4, HALF])
        SG = sb("s_silu", [P, 2, HALF])
        C = sb("s_wins", [P, 6, HALF], BF16)
        W1 = sb("s_sums1", [P, 4, HALF], BF16)
        W2 = sb("s_sums2", [P, 4, HALF], BF16)
        HS = sb("s_kept", [P, 4, HALF])
        HH, HL = (sb(f"s_kept_{n}", [P, 2, 4, HALF], F32R) for n in ("high", "low"))
        x = SplitX(nm, sb, "s")
        NB = 3
        GP, UP = [ps(f"s_gate{n}") for n in range(NB)], [ps(f"s_up{n}") for n in range(NB)]
        OUT = [ps(f"s_out{n}") for n in range(2)]
        NT, STEPS = HALF // P, 4
        g_ps, u_ps, sg_r, ab_r, h_r, c_r, w1_r, w2_r, hs_r, hh_r, hl_r, o_ps, x_added = (
            nm.sems.new(f"s_{n}") for n in ("gate_ps", "up_ps", "silu_r", "abs_r", "h_r", "wins_r", "sums1_r", "sums2_r",
                                            "kept_r", "high_r", "low_r", "down", "x_added"))
        block = ctx.enter_context(nc.Block())

        @block.gpsimd
        def _(eng):
            nm.gpsimd(eng, 2)
            nm.sems.clear_stale(eng)
            for q in range(STEPS):
                for j in range(4):
                    eng.wait_ge(hh_r, 4 * q + j + 1)
                    if q >= 2:
                        eng.wait_ge(o_ps, q - 1)
                    eng.tensor_tensor(HL[:, q % 2, j, :], HS[:, j, :], HH[:, q % 2, j, :].bitcast(F32),
                                      ALU.subtract).then_inc(hl_r, 1)

        @block.tensor
        def _(eng):
            nm.tensor(eng, 2, OUT)

            def gates(q, j):
                u, at = 4 * q + j, (4 * (q % 2) + j) * P
                if u >= NB:
                    eng.wait_ge(sg_r, u - NB + 1)
                    eng.wait_ge(h_r, u - NB + 1)
                for bank, name, c in ((GP[u % NB], "f_gate", g_ps), (UP[u % NB], "f_up", u_ps)):
                    split_product(eng, bank[:, :], [
                        (w[name + "_high"][:, k, at:at + P], w[name + "_low"][:, k, at:at + P],
                         *x.half(k, q // 2)) for k in range(KD)]).then_inc(c, 1)

            def downs(q):
                for j in range(4):
                    eng.wait_ge(hl_r, 4 * q + j + 1)
                    if q == 0 and j == 0:
                        eng.wait_ge(nm.xnT_ready, 3 * B)
                    if q == 2 and j == 0:
                        eng.wait_ge(x_added, 2)
                    n = 4 * (q % 2) + j
                    for t in range(NT):
                        rows = slice(t * P, (t + 1) * P)
                        mm = split_product(eng, OUT[t // 2][:, (t % 2) * D:(t % 2 + 1) * D], [
                            (HH[:, q % 2, j, rows], HL[:, q % 2, j, rows], w["f_down_high"][:, n, :], w["f_down_low"][:, n, :])],
                            start=(n == 0 and t % 2 == 0), stop=(n == 7))
                mm.then_inc(o_ps, 1)

            for q in range(STEPS):
                eng.wait_ge(x.low_ready, q // 2 + 1)
                for j in range(4):
                    gates(q, j)
                if q:
                    downs(q - 1)
            downs(STEPS - 1)

        @block.scalar
        def _(eng):
            nm.scalar(eng, 2, OUT, after=x.scalar)

            def highs(q):
                for j in range(4):
                    eng.wait_ge(hs_r, 4 * q + j + 1)
                    if q >= 2:
                        eng.wait_ge(o_ps, q - 1)
                    eng.activation(HH[:, q % 2, j, :], HS[:, j, :], ACT.Copy).then_inc(hh_r, 1)

            for q in range(STEPS):
                for j in range(4):
                    u = 4 * q + j
                    eng.wait_ge(g_ps, u + 1)
                    if u >= 2:
                        eng.wait_ge(h_r, u - 1)
                    eng.activation(SG[:, u % 2, :], GP[u % NB][:, :], ACT.Silu).then_inc(sg_r, 1)
                    if q and j == 0:
                        highs(q - 1)
                    eng.wait_ge(h_r, u + 1)
                    if q:
                        eng.wait_ge(c_r, 6 * q)
                    eng.activation(A[:, j, :], H[:, j, :], ACT.Abs).then_inc(ab_r, 1)
            highs(STEPS - 1)

        @block.vector
        def _(eng):
            nm.vector(eng, 2)
            x.vector(eng)

            def wins(q, a, b, n):
                eng.wait_ge(ab_r, 4 * q + b + 1)
                if q:
                    eng.wait_ge(w2_r, 4 * q)
                eng.tensor_tensor(C[:, n, :], A[:, a, :], A[:, b, :], ALU.is_ge).then_inc(c_r, 1)

            def add(i):
                eng.wait_ge(o_ps, 2 * i + 2)
                for n in range(2):
                    b = 2 * i + n
                    eng.tensor_tensor(nm.X[:, b, :, :], nm.X[:, b, :, :], OUT[n][:, :].rearrange("p (h f) -> p h f", h=TT),
                                      ALU.add).then_inc(x_added, 1)

            def statistics(i):
                for b in (2 * i, 2 * i + 1):
                    eng.wait_ge(x_added, b + 1)
                    nm.statistics(eng, 3, b)

            for q in range(STEPS):
                for j in range(4):
                    u = 4 * q + j
                    eng.wait_ge(sg_r, u + 1)
                    eng.wait_ge(u_ps, u + 1)
                    if q:
                        eng.wait_ge(hs_r, u - 3)
                    eng.tensor_tensor(H[:, j, :], SG[:, u % 2, :], UP[u % NB][:, :], ALU.mult).then_inc(h_r, 1)
                    if q == 3 and j == 1:
                        add(0)
                    for a, n in ((), ((0, 0),), ((1, 5), (0, 2)), ((2, 1), (1, 3), (0, 4)))[j]:
                        wins(q, a, j, n)
                eng.wait_ge(c_r, 6 * q + 6)
                for j, (a, b) in enumerate(((0, 2), (5, 3), (2, 5), (4, 3))):
                    eng.tensor_tensor(W1[:, j, :], C[:, a, :], C[:, b, :], ALU.add).then_inc(w1_r, 1)
                for j, (a, b, op) in enumerate(((W1[:, 0, :], C[:, 4, :], ALU.add), (W1[:, 1, :], C[:, 0, :], ALU.subtract),
                                                (C[:, 1, :], W1[:, 2, :], ALU.subtract), (W1[:, 3, :], C[:, 1, :], ALU.add))):
                    eng.wait_ge(w1_r, 4 * q + j + 1)
                    eng.tensor_tensor(W2[:, j, :], a, b, op).then_inc(w2_r, 1)
                for j, (least, op) in enumerate(((2.0, ALU.is_ge), (1.0, ALU.is_ge), (0.0, ALU.is_ge), (1.0, ALU.is_le))):
                    eng.wait_ge(w2_r, 4 * q + j + 1)
                    if q:
                        eng.wait_ge(hl_r, 4 * q)
                    eng.scalar_tensor_tensor(HS[:, j, :], W2[:, j, :], least, H[:, j, :], op, ALU.mult).then_inc(hs_r, 1)
            statistics(0)
            add(1)
            statistics(1)


def scan_inputs(nc, nm, w, dram, keep):
    with ExitStack() as ctx:
        sb, ps = buffers(ctx, nc)
        NT = B * TT
        sq, ss, ms, rms = (sb(f"m_{n}", [P, NT]) for n in ("rstd_sq", "mean_sq", "mean_sq_eps", "rms"))
        XR = sb("m_xr", [P, B, TT, D])
        x = SplitX(nm, sb, "m")
        w_high, w_low = ({name: sb(f"{name}_{n}", [P, KD, EI], F32R) for name in ("m_in", "m_skip")} for n in ("high", "low"))
        w_high_ready, w_low_ready = nm.sems.new("m_w_high"), nm.sems.new("m_w_low")
        cin = sb("m_conv_in", [P, 2, 2, S + KC - 1])
        cv = sb("m_conv", [P, 2, 2, S])
        d1 = sb("m_d1T", [P, HALF])
        az, lz = sb("m_abs_z", [P, HALF]), sb("m_ln_z", [P, 2, HALF])
        ez = lambda e: XR[:, e, :, :].rearrange("p h f -> p (h f)")
        bc = sb("m_bcT", [2 * NS, T])
        small = w["m_small"][0]
        norm_w, conv_b, b_d2 = small[:, 0:KD], small[:, KD:KD + KE], small[:, KD + KE:KD + 2 * KE]
        conv_w = small[:, KD + 4 * KE:KD + 4 * KE + KE * KC]
        a_log = small[:, KD + 4 * KE + KE * KC:]
        IN, SK = [ps(f"m_in{n}") for n in range(2)], [ps(f"m_skip{n}") for n in range(2)]
        D2 = [ps(f"m_d2_{n}") for n in range(2)]
        D1, BC = ps("m_d1_ps"), ps("m_bc_ps")
        sem = lambda n: nm.sems.new(n)
        ms_ready, rms_ready, xr_ready = sem("m_ms"), sem("m_rms_r"), sem("m_xr_r")
        a_ready, padded, bc_out = sem("m_a"), sem("m_pad"), sem("m_bc_out")
        (in_ps, sk_ps, d1_ps, d2_ps, bc_ps, cin_r, x2_r, gt_r, d1_r, bc_r, az_r, ez_r, lz_r, cv_r, tap_r, rz_r,
         dl_r) = cs = counts(
            nm.sems, m_in_ps=4, m_sk_ps=4, m_d1p=1, m_d2p=4, m_bcp=1, m_cin_r=4, m_x2_r=4, m_gt_r=4, m_d1r=1,
            m_bc_r=1, m_az_r=4, m_ez_r=4, m_lz_r=4, m_cv_r=4, m_tap_r=12, m_rz_r=4, m_dl_r=4)
        pe = [in_ps, sk_ps, d1_ps, d2_ps, bc_ps]
        act = [cin_r, x2_r, gt_r, d1_r, bc_r, az_r, ez_r, lz_r]
        block = ctx.enter_context(nc.Block())

        def half(t, e, i):
            return t[:, e, bass.ds(i * HALF, HALF)]

        @block.sync
        def _(eng):
            for i in range(2):
                bc_r.now(eng, i, 0)
                at = slice(i * HALF, (i + 1) * HALF)
                eng.dma_start(keep.bc_dram[:, at], bc[:, at]).then_inc(bc_out, 16)
                eng.wait_ge(bc_out, 16 * (i + 1))
                if i == 0:
                    for nh in range(2):
                        keep.load_b(eng, 0, nh)
                        keep.load_c(eng, 0, nh)

        @block.gpsimd
        def _(eng):
            eng.memset(cin[:, :, :, 0:KC - 1], 0.0).then_inc(padded, 1)
            nm.gpsimd(eng, 3)
            eng.wait_ge(nm.rstd_ready, 4)
            eng.tensor_tensor(sq[:, :], nm.rstd[:, :], nm.rstd[:, :], ALU.mult).then_inc(ms_ready, 1)
            eng.wait_ge(ms_ready, 1)
            eng.tensor_tensor(ss[:, :], sq[:, :], nm.mv[:, :, 1], ALU.mult).then_inc(ms_ready, 1)
            eng.wait_ge(ms_ready, 2)
            eng.tensor_scalar(ms[:, :], ss[:, :], EPS_LN, None, ALU.add).then_inc(ms_ready, 1)
            eng.wait_ge(ms_ready, 3)
            eng.tensor_tensor(rms[:, :], ms[:, :], nm.mhalf[:, :], ALU.pow).then_inc(rms_ready, 1)
            for n, name in enumerate(("m_in", "m_skip")):
                eng.wait_ge(w_high_ready, n + 1)
                eng.tensor_tensor(w_low[name][:, :, :], w[name][0][:, :, :], w_high[name][:, :, :].bitcast(F32), ALU.subtract)\
                   .then_inc(w_low_ready, 1)
            eng.wait_ge(nm.xn_ready, 4 * NT)
            eng.tensor_tensor(nm.X[:, :, :, :], nm.X[:, :, :, :], nm.XN[:, :, :, :], ALU.add)
            nm.sems.clear_stale(eng)

        @block.tensor
        def _(eng):
            for c in pe:
                c.credit(eng)
            nm.tensor(eng, 3, D2, XR, xr_ready, TT)
            for name in ("m_d1", "m_d2", "m_bc"):
                eng.wait_ge(w[name][1], 16)
            eng.wait_ge(w_low_ready, 2)
            with eng.Fori(0, 2) as i:
                eng.wait_ge(x.low_ready, i + 1)
                for e in range(KE):
                    for bank, name, out_c, used in ((IN[e % 2], "m_in", in_ps, cin_r), (SK[e % 2], "m_skip", sk_ps, gt_r)):
                        (used.now(eng, i, e - 2) if e >= 2 else used.before(eng, i, e + 2))
                        cols = slice(e * P, (e + 1) * P)
                        split_product(eng, bank[:, :], [
                            (w_high[name][:, k, cols], w_low[name][:, k, cols], half(x.high, k, i), half(x.low, k, i))
                            for k in range(KD)]).then_inc(out_c.sem, 1)
            with eng.Fori(0, 2) as i:
                d1_r.before(eng, i, 0)
                for e in range(KE):
                    x2_r.now(eng, i, e)
                    mm = eng.matmul(D1[:, :], w["m_d1"][0][:, e, :], half(keep.x2, e, i), start=(e == 0), stop=(e == KE - 1))
                mm.then_inc(d1_ps.sem, 1)
                bc_r.before(eng, i, 0)
                for e in range(KE):
                    with fresh_addresses(nc):
                        mm = eng.matmul(BC[0:2 * NS, :], w["m_bc"][0][:, e, :], half(keep.x2, e, i), start=(e == 0),
                                        stop=(e == KE - 1))
                mm.then_inc(bc_ps.sem, 1)
                d1_r.now(eng, i, 0)
                for e in range(KE):
                    if e >= 2:
                        az_r.now(eng, i, e - 2)
                        rz_r.now(eng, i, e - 2)
                    else:
                        az_r.before(eng, i, e + 2)
                        rz_r.before(eng, i, e + 2)
                    eng.matmul(D2[e % 2][:, :], w["m_d2"][0][:, e * P:(e + 1) * P], d1[:, :], start=True,
                               stop=True).then_inc(d2_ps.sem, 1)

        @block.scalar
        def _(eng):
            for c in act:
                c.credit(eng)
            eng.wait_ge(w["m_small"][1], 16)
            eng.activation(keep.A[:, :], a_log, ACT.Exp).then_inc(a_ready, 1)
            for name in ("m_in", "m_skip"):
                eng.wait_ge(w[name][1], 16)
                eng.activation(w_high[name][:, :, :], w[name][0][:, :, :], ACT.Copy).then_inc(w_high_ready, 1)
            nm.scalar(eng, 3, D2, norm_w, after=x.scalar)
            nm.load_table(eng, ACT.Silu)
            with eng.Fori(0, 2) as i:
                for e in range(KE):
                    in_ps.now(eng, i, e)
                    (cv_r.now(eng, i, e - 2) if e >= 2 else cv_r.before(eng, i, e + 2))
                    eng.activation(cin[:, e % 2, :, KC - 1:], IN[e % 2][:, :].rearrange("p (b t) -> p b t", b=2),
                                   ACT.Copy).then_inc(cin_r.sem, 1)
                    sk_ps.now(eng, i, e)
                    eng.activation(half(keep.gate, e, i), SK[e % 2][:, :], ACT.Silu).then_inc(gt_r.sem, 1)
                    if e:
                        cv_r.now(eng, i, e - 1)
                        eng.activation(half(keep.x2, e - 1, i), cv[:, (e - 1) % 2, :, :].rearrange("p b t -> p (b t)"),
                                       ACT.Silu, bias=conv_b[:, e - 1:e]).then_inc(x2_r.sem, 1)
                cv_r.now(eng, i, KE - 1)
                eng.activation(half(keep.x2, KE - 1, i), cv[:, (KE - 1) % 2, :, :].rearrange("p b t -> p (b t)"),
                               ACT.Silu, bias=conv_b[:, KE - 1:KE]).then_inc(x2_r.sem, 1)
            with eng.Fori(0, 2) as i:
                d1_ps.now(eng, i, 0)
                d2_ps.before(eng, i, 3)
                eng.activation(d1[:, :], D1[:, :], ACT.Copy).then_inc(d1_r.sem, 1)
                bc_ps.now(eng, i, 0)
                eng.activation(bc[:, bass.ds(i * HALF, HALF)], BC[0:2 * NS, :], ACT.Copy).then_inc(bc_r.sem, 1)
                for e in range(KE):
                    d2_ps.now(eng, i, e)
                    (ez_r.now(eng, i, e - 1) if e else ez_r.before(eng, i, KE - 1))
                    eng.activation(az[:, :], D2[e % 2][:, :], ACT.Abs, bias=b_d2[:, e:e + 1]).then_inc(az_r.sem, 1)
                    az_r.now(eng, i, e)
                    lz_r.before(eng, i, e)
                    eng.activation(ez(e), az[:, :], ACT.Exp, scale=-1.0).then_inc(ez_r.sem, 1)
                for e in range(KE):
                    ez_r.now(eng, i, e)
                    (dl_r.now(eng, i, e - 2) if e >= 2 else dl_r.before(eng, i, e + 2))
                    eng.activation(lz[:, e % 2, :], ez(e), ACT.Ln, bias=1.0).then_inc(lz_r.sem, 1)

        @block.vector
        def _(eng):
            for c in cs:
                if c not in pe + act:
                    c.credit(eng)
            nm.vector(eng, 3)
            eng.wait_ge(rms_ready, 1)
            for t in range(NT):
                eng.wait_ge(nm.xn_ready, 3 * NT + t + 1)
                eng.tensor_scalar(XR[:, t // TT, t % TT, :], nm.XN[:, t // TT, t % TT, :], rms[:, t:t + 1], None,
                                  ALU.mult).then_inc(xr_ready, 1)
            x.vector(eng)
            eng.wait_ge(padded, 1)
            eng.wait_ge(a_ready, 1)
            eng.tensor_scalar(keep.A[:, :], keep.A[:, :], -1.0, None, ALU.mult).then_inc(a_ready, 1)

            def relu_z(i, e):
                d2_ps.now(eng, i, e)
                az_r.now(eng, i, e)
                eng.tensor_scalar(half(keep.delta, e, i), D2[e % 2][:, :], b_d2[:, e:e + 1], 0.0, ALU.add, ALU.max)\
                   .then_inc(rz_r.sem, 1)

            def delta(i, e):
                lz_r.now(eng, i, e)
                rz_r.now(eng, i, e)
                eng.tensor_tensor(half(keep.delta, e, i), half(keep.delta, e, i), lz[:, e % 2, :], ALU.add).then_inc(dl_r.sem, 1)
                dl_r.now(eng, i, e)
                eng.tensor_tensor(half(keep.dx, e, i), half(keep.delta, e, i), half(keep.x2, e, i), ALU.mult)

            with eng.Fori(0, 2) as i:
                for e in range(KE):
                    cin_r.now(eng, i, e)
                    (x2_r.now(eng, i, e - 2) if e >= 2 else x2_r.before(eng, i, e + 2))
                    eng.tensor_scalar(cv[:, e % 2, :, :], cin[:, e % 2, :, 0:S], conv_w[:, e * KC:e * KC + 1], None,
                                      ALU.mult).then_inc(tap_r.sem, 1)
                    for q in range(1, KC):
                        tap_r.now(eng, i, 3 * e + q - 1)
                        eng.scalar_tensor_tensor(cv[:, e % 2, :, :], cin[:, e % 2, :, q:q + S],
                                                 conv_w[:, e * KC + q:e * KC + q + 1], cv[:, e % 2, :, :],
                                                 ALU.mult, ALU.add).then_inc((cv_r if q == KC - 1 else tap_r).sem, 1)
            with eng.Fori(0, 2) as i:
                for e in range(KE):
                    relu_z(i, e)
                for e in range(KE):
                    delta(i, e)


class Keep:

    def __init__(self, ctx, nc):
        sb, _ = buffers(ctx, nc)
        self.x2, self.gate = sb("m_x2T", [P, KE, T]), sb("m_gateT", [P, KE, T])
        self.delta, self.dx = sb("m_deltaT", [P, KE, T]), sb("m_dxT", [P, KE, T])
        self.A = sb("m_A", [P, KE * NS])
        self.B, self.C = sb("m_B", [P, 2, NS // 2, S]), sb("m_C", [P, 2, NS // 2, S])
        self.b_in = [nc.alloc_semaphore(f"m_b_in{n}") for n in range(2)]
        self.c_in = [nc.alloc_semaphore(f"m_c_in{n}") for n in range(2)]
        self.bc_dram = nc.dram_tensor("bc_scratch", (2 * NS, T), F32, kind="Internal").ap()

    def rows(self, b, at):
        return self.bc_dram[at:at + NS // 2, bass.ds(b * S, S)][None, :, :].to_broadcast((P, NS // 2, S))

    def load_b(self, eng, b, nh):
        eng.dma_start(self.B[:, nh, :, :], self.rows(b, nh * NS // 2)).then_inc(self.b_in[nh], 16)

    def load_c(self, eng, b, nh):
        eng.dma_start(self.C[:, nh, :, :], self.rows(b, NS + nh * NS // 2)).then_inc(self.c_in[nh], 16)


def scan(nc, nm, w, dram, keep):
    with ExitStack() as ctx:
        sb, ps = buffers(ctx, nc)
        NH = NS // 2
        U = 2 * KE
        NB, ND = 4, 2
        Bb, Cb, b_in, c_in = keep.B, keep.C, keep.b_in, keep.c_in
        dec = sb("m_decay", [P, ND, NH, S])
        hb = sb("m_h", [P, NB, NH, S])
        y1, yT = sb("m_y1", [P, KE, S]), sb("m_yT", [P, KE, S])
        Y = ps("m_y_ps", 2)
        O = ps("m_out_ps")
        W_D = w["m_small"][0][:, KD + 2 * KE:KD + 3 * KE]
        zeroed = nm.sems.new("m_zeroed")
        (y_ps, dec_r, u_r, h_r, p_r) = counts(nm.sems, m_y_r=U, m_dec_r=U, m_u_r=U, m_h_r=U, m_p_r=U)
        (y1_r, yT_r, o_ps, x_r) = counts(nm.sems, m_y1_r=KE, m_yT_r=1, m_o_r=1, m_xadd=1)

        def batches(eng, body):
            body(0, False)
            with eng.Fori(1, B) as i:
                body(i, True)

        block = ctx.enter_context(nc.Block())

        @block.sync
        def _(eng):
            with eng.Fori(1, B) as i:
                for nh in range(2):
                    u_r.before(eng, i, KE * (nh + 1) - 1)
                    keep.load_b(eng, i, nh)
                    p_r.before(eng, i, KE * (nh + 1) - 1)
                    keep.load_c(eng, i, nh)

        @block.scalar
        def _(eng):
            dec_r.credit(eng)
            eng.wait_ge(zeroed, 1)
            with fresh_addresses(nc), eng.Fori(0, B) as i:
                for u in range(U):
                    nh, e = u // KE, u % KE
                    (h_r.now(eng, i, u - ND) if u >= ND else h_r.before(eng, i, U - ND + u))
                    for n in range(NH):
                        s = e * NS + nh * NH + n
                        a = eng.activation(dec[:, u % ND, n, 1:S], keep.delta[:, e, bass.ds(i * S + 1, S - 1)], ACT.Exp,
                                           scale=keep.A[:, s:s + 1])
                    a.then_inc(dec_r.sem, 1)

        @block.gpsimd
        def _(eng):
            u_r.credit(eng)
            eng.memset(dec[:, :, :, 0:1], 0.0).then_inc(zeroed, 1)

            with fresh_addresses(nc), eng.Fori(0, B) as i:
                for u in range(U):
                    nh, e = u // KE, u % KE
                    if e == 0:
                        eng.wait_ge(b_in[nh], 16 * i + 16)
                    (y_ps.now(eng, i, u - NB) if u >= NB else y_ps.before(eng, i, U - NB + u))
                    eng.tensor_tensor(hb[:, u % NB, :, :], Bb[:, nh, :, :],
                                      keep.dx[:, e, bass.ds(i * S, S)][:, None, :].to_broadcast((P, NH, S)),
                                      ALU.mult).then_inc(u_r.sem, 1)
            nm.sems.clear_stale(eng)

        @block.vector
        def _(eng):
            for c in (h_r, p_r):
                c.credit(eng)
            for c in (y1_r, yT_r, x_r):
                c.credit(eng, 2)
            flat = lambda t: t.rearrange("p n t -> p (n t)")

            def gated(i):
                yT_r.before(eng, i, 0)
                for e in range(KE):
                    y_ps.before(eng, i, KE + e | 1)
                    eng.scalar_tensor_tensor(y1[:, e, :], keep.x2[:, e, bass.ds((i - 1) * S, S)], W_D[:, e:e + 1],
                                             Y[:, e * S:(e + 1) * S], ALU.mult, ALU.add).then_inc(y1_r.sem, 1)
                y1_r.now(eng, i, KE - 1)
                o_ps.before(eng, i, 0)
                eng.tensor_tensor(yT[:, :, :], y1[:, :, :], keep.gate[:, :, bass.ds((i - 1) * S, S)], ALU.mult)\
                   .then_inc(yT_r.sem, 1)

            def add(i):
                o_ps.now(eng, i, 0)
                eng.tensor_tensor(nm.X[:, i - 1, :, :], nm.X[:, i - 1, :, :], O[:, :].rearrange("p (h f) -> p h f", h=TT),
                                  ALU.add).then_inc(x_r.sem, 1)

            def units(i, end_before):
                for u in range(U):
                    nh, e = u // KE, u % KE
                    dec_r.now(eng, i, u)
                    u_r.now(eng, i, u)
                    eng.tensor_tensor_scan(flat(hb[:, u % NB, :, :]), flat(dec[:, u % ND, :, :]), flat(hb[:, u % NB, :, :]),
                                           0.0, ALU.mult, ALU.add).then_inc(h_r.sem, 1)
                    if e == 0:
                        eng.wait_ge(c_in[nh], 16 * i + 16)
                    h_r.now(eng, i, u)
                    eng.tensor_tensor(hb[:, u % NB, :, :], hb[:, u % NB, :, :], Cb[:, nh, :, :], ALU.mult).then_inc(p_r.sem, 1)
                    if end_before and u == 0:
                        gated(i)
                    if end_before and u == 3:
                        add(i)

            batches(eng, units)
            gated(B)
            x_r.before(eng, B, 0)
            for b in range(B - 1):
                nm.statistics(eng, 4, b)
            add(B)
            x_r.now(eng, B, 0)
            nm.statistics(eng, 4, B - 1)

        @block.tensor
        def _(eng):
            y_ps.credit(eng)
            o_ps.credit(eng, 2)
            eng.wait_ge(w["m_out"][1], 16)

            def out_product(i):
                yT_r.now(eng, i, 0)
                x_r.before(eng, i, 0)
                for h in range(TT):
                    for e in range(KE):
                        mm = eng.matmul(O[:, h * D:(h + 1) * D], yT[:, e, h * P:(h + 1) * P], w["m_out"][0][:, e, :],
                                        start=(e == 0), stop=(e == KE - 1))
                mm.then_inc(o_ps.sem, 1)

            def units(i, end_before):
                y1_r.now(eng, i, KE - 1)
                for u in range(U):
                    nh, e = u // KE, u % KE
                    p_r.now(eng, i, u)
                    for n in range(NH):
                        mm = eng.matmul(Y[:, e * S:(e + 1) * S], nm.ident[:, :], hb[:, u % NB, n, :],
                                        start=(nh == 0 and n == 0 and e % 2 == 0), stop=(nh == 1 and n == NH - 1),
                                        skip_group_check=True)
                    mm.then_inc(y_ps.sem, 1)
                    if end_before and u == 1:
                        out_product(i)

            batches(eng, units)
            out_product(B)


def selective_scan(nc, nm, w, dram):
    with ExitStack() as ctx:
        keep = Keep(ctx, nc)
        scan_inputs(nc, nm, w, dram, keep)
        nm.sems.next_phase()
        scan(nc, nm, w, dram, keep)


def context_attention(nc, nm, w, dram):
    with ExitStack() as ctx:
        sb, ps = buffers(ctx, nc)
        qkT = sb("c_qkT", [P, B, 2, S])
        nmax, sums, rs = sb("c_neg_max", [P, B, TT]), sb("c_sums", [P, B, TT]), sb("c_rsums", [P, B, TT])
        E, AN = sb("c_exp", [P, B, TT, S]), sb("c_probs", [P, B, TT, S])
        AT = sb("c_probsT", [P, B, KD, S])
        BANK = [ps(f"c_bank{b}") for b in range(B)]
        LN = [ps(f"c_ln{n}") for n in range(2)]
        q_ps, e_ps, t_ps, o_ps, qk_sb, ex, at_sb, mx, rs_r, an_r, x_added = (
            nm.sems.new(f"c_{n}") for n in ("qk_ps", "energy_ps", "turned_ps", "out_ps", "qk_sb", "exp", "probsT", "max",
                                            "rsums", "probs", "x_added"))
        qk = w["x_qk"][0]
        block = ctx.enter_context(nc.Block())

        @block.gpsimd
        def _(eng):
            nm.gpsimd(eng, 4)
            nm.sems.clear_stale(eng)

        @block.tensor
        def _(eng):
            eng.wait_ge(w["ctxT"][1], 16)
            eng.wait_ge(w["x_qk"][1], 16)
            for b in range(B):
                for n in range(2):
                    mm = eng.matmul(BANK[b][:, n * S:(n + 1) * S], qk[:, n * P:(n + 1) * P], w["ctxT"][0][:, b, :],
                                    start=True, stop=True)
                mm.then_inc(q_ps, 1)
            for b in range(B):
                eng.wait_ge(qk_sb, 2 * b + 2)
                for h in range(TT):
                    mm = eng.matmul(BANK[b][:, h * S:(h + 1) * S], qkT[:, b, 0, h * P:(h + 1) * P], qkT[:, b, 1, :],
                                    start=True, stop=True)
                mm.then_inc(e_ps, 1)
            nm.tensor(eng, 4, LN)
            for b in range(B):
                eng.wait_ge(an_r, TT * (b + 1))
                for h in range(TT):
                    for k in range(KD):
                        mm = eng.transpose(BANK[b][:, k * S + h * P:k * S + (h + 1) * P], AN[:, b, h, k * P:(k + 1) * P],
                                           nm.ident[:, :])
                mm.then_inc(t_ps, 1)
            eng.wait_ge(nm.xnT_ready, 5 * B)
            for b in range(B):
                eng.wait_ge(at_sb, b + 1)
                for h in range(TT):
                    at = b * S + h * P
                    for k in range(KD):
                        mm = eng.matmul(BANK[b][:, h * S:(h + 1) * S], nm.xnT[:, k, at:at + P], AT[:, b, k, :],
                                        start=(k == 0), stop=(k == KD - 1))
                mm.then_inc(o_ps, 1)

        @block.scalar
        def _(eng):
            for b in range(B):
                eng.wait_ge(q_ps, b + 1)
                for n in range(2):
                    eng.activation(qkT[:, b, n, :], BANK[b][:, n * S:(n + 1) * S], ACT.Identity,
                                   bias=qk[:, 2 * P + n:2 * P + n + 1]).then_inc(qk_sb, 1)
            for b in range(B):
                eng.wait_ge(mx, b + 1)
                for h in range(TT):
                    eng.activation(E[:, b, h, :], BANK[b][:, h * S:(h + 1) * S], ACT.Exp, bias=nmax[:, b, h:h + 1],
                                   accum_out=sums[:, b, h:h + 1]).then_inc(ex, 1)
            nm.scalar(eng, 4, LN)
            for b in range(B):
                eng.wait_ge(t_ps, b + 1)
                eng.activation(AT[:, b, :, :], BANK[b][:, :].rearrange("p (k t) -> p k t", k=KD), ACT.Copy).then_inc(at_sb, 1)

        @block.vector
        def _(eng):
            def maxima():
                for b in range(B):
                    eng.wait_ge(e_ps, b + 1)
                    eng.tensor_reduce(nmax[:, b, :], BANK[b][:, :].rearrange("p (h t) -> p h t", h=TT), AX.X, ALU.max,
                                      negate=True).then_inc(mx, 1)

            nm.vector(eng, 4, beside=maxima)
            for b in range(B):
                eng.wait_ge(ex, TT * (b + 1))
                eng.reciprocal(rs[:, b, :], sums[:, b, :]).then_inc(rs_r, 1)
                eng.wait_ge(rs_r, b + 1)
                for h in range(TT):
                    eng.tensor_scalar(AN[:, b, h, :], E[:, b, h, :], rs[:, b, h:h + 1], None, ALU.mult).then_inc(an_r, 1)
            for b in range(B):
                eng.wait_ge(o_ps, b + 1)
                eng.tensor_tensor(nm.X[:, b, :, :], nm.X[:, b, :, :], BANK[b][:, :].rearrange("p (h f) -> p h f", h=TT),
                                  ALU.add).then_inc(x_added, 1)
                eng.wait_ge(x_added, b + 1)
                nm.statistics(eng, 5, b)


def experts(nc, nm, w, dram, out):
    with ExitStack() as ctx:
        sb, ps = buffers(ctx, nc)
        NT, NR, NW = B * TT, NX + 1, NX + 4
        nmax, tops = sb("e_neg_max", [P, NT]), sb("e_tops", [P, NT, 8])
        EV, REST = sb("e_exp", [P, NT, NW]), sb("e_rest", [P, NT, NW])
        tot, rtot = sb("e_total", [P, NT]), sb("e_rtotal", [P, NT])
        SH0, SH = sb("e_share0", [P, NT, NX]), sb("e_share", [P, NT, NR])
        SHT = sb("e_shareT", [NR, T])
        RING = 3
        W = sb("e_weights", [P, RING, 3 * KD * P])
        WH, WL = (sb(f"e_weights_{n}", [P, RING, 3 * KD * P], F32R) for n in ("high", "low"))
        x = SplitX(nm, sb, "e")
        AH, AL = (sb(f"e_act_{n}", [P, 2, HALF], F32R) for n in ("high", "low"))
        CB = sb("e_share_rows", [P, RING, T])
        SG = sb("e_silu", [P, 2, HALF])
        GU = sb("e_gated", [P, 2, HALF])
        AC = sb("e_act", [P, 2, HALF])
        GP, UP = [ps(f"e_gate{n}") for n in range(2)], [ps(f"e_up{n}") for n in range(2)]
        OUT = [ps(f"e_out{n}") for n in range(4)]
        sem = lambda n: nm.sems.new(n)
        lg_r, nmx_r, ev_r, top_r, cut_r, rest_r = (sem(f"e_{n}") for n in ("lg", "nmx", "ev", "top", "cut", "rest"))
        sh0_r, tot_r, rtot_r, sh_r, sht_ps, sht_r, sht_out, done, stored = (
            sem(f"e_{n}") for n in ("sh0", "tot", "rtot", "sh", "shtp", "sht", "shtout", "done", "stored"))
        w_in = [sem(f"e_w_in{n}") for n in range(RING)]
        c_in = [[sem(f"e_c_in{n}{a}") for a in range(2)] for n in range(RING)]
        (g_ps, u_ps, dn, si, gu_r, ac_r, wh_r, wl_r, ah_r, al_r) = cs = counts(
            nm.sems, e_g_ps=6, e_u_ps=6, e_dn=6, e_si=6, e_gu=6, e_ac=6, e_wh=3, e_wl=3, e_ah=6, e_al=6)
        pe, act, pool = [g_ps, u_ps, dn], [si, wh_r, ah_r], [ac_r]
        share_dram = nc.dram_tensor("share_scratch", (NR, T), F32, kind="Internal").ap()
        HT = HALF // P
        PASSES = 1 + NX * FX // P // RING
        LAST = PASSES

        def passes(eng, body):
            body(0, RING, True, False)
            with eng.Fori(1, PASSES) as i:
                body(i, RING, False, False)
            body(LAST, 1, False, True)

        block = ctx.enter_context(nc.Block())

        def owners(i, r):
            if i is None:
                return [(a * P // 2, P // 2, NX) for a in range(2)]
            cut, e = FX - r * (P - FX), (RING + 1) * (i - 1) + r
            return [(0, cut, e), (cut, P - cut, e + 1)]

        @block.sync
        def _(eng):
            def weights_of(i, r):
                eng.dma_start(W[:, r, :], dram["experts"][bass.ds(i * RING + r, 1)].rearrange("a p n -> (a p) n"))\
                   .then_inc(w_in[r], 16)

            for r in range(RING):
                weights_of(0, r)
            eng.wait_ge(sht_r, 2)
            eng.dma_start(share_dram, SHT[:, :]).then_inc(sht_out, 16)
            eng.wait_ge(sht_out, 16)

            def loads(i, slots, first, last):
                for r in range(slots):
                    if not first:
                        wl_r.before(eng, i, r)
                        weights_of(i, r)
                    for a, (p, n, e) in enumerate(owners(None if first or last else i, r)):
                        if not first:
                            ac_r.before(eng, i, 2 * r + 1)
                        eng.dma_start(CB[p:p + n, r, :], share_dram[bass.ds(e, 1), :].to_broadcast((n, T)))\
                           .then_inc(c_in[r][a], 16)

            passes(eng, loads)
            for b in range(B):
                eng.wait_ge(done, b + 1)
                eng.dma_start(out[b].rearrange("(h p) f -> p h f", p=P), nm.X[:, b, :, :]).then_inc(stored, 16)
            eng.wait_ge(stored, 16 * B)

        @block.gpsimd
        def _(eng):
            for c in pool:
                c.credit(eng)
            nm.gpsimd(eng, 5)
            eng.memset(EV[:, :, NX:NW], -1.0).then_inc(cut_r, 1)
            nm.sems.clear_stale(eng)

            def share(i, slots, first, last):
                for r in range(slots):
                    eng.wait_ge(c_in[r][0], 16 * i + 16)
                    eng.wait_ge(c_in[r][1], 16 * i + 16)
                    for h in range(2):
                        u = 2 * r + h
                        gu_r.now(eng, i, u)
                        (al_r.now(eng, i, u - 2) if u >= 2 else al_r.before(eng, i, 4 + u))
                        eng.tensor_tensor(AC[:, h, :], GU[:, h, :], CB[:, r, h * HALF:(h + 1) * HALF], ALU.mult).then_inc(ac_r.sem, 1)

            passes(eng, share)

        @block.tensor
        def _(eng):
            for c in pe:
                c.credit(eng)
            nm.tensor(eng, 5, GP)
            eng.wait_ge(nm.xnT_ready, 6 * B)
            eng.wait_ge(w["router"][1], 16)
            for t in range(NT):
                for k in range(KD):
                    mm = eng.matmul(OUT[0][:, t * 64:t * 64 + NR], nm.xnT[:, k, t * P:(t + 1) * P], w["router"][0][:, k, :],
                                    start=(k == 0), stop=(k == KD - 1))
            mm.then_inc(lg_r, 1)
            eng.wait_ge(x.low_ready, 2)

            def turn_shares():
                eng.wait_ge(sh_r, 2)
                for t in range(NT):
                    mm = eng.transpose(OUT[2 + t // 4][0:NR, (t % 4) * P:(t % 4 + 1) * P], SH[:, t, :], nm.ident[:, :])
                mm.then_inc(sht_ps, 1)

            def down(r, h, ready, start=False, stop=False):
                ready()
                at = slice(2 * KD * P, None)
                for t in range(HT):
                    n = h * HT + t
                    rows = slice(t * P, (t + 1) * P)
                    mm = split_product(eng, OUT[n // 2][:, (n % 2) * D:(n % 2 + 1) * D],
                                       [(AH[:, h, rows], AL[:, h, rows], WH[:, r, at], WL[:, r, at])],
                                       start=(start and n % 2 == 0), stop=stop)
                mm.then_inc(dn.sem, 1)

            def chunks(i, slots, first, last):
                for u in range(2 * slots):
                    r, h = u // 2, u % 2
                    if h == 0:
                        wl_r.now(eng, i, r)
                    if u >= 2:
                        si.now(eng, i, u - 2)
                        gu_r.now(eng, i, u - 2)
                    else:
                        si.before(eng, i, 4 + u)
                        gu_r.before(eng, i, 4 + u)
                    for bank, at, cnt in ((GP[h], 0, g_ps), (UP[h], KD * P, u_ps)):
                        cols = lambda k: slice(at + k * P, at + (k + 1) * P)
                        split_product(eng, bank[:, :], [(WH[:, r, cols(k)], WL[:, r, cols(k)], *x.half(k, h))
                                                        for k in range(KD)]).then_inc(cnt.sem, 1)
                    if first and u == 1:
                        turn_shares()
                    if first and u == 2:
                        eng.wait_ge(sht_r, 2)
                    if u >= 2:
                        down(r - 1, h, lambda: al_r.now(eng, i, u - 2), first and r == 1)
                    elif not first:
                        down(RING - 1, h, lambda: al_r.before(eng, i, 4 + u))

            passes(eng, chunks)
            for h in range(2):
                down(0, h, lambda: al_r.now(eng, LAST, h), stop=True)

        @block.scalar
        def _(eng):
            for c in act:
                c.credit(eng)
            def high_weights(i, r, first):
                if r == RING:
                    dn.now(eng, i, 1)
                elif not first:
                    dn.before(eng, i, 2 * r + 1)
                eng.wait_ge(w_in[r % RING], 16 * (i + r // RING) + 16)
                eng.activation(WH[:, r % RING, :], W[:, r % RING, :], ACT.Copy).then_inc(wh_r.sem, 1)

            nm.scalar(eng, 5, GP, after=x.scalar)
            high_weights(0, 0, True)
            eng.wait_ge(nmx_r, 1)
            eng.wait_ge(cut_r, 1)
            lg = OUT[0][:, :].rearrange("p (t c) -> p t c", c=64)
            for t in range(NT):
                eng.activation(EV[:, t, 0:NX], lg[:, t, 0:NX], ACT.Exp, bias=nmax[:, t:t + 1]).then_inc(ev_r, 1)
            eng.activation(SH[:, :, NX], lg[:, :, NX], ACT.Sigmoid).then_inc(sh_r, 1)
            for n in range(2):
                eng.wait_ge(sht_ps, 1)
                eng.activation(SHT[:, n * HALF:(n + 1) * HALF], OUT[2 + n][0:NR, :], ACT.Copy).then_inc(sht_r, 1)

            def high(i, u, ac, free):
                ac()
                free()
                eng.activation(AH[:, u % 2, :], AC[:, u % 2, :], ACT.Copy).then_inc(ah_r.sem, 1)

            def silus(i, slots, first, last):
                for u in range(2 * slots):
                    if u % 2 == 0 and not last:
                        high_weights(i, u // 2 + 1, first)
                    g_ps.now(eng, i, u)
                    (gu_r.now(eng, i, u - 2) if u >= 2 else gu_r.before(eng, i, 4 + u))
                    eng.activation(SG[:, u % 2, :], GP[u % 2][:, :], ACT.Silu).then_inc(si.sem, 1)
                    if u:
                        high(i, u - 1, lambda: ac_r.now(eng, i, u - 1),
                             lambda: dn.now(eng, i, u - 3) if u >= 3 else dn.before(eng, i, u + 3))
                    elif not first:
                        high(i, 5, lambda: ac_r.before(eng, i, 5), lambda: dn.before(eng, i, 3))

            passes(eng, silus)
            high(LAST, 1, lambda: ac_r.now(eng, LAST, 1), lambda: dn.before(eng, LAST, 5))

        @block.vector
        def _(eng):
            for c in cs:
                if c not in pe + act + pool:
                    c.credit(eng)
            def low_weights(i, r, first):
                wh_r.now(eng, i, r)
                if r == RING:
                    dn.now(eng, i, 1)
                elif not first:
                    dn.before(eng, i, 2 * r + 1)
                eng.tensor_tensor(WL[:, r % RING, :], W[:, r % RING, :], WH[:, r % RING, :].bitcast(F32), ALU.subtract)\
                   .then_inc(wl_r.sem, 1)

            nm.vector(eng, 5)
            x.vector(eng)
            low_weights(0, 0, True)
            eng.wait_ge(lg_r, 1)
            lg = OUT[0][:, :].rearrange("p (t c) -> p t c", c=64)
            eng.tensor_reduce(nmax[:, :], lg[:, :, 0:NX], AX.X, ALU.max, negate=True).then_inc(nmx_r, 1)
            for t in range(NT):
                eng.wait_ge(ev_r, t + 1)
                eng.max(tops[:, t, :], EV[:, t, 0:NX]).then_inc(top_r, 1)
            eng.wait_ge(top_r, NT)
            eng.memset(tops[:, :, 4:8], -1.0).then_inc(cut_r, 1)
            eng.wait_ge(cut_r, 2)
            for t in range(NT):
                eng.match_replace(REST[:, t, :], tops[:, t, :], EV[:, t, :], 0.0).then_inc(rest_r, 1)
            eng.wait_ge(rest_r, NT)
            eng.tensor_tensor(SH0[:, :, :], EV[:, :, 0:NX], REST[:, :, 0:NX], ALU.subtract).then_inc(sh0_r, 1)
            eng.wait_ge(sh0_r, 1)
            eng.tensor_reduce(tot[:, :], SH0[:, :, :], AX.X, ALU.add).then_inc(tot_r, 1)
            eng.wait_ge(tot_r, 1)
            eng.reciprocal(rtot[:, :], tot[:, :]).then_inc(rtot_r, 1)
            eng.wait_ge(rtot_r, 1)
            eng.tensor_tensor(SH[:, :, 0:NX], SH0[:, :, :], rtot[:, :, None].to_broadcast((P, NT, NX)), ALU.mult).then_inc(sh_r, 1)

            def low(i, u, ah, free):
                ah()
                free()
                eng.tensor_tensor(AL[:, u % 2, :], AC[:, u % 2, :], AH[:, u % 2, :].bitcast(F32), ALU.subtract)\
                   .then_inc(al_r.sem, 1)

            def gated(i, slots, first, last):
                for u in range(2 * slots):
                    if u % 2 == 0 and not last:
                        low_weights(i, u // 2 + 1, first)
                    si.now(eng, i, u)
                    u_ps.now(eng, i, u)
                    (ac_r.now(eng, i, u - 2) if u >= 2 else ac_r.before(eng, i, 4 + u))
                    eng.tensor_tensor(GU[:, u % 2, :], SG[:, u % 2, :], UP[u % 2][:, :], ALU.mult).then_inc(gu_r.sem, 1)
                    if u:
                        low(i, u - 1, lambda: ah_r.now(eng, i, u - 1),
                            lambda: dn.now(eng, i, u - 3) if u >= 3 else dn.before(eng, i, u + 3))
                    elif not first:
                        low(i, 5, lambda: ah_r.before(eng, i, 5), lambda: dn.before(eng, i, 3))

            passes(eng, gated)
            low(LAST, 1, lambda: ah_r.now(eng, LAST, 1), lambda: dn.before(eng, LAST, 5))
            for b in range(B):
                dn.now(eng, LAST, b // 2)
                eng.tensor_tensor(nm.X[:, b, :, :], nm.X[:, b, :, :], OUT[b][:, :].rearrange("p (h f) -> p h f", h=TT),
                                  ALU.add).then_inc(done, 1)


def build(nc, dram, out, upto=99):
    with ExitStack() as ctx:
        nm = Norm(ctx, nc)
        late = weights(ctx, nc, LATE)
        with ExitStack() as parts:
            sb, _ = buffers(parts, nc)
            split = {f"{name}_{n}": sb(f"{name}_{n}", shape, F32R)
                     for name, shape in EARLY if name in SPLIT for n in ("high", "low")}
            with ExitStack() as first:
                w = weights(first, nc, EARLY) | late
                attention(nc, nm, w, split, dram)
                nm.sems.next_phase()
                if upto > 1:
                    quantised(nc, nm, w, split, dram)
                    nm.sems.next_phase()
            if upto > 2:
                sparse(nc, nm, split, dram)
                nm.sems.next_phase()
        for phase in PHASES[:max(upto - 3, 0)]:
            phase(nc, nm, late, dram, *([out] if phase is experts else []))
            nm.sems.next_phase()


PHASES = (selective_scan, context_attention, experts)


def layout(i):
    c = np.ascontiguousarray

    def tiles(a):
        return c(a.reshape(-1, P, a.shape[-1]).transpose(1, 0, 2))

    def cols(a):
        return a.reshape(-1, P).T

    low_rows = np.stack([np.arange(P) // (2 * HD) % 2, np.arange(P) // HD % 2], axis=1)
    out = {
        "part_masks": np.where(low_rows, -1, 0).astype(np.float32),
        "x": c(i["x"].reshape(B, TT, P, D).transpose(0, 2, 1, 3)),
        "wq": tiles(i["L0_attn_Wq"].T), "wk": tiles(i["L0_attn_Wk"].T),
        "wv": tiles(i["L0_attn_Wv"].T), "wo": tiles(i["L0_attn_Wo"].T),
        "fsT": c(i["fside_BxS2xS2_0"].transpose(0, 2, 1).reshape(B, KD, P, D).transpose(2, 0, 1, 3)),
        "ctxT": c(i["ctx_1024"].transpose(2, 0, 1)),
        "f_gate": tiles(i["L0_ffn_w_gate"].reshape(D, 2, P, 4).transpose(0, 1, 3, 2).reshape(D, FF)),
        "f_up": tiles(i["L0_ffn_w_up"].reshape(D, 2, P, 4).transpose(0, 1, 3, 2).reshape(D, FF)),
        "f_down": c(i["L0_ffn_w_down"].reshape(2, P, 4, D).transpose(1, 0, 2, 3).reshape(P, 8, D)),
        "m_small": c(np.concatenate([
            cols(i["L1_attn_norm_w"]), cols(i["L1_attn_conv_b"]), cols(i["L1_attn_b_d2"]), cols(i["L1_attn_W_D"]),
            np.zeros((P, KE), np.float32),
            i["L1_attn_conv_w"].reshape(KE, P, KC).transpose(1, 0, 2).reshape(P, KE * KC),
            i["L1_attn_A_log"].reshape(KE, P, NS).transpose(1, 0, 2).reshape(P, KE * NS)], axis=1)),
        "m_skip": tiles(i["L1_attn_W_skip"].T), "m_in": tiles(i["L1_attn_W_in"].T),
        "m_d1": tiles(i["L1_attn_W_d1"].T), "m_d2": c(i["L1_attn_W_d2"].T),
        "m_bc": tiles(np.concatenate([i["L1_attn_W_Bm"], i["L1_attn_W_Cm"]], axis=0).T),
        "m_out": tiles(i["L1_attn_W_out"].T),
        "x_qk": c(np.concatenate([i["L1_xattn_Wq"].T, i["L1_xattn_Wk"].T, i["L1_xattn_bq"][:, None],
                                  i["L1_xattn_bk"][:, None]], axis=1)),
        "router": tiles(np.concatenate([i["L1_ffn_router_weight"].T, i["L1_ffn_sgate_w"]], axis=1)),
    }

    def experts(w, shared):
        flat = np.concatenate([shared, w.transpose(1, 0, 2).reshape(D, NX * FX)], axis=1)
        return flat.reshape(KD, P, NCH, P).transpose(2, 1, 0, 3)

    gate = experts(i["L1_ffn_w_gate"], i["L1_ffn_sw_gate"])
    up = experts(i["L1_ffn_w_up"], i["L1_ffn_sw_up"])
    down = np.concatenate([i["L1_ffn_sw_down"], i["L1_ffn_w_down"].reshape(NX * FX, D)], axis=0).reshape(NCH, P, 1, D)
    order = [0, 1, 2, *range(SCH, NCH), SCH - 1]
    out["experts"] = c(np.concatenate([gate.reshape(NCH, P, 256), up.reshape(NCH, P, 256),
                                       down.reshape(NCH, P, 256)], axis=2)[order])
    return out


def kernel(**inputs):
    import concourse.bacc as bacc
    from concourse.bass_utils import run_bass_kernel_spmd as run

    arrays = layout({k: np.asarray(v) for k, v in inputs.items()})
    nc = bacc.Bacc("TRN2", target_bir_lowering=False, num_devices=1)
    dram = {n: nc.dram_tensor(f"in_{n}", a.shape, mybir.dt.from_np(a.dtype), kind="ExternalInput").ap()
            for n, a in arrays.items()}
    out = nc.dram_tensor("out_x", (B, S, D), F32, kind="ExternalOutput").ap()
    build(nc, dram, out)
    r = run(nc, [{f"in_{n}": a for n, a in arrays.items()}], core_ids=[0])
    return r.results[0]["out_x"]
```
